# Optimizing a Trainium2 kernel written in Bass

```python
import numpy as np
import jax
import jax.numpy as jnp

def _softmax(x, axis=-1):
    return jax.nn.softmax(x, axis=axis)

def _gelu(x):
    return jax.nn.gelu(x, approximate=True)

def _silu(x):
    return jax.nn.silu(x)

def _sigmoid(x):
    return jax.nn.sigmoid(x)

def _layernorm(x, axis=-1, eps=1e-05):
    m = jnp.mean(x, axis=axis, keepdims=True)
    v = jnp.var(x, axis=axis, keepdims=True)
    return (x - m) / jnp.sqrt(v + eps)

def _scatter_add(tgt, idx, src, axis=0):
    return tgt.at[idx].add(src)

def _segment_sum(src, seg, n):
    return jax.ops.segment_sum(src, seg, n)
kernel_name = 'mk_xattn_seq_d4_seqx_r8_dd26f0'

def setup_inputs(seed: int=0):
    np.random.seed(seed)
    _w = jnp.asarray

    def _rec_inputs():
        import jax
        import jax.numpy as jnp
        _rk = jax.random.key(seed)
        x = -0.0005207 + 1.001 * jax.random.normal(jax.random.fold_in(_rk, 1), (16, 64, 128), jnp.float32)
        _lenS = 64 - jax.random.randint(jax.random.fold_in(_rk, 7), (16,), 0, max(1, 64 // 4) + 1, jnp.int32)
        _lenS2 = 64 - jax.random.randint(jax.random.fold_in(_rk, 8), (16,), 0, max(1, 64 // 4) + 1, jnp.int32)
        _ctx_1024P = jax.random.normal(jax.random.fold_in(_rk, 11), (16, 16, 128), jnp.float32)
        _ctx_1024c = jax.random.dirichlet(jax.random.fold_in(_rk, 511), 0.3 * jnp.ones((16,), jnp.float32), (16, 64))
        _ctx_1024t = jnp.einsum('bsk,bkd->bsd', _ctx_1024c, _ctx_1024P)
        _ctx_1024t = _ctx_1024t * jax.lax.rsqrt(jnp.mean(jnp.square(_ctx_1024t)) + 1e-12) * 0.953939
        ctx_1024 = 4.13588e-05 + 0.999923 * (_ctx_1024t + 0.3 * jax.random.normal(jax.random.fold_in(_rk, 611), (16, 64, 128), jnp.float32))
        itok_BxS_0_255 = jax.random.randint(jax.random.fold_in(_rk, 13), (16, 64), 0, 32, jnp.int32)
        _validS = jnp.arange(64)[None, :] < _lenS[:, None]
        _validS2 = jnp.arange(64)[None, :] < _lenS2[:, None]
        _causal = jnp.tril(jnp.ones((64, 64), dtype=bool))
        mask_BxS2_bf1 = jnp.ones((16, 64), dtype=bool)
        return (x, ctx_1024, itok_BxS_0_255, mask_BxS2_bf1)
    x, ctx_1024, itok_BxS_0_255, mask_BxS2_bf1 = _rec_inputs()

    def _L0_xattn_setup():
        import jax, jax.numpy as jnp
        import numpy as np
        D = 128
        H = 16
        DH = D // H
        STRIDE = 4
        EPS = 1e-05
        SCALE = 1.0 / np.sqrt(DH).astype(np.float32)

        def _ln(x, g, b):
            m = jnp.mean(x, axis=-1, keepdims=True)
            v = jnp.mean(jnp.square(x - m), axis=-1, keepdims=True)
            return (x - m) * jax.lax.rsqrt(v + EPS) * g + b
        key = jax.random.key(seed)
        ks = jax.random.split(key, 20)
        s = 0.02
        B, T, S = (2, 128, 512)
        return {'tgt': jax.random.normal(ks[0], (B, T, D), jnp.float32), 'memory': jax.random.normal(ks[1], (B, S, D), jnp.float32), 'sa_in_w': jax.random.normal(ks[2], (3 * D, D), jnp.float32) * s, 'sa_in_b': jnp.zeros((3 * D,), jnp.float32), 'sa_out_w': jax.random.normal(ks[3], (D, D), jnp.float32) * s, 'sa_out_b': jnp.zeros((D,), jnp.float32), 'ca_q_w': jax.random.normal(ks[4], (D, D), jnp.float32) * s, 'ca_q_b': jnp.zeros((D,), jnp.float32), 'ca_k_w': jax.random.normal(ks[5], (D, D), jnp.float32) * s, 'ca_k_b': jnp.zeros((D,), jnp.float32), 'ca_v_w': jax.random.normal(ks[6], (D, D), jnp.float32) * s, 'ca_v_b': jnp.zeros((D,), jnp.float32), 'ca_o_w': jax.random.normal(ks[7], (D, D), jnp.float32) * s, 'ca_o_b': jnp.zeros((D,), jnp.float32), 'ffn_w1': jax.random.normal(ks[8], (4 * D, D), jnp.float32) * s, 'ffn_b1': jnp.zeros((4 * D,), jnp.float32), 'ffn_w2': jax.random.normal(ks[9], (D, 4 * D), jnp.float32) * s, 'ffn_b2': jnp.zeros((D,), jnp.float32), 'ln1_g': jnp.ones((D,), jnp.float32), 'ln1_b': jnp.zeros((D,), jnp.float32), 'ln2_g': jnp.ones((D,), jnp.float32), 'ln2_b': jnp.zeros((D,), jnp.float32), 'ln3_g': jnp.ones((D,), jnp.float32), 'ln3_b': jnp.zeros((D,), jnp.float32)}
    _L0_xattn_all = _L0_xattn_setup()
    _L0_xattn_in = {k: v for k, v in _L0_xattn_all.items() if k in ('sa_in_w', 'sa_in_b', 'sa_out_w', 'sa_out_b', 'ca_q_w', 'ca_q_b', 'ca_k_w', 'ca_k_b', 'ca_v_w', 'ca_v_b', 'ca_o_w', 'ca_o_b', 'ffn_w1', 'ffn_b1', 'ffn_w2', 'ffn_b2', 'ln1_g', 'ln1_b', 'ln2_g', 'ln2_b', 'ln3_g', 'ln3_b')}
    del _L0_xattn_all

    def _L1_xattn_setup():
        import jax, jax.numpy as jnp
        import numpy as np
        STATE_DIM = 128
        TOKEN_DIM = 128
        NUM_HEADS = 16
        HEAD_DIM = STATE_DIM // NUM_HEADS

        def _pulse(states, tokens, attention_mask, W_state, b_state, W_token, b_token, W_out, b_out, W_upd, b_upd, ln_gamma, ln_beta):
            B, NS, sd = states.shape
            S = tokens.shape[1]
            H, D = (NUM_HEADS, HEAD_DIM)
            scale = D ** (-0.5)
            q = (states @ W_state + b_state).reshape(B, NS, H, D)
            kv = (tokens @ W_token + b_token).reshape(B, S, H, D)
            scores = jnp.einsum('bnhd,bshd->bhns', q, kv) * scale
            scores = jnp.where(attention_mask[:, None, None, :], scores, -jnp.inf)
            weights = jax.nn.softmax(scores, axis=-1)
            attended = jnp.einsum('bhns,bshd->bnhd', weights, kv).reshape(B, NS, sd)
            attended = attended @ W_out + b_out
            upd = jnp.concatenate([states, attended], axis=-1) @ W_upd + b_upd
            x = states + upd
            mu = jnp.mean(x, axis=-1, keepdims=True)
            var = jnp.var(x, axis=-1, keepdims=True)
            return (x - mu) * jax.lax.rsqrt(var + 1e-05) * ln_gamma + ln_beta
        key = jax.random.key(seed)
        ks = jax.random.split(key, 12)
        B, NS, S = (8, 32, 512)
        sd, td = (STATE_DIM, TOKEN_DIM)
        init = lambda k, shp, fan_in: jax.random.uniform(k, shp, jnp.float32, -1.0, 1.0) / np.sqrt(fan_in)
        return {'states': jax.random.normal(ks[0], (B, NS, sd), jnp.float32), 'tokens': jax.random.normal(ks[1], (B, S, td), jnp.float32), 'attention_mask': jnp.ones((B, S), dtype=bool), 'W_state': init(ks[2], (sd, sd), sd), 'b_state': init(ks[3], (sd,), sd), 'W_token': init(ks[4], (td, sd), td), 'b_token': init(ks[5], (sd,), td), 'W_out': init(ks[6], (sd, sd), sd), 'b_out': init(ks[7], (sd,), sd), 'W_upd': init(ks[8], (2 * sd, sd), 2 * sd), 'b_upd': init(ks[9], (sd,), 2 * sd), 'ln_gamma': jnp.ones((sd,), jnp.float32), 'ln_beta': jnp.zeros((sd,), jnp.float32)}
    _L1_xattn_all = _L1_xattn_setup()
    _L1_xattn_in = {k: v for k, v in _L1_xattn_all.items() if k in ('W_state', 'b_state', 'W_token', 'b_token', 'W_out', 'b_out', 'W_upd', 'b_upd', 'ln_gamma', 'ln_beta')}
    del _L1_xattn_all

    def _L2_xattn_setup():
        import jax, jax.numpy as jnp
        import numpy as np
        B, S, D_MODEL, H, D_FF = (2, 256, 128, 16, 512)
        D_HEAD = D_MODEL // H
        LN_EPS = 1e-05

        def _xavier(key, shape):
            fan_out, fan_in = shape
            std = (2.0 / (fan_in + fan_out)) ** 0.5
            return jax.random.normal(key, shape, dtype=jnp.float32) * std

        def _layer_norm(x, g, b):
            mu = jnp.mean(x, axis=-1, keepdims=True)
            var = jnp.mean((x - mu) ** 2, axis=-1, keepdims=True)
            return (x - mu) * jax.lax.rsqrt(var + LN_EPS) * g + b
        key = jax.random.key(seed)
        ks = jax.random.split(key, 8)
        return {'q': jax.random.normal(ks[0], (B, S, D_MODEL), dtype=jnp.float32), 'k': jax.random.normal(ks[1], (B, S, D_MODEL), dtype=jnp.float32), 'Wq': _xavier(ks[2], (D_MODEL, D_MODEL)), 'bq': jnp.zeros((D_MODEL,), jnp.float32), 'Wk': _xavier(ks[3], (D_MODEL, D_MODEL)), 'bk': jnp.zeros((D_MODEL,), jnp.float32), 'Wv': _xavier(ks[4], (D_MODEL, D_MODEL)), 'bv': jnp.zeros((D_MODEL,), jnp.float32), 'W1': _xavier(ks[5], (D_FF, D_MODEL)), 'b1': jnp.zeros((D_FF,), jnp.float32), 'W2': _xavier(ks[6], (D_MODEL, D_FF)), 'b2': jnp.zeros((D_MODEL,), jnp.float32), 'ln_g': jnp.ones((D_MODEL,), jnp.float32), 'ln_b': jnp.zeros((D_MODEL,), jnp.float32), 'use_causal_mask': 1}
    _L2_xattn_all = _L2_xattn_setup()
    _L2_xattn_in = {k: v for k, v in _L2_xattn_all.items() if k in ('Wq', 'bq', 'Wk', 'bk', 'Wv', 'bv', 'W1', 'b1', 'W2', 'b2', 'ln_g', 'ln_b')}
    del _L2_xattn_all

    def _L3_xattn_setup():
        import jax, jax.numpy as jnp
        import numpy as np
        import math
        EPS_RMS = 1.1920929e-07
        EPS_DEN = 1e-06

        def rmsnorm(x, gamma):
            ms = jnp.mean(x * x, axis=-1, keepdims=True)
            return x * jax.lax.rsqrt(ms + EPS_RMS) * gamma
        key = jax.random.key(seed)
        ks = jax.random.split(key, 8)
        B, T, K, D = (4, 512, 32, 128)
        x_tokens = jax.random.normal(ks[0], (B, T, D), dtype=jnp.float32)
        ctx = jax.random.normal(ks[1], (B, K, D), dtype=jnp.float32)
        idx = jnp.sort(jax.random.randint(ks[2], (B, T), 0, K), axis=-1)
        s = 1.0 / math.sqrt(D)
        Wq = jax.random.normal(ks[3], (D, D), dtype=jnp.float32) * s
        Wk = jax.random.normal(ks[4], (D, D), dtype=jnp.float32) * s
        Wv = jax.random.normal(ks[5], (D, D), dtype=jnp.float32) * s
        Wo = jax.random.normal(ks[6], (D, D), dtype=jnp.float32) * s
        return {'x_tokens': x_tokens, 'ctx': ctx, 'ctx_index_per_token': idx, 'gamma_q': jnp.ones((D,), jnp.float32), 'gamma_kv': jnp.ones((D,), jnp.float32), 'Wq': Wq, 'Wk': Wk, 'Wv': Wv, 'Wo': Wo}
    _L3_xattn_all = _L3_xattn_setup()
    _L3_xattn_in = {k: v for k, v in _L3_xattn_all.items() if k in ('gamma_q', 'gamma_kv', 'Wq', 'Wk', 'Wv', 'Wo')}
    del _L3_xattn_all
    return {'x': x, 'ctx_1024': ctx_1024, 'itok_BxS_0_255': itok_BxS_0_255, 'mask_BxS2_bf1': mask_BxS2_bf1, 'L0_xattn_sa_in_w': _L0_xattn_in['sa_in_w'], 'L0_xattn_sa_in_b': _L0_xattn_in['sa_in_b'], 'L0_xattn_sa_out_w': _L0_xattn_in['sa_out_w'], 'L0_xattn_sa_out_b': _L0_xattn_in['sa_out_b'], 'L0_xattn_ca_q_w': _L0_xattn_in['ca_q_w'], 'L0_xattn_ca_q_b': _L0_xattn_in['ca_q_b'], 'L0_xattn_ca_k_w': _L0_xattn_in['ca_k_w'], 'L0_xattn_ca_k_b': _L0_xattn_in['ca_k_b'], 'L0_xattn_ca_v_w': _L0_xattn_in['ca_v_w'], 'L0_xattn_ca_v_b': _L0_xattn_in['ca_v_b'], 'L0_xattn_ca_o_w': _L0_xattn_in['ca_o_w'], 'L0_xattn_ca_o_b': _L0_xattn_in['ca_o_b'], 'L0_xattn_ffn_w1': _L0_xattn_in['ffn_w1'], 'L0_xattn_ffn_b1': _L0_xattn_in['ffn_b1'], 'L0_xattn_ffn_w2': _L0_xattn_in['ffn_w2'], 'L0_xattn_ffn_b2': _L0_xattn_in['ffn_b2'], 'L0_xattn_ln1_g': _L0_xattn_in['ln1_g'], 'L0_xattn_ln1_b': _L0_xattn_in['ln1_b'], 'L0_xattn_ln2_g': _L0_xattn_in['ln2_g'], 'L0_xattn_ln2_b': _L0_xattn_in['ln2_b'], 'L0_xattn_ln3_g': _L0_xattn_in['ln3_g'], 'L0_xattn_ln3_b': _L0_xattn_in['ln3_b'], 'L1_xattn_W_state': _L1_xattn_in['W_state'], 'L1_xattn_b_state': _L1_xattn_in['b_state'], 'L1_xattn_W_token': _L1_xattn_in['W_token'], 'L1_xattn_b_token': _L1_xattn_in['b_token'], 'L1_xattn_W_out': _L1_xattn_in['W_out'], 'L1_xattn_b_out': _L1_xattn_in['b_out'], 'L1_xattn_W_upd': _L1_xattn_in['W_upd'], 'L1_xattn_b_upd': _L1_xattn_in['b_upd'], 'L1_xattn_ln_gamma': _L1_xattn_in['ln_gamma'], 'L1_xattn_ln_beta': _L1_xattn_in['ln_beta'], 'L2_xattn_Wq': _L2_xattn_in['Wq'], 'L2_xattn_bq': _L2_xattn_in['bq'], 'L2_xattn_Wk': _L2_xattn_in['Wk'], 'L2_xattn_bk': _L2_xattn_in['bk'], 'L2_xattn_Wv': _L2_xattn_in['Wv'], 'L2_xattn_bv': _L2_xattn_in['bv'], 'L2_xattn_W1': _L2_xattn_in['W1'], 'L2_xattn_b1': _L2_xattn_in['b1'], 'L2_xattn_W2': _L2_xattn_in['W2'], 'L2_xattn_b2': _L2_xattn_in['b2'], 'L2_xattn_ln_g': _L2_xattn_in['ln_g'], 'L2_xattn_ln_b': _L2_xattn_in['ln_b'], 'L3_xattn_gamma_q': _L3_xattn_in['gamma_q'], 'L3_xattn_gamma_kv': _L3_xattn_in['gamma_kv'], 'L3_xattn_Wq': _L3_xattn_in['Wq'], 'L3_xattn_Wk': _L3_xattn_in['Wk'], 'L3_xattn_Wv': _L3_xattn_in['Wv'], 'L3_xattn_Wo': _L3_xattn_in['Wo']}

def reference(x, ctx_1024, itok_BxS_0_255, mask_BxS2_bf1, L0_xattn_sa_in_w, L0_xattn_sa_in_b, L0_xattn_sa_out_w, L0_xattn_sa_out_b, L0_xattn_ca_q_w, L0_xattn_ca_q_b, L0_xattn_ca_k_w, L0_xattn_ca_k_b, L0_xattn_ca_v_w, L0_xattn_ca_v_b, L0_xattn_ca_o_w, L0_xattn_ca_o_b, L0_xattn_ffn_w1, L0_xattn_ffn_b1, L0_xattn_ffn_w2, L0_xattn_ffn_b2, L0_xattn_ln1_g, L0_xattn_ln1_b, L0_xattn_ln2_g, L0_xattn_ln2_b, L0_xattn_ln3_g, L0_xattn_ln3_b, L1_xattn_W_state, L1_xattn_b_state, L1_xattn_W_token, L1_xattn_b_token, L1_xattn_W_out, L1_xattn_b_out, L1_xattn_W_upd, L1_xattn_b_upd, L1_xattn_ln_gamma, L1_xattn_ln_beta, L2_xattn_Wq, L2_xattn_bq, L2_xattn_Wk, L2_xattn_bk, L2_xattn_Wv, L2_xattn_bv, L2_xattn_W1, L2_xattn_b1, L2_xattn_W2, L2_xattn_b2, L2_xattn_ln_g, L2_xattn_ln_b, L3_xattn_gamma_q, L3_xattn_gamma_kv, L3_xattn_Wq, L3_xattn_Wk, L3_xattn_Wv, L3_xattn_Wo):
    import jax
    import jax.numpy as jnp

    def _L0_xattn_ref(tgt, memory, sa_in_w, sa_in_b, sa_out_w, sa_out_b, ca_q_w, ca_q_b, ca_k_w, ca_k_b, ca_v_w, ca_v_b, ca_o_w, ca_o_b, ffn_w1, ffn_b1, ffn_w2, ffn_b2, ln1_g, ln1_b, ln2_g, ln2_b, ln3_g, ln3_b):
        import jax, jax.numpy as jnp
        import numpy as np
        D = 128
        H = 16
        DH = D // H
        STRIDE = 4
        EPS = 1e-05
        SCALE = 1.0 / np.sqrt(DH).astype(np.float32)

        def _ln(x, g, b):
            m = jnp.mean(x, axis=-1, keepdims=True)
            v = jnp.mean(jnp.square(x - m), axis=-1, keepdims=True)
            return (x - m) * jax.lax.rsqrt(v + EPS) * g + b
        B, T, _ = tgt.shape
        S = memory.shape[1]

        def heads(x, L):
            return x.reshape(B, L, H, DH).transpose(0, 2, 1, 3)
        qkv = tgt @ sa_in_w.T + sa_in_b
        q, k, v = jnp.split(qkv, 3, axis=-1)
        q, k, v = (heads(q, T), heads(k, T), heads(v, T))
        scores = jnp.einsum('bhtd,bhsd->bhts', q, k) * SCALE
        attn = jax.nn.softmax(scores, axis=-1)
        ctx = jnp.einsum('bhts,bhsd->bhtd', attn, v)
        sa_out = ctx.transpose(0, 2, 1, 3).reshape(B, T, D) @ sa_out_w.T + sa_out_b
        x = _ln(tgt + sa_out, ln1_g, ln1_b)
        q = heads(x @ ca_q_w.T + ca_q_b, T)
        k = heads(memory @ ca_k_w.T + ca_k_b, S)
        v = heads(memory @ ca_v_w.T + ca_v_b, S)
        scores = jnp.einsum('bhtd,bhsd->bhts', q, k) * SCALE
        s_idx = jnp.arange(S)[None, None, None, :]
        h_idx = jnp.arange(H)[None, :, None, None]
        hepos_mask = (s_idx - h_idx) % STRIDE != 0
        scores = jnp.where(hepos_mask, -jnp.inf, scores)
        attn = jax.nn.softmax(scores, axis=-1)
        ctx = jnp.einsum('bhts,bhsd->bhtd', attn, v)
        ca_out = ctx.transpose(0, 2, 1, 3).reshape(B, T, D) @ ca_o_w.T + ca_o_b
        x = _ln(x + ca_out, ln2_g, ln2_b)
        h = jax.nn.gelu(x @ ffn_w1.T + ffn_b1, approximate=False)
        f = h @ ffn_w2.T + ffn_b2
        return _ln(x + f, ln3_g, ln3_b)

    def _L1_xattn_ref(states, tokens, attention_mask, W_state, b_state, W_token, b_token, W_out, b_out, W_upd, b_upd, ln_gamma, ln_beta):
        import jax, jax.numpy as jnp
        import numpy as np
        STATE_DIM = 128
        TOKEN_DIM = 128
        NUM_HEADS = 16
        HEAD_DIM = STATE_DIM // NUM_HEADS

        def _pulse(states, tokens, attention_mask, W_state, b_state, W_token, b_token, W_out, b_out, W_upd, b_upd, ln_gamma, ln_beta):
            B, NS, sd = states.shape
            S = tokens.shape[1]
            H, D = (NUM_HEADS, HEAD_DIM)
            scale = D ** (-0.5)
            q = (states @ W_state + b_state).reshape(B, NS, H, D)
            kv = (tokens @ W_token + b_token).reshape(B, S, H, D)
            scores = jnp.einsum('bnhd,bshd->bhns', q, kv) * scale
            scores = jnp.where(attention_mask[:, None, None, :], scores, -jnp.inf)
            weights = jax.nn.softmax(scores, axis=-1)
            attended = jnp.einsum('bhns,bshd->bnhd', weights, kv).reshape(B, NS, sd)
            attended = attended @ W_out + b_out
            upd = jnp.concatenate([states, attended], axis=-1) @ W_upd + b_upd
            x = states + upd
            mu = jnp.mean(x, axis=-1, keepdims=True)
            var = jnp.var(x, axis=-1, keepdims=True)
            return (x - mu) * jax.lax.rsqrt(var + 1e-05) * ln_gamma + ln_beta
        return _pulse(states, tokens, attention_mask, W_state, b_state, W_token, b_token, W_out, b_out, W_upd, b_upd, ln_gamma, ln_beta)

    def _L2_xattn_ref(q, k, Wq, bq, Wk, bk, Wv, bv, W1, b1, W2, b2, ln_g, ln_b, use_causal_mask):
        import jax, jax.numpy as jnp
        import numpy as np
        B, S, D_MODEL, H, D_FF = (2, 256, 128, 16, 512)
        D_HEAD = D_MODEL // H
        LN_EPS = 1e-05

        def _xavier(key, shape):
            fan_out, fan_in = shape
            std = (2.0 / (fan_in + fan_out)) ** 0.5
            return jax.random.normal(key, shape, dtype=jnp.float32) * std

        def _layer_norm(x, g, b):
            mu = jnp.mean(x, axis=-1, keepdims=True)
            var = jnp.mean((x - mu) ** 2, axis=-1, keepdims=True)
            return (x - mu) * jax.lax.rsqrt(var + LN_EPS) * g + b
        Bq, Sq, _ = q.shape
        Sk = k.shape[1]
        Q = q @ Wq.T + bq
        K = k @ Wk.T + bk
        V = k @ Wv.T + bv
        Q_ = Q.reshape(Bq, Sq, H, D_HEAD).transpose(0, 2, 1, 3)
        K_ = K.reshape(Bq, Sk, H, D_HEAD).transpose(0, 2, 1, 3)
        V_ = V.reshape(Bq, Sk, H, D_HEAD).transpose(0, 2, 1, 3)
        scores = jnp.einsum('bhqd,bhkd->bhqk', Q_, K_) / D_HEAD ** 0.5
        if use_causal_mask:
            causal = jnp.tril(jnp.ones((Sq, Sk), dtype=bool))
            scores = jnp.where(causal, scores, jnp.float32(-1000000000.0))
        sim = jax.nn.softmax(scores, axis=-1)
        att = jnp.einsum('bhqk,bhkd->bhqd', sim, V_)
        att_h = att.transpose(0, 2, 1, 3).reshape(Bq, Sq, D_MODEL)
        att_h = att_h + q
        att_h = _layer_norm(att_h, ln_g, ln_b)
        ff = jax.nn.gelu(att_h @ W1.T + b1, approximate=False) @ W2.T + b2
        return ff + att_h

    def _L3_xattn_ref(x_tokens, ctx, ctx_index_per_token, gamma_q, gamma_kv, Wq, Wk, Wv, Wo):
        import jax, jax.numpy as jnp
        import numpy as np
        import math
        EPS_RMS = 1.1920929e-07
        EPS_DEN = 1e-06

        def rmsnorm(x, gamma):
            ms = jnp.mean(x * x, axis=-1, keepdims=True)
            return x * jax.lax.rsqrt(ms + EPS_RMS) * gamma
        B, T, D = x_tokens.shape
        K = ctx.shape[1]
        H = 16
        hd = D // H

        def split(x):
            return x.reshape(B, -1, H, hd).transpose(0, 2, 1, 3)
        q = split(rmsnorm(x_tokens, gamma_q) @ Wq.T)
        kn = rmsnorm(ctx, gamma_kv)
        k = split(kn @ Wk.T)
        v = split(kn @ Wv.T)
        ctx_pos = jnp.arange(K)[None, None, :]
        mask = (jnp.abs(ctx_pos - ctx_index_per_token[:, :, None]) <= 1)[:, None]
        scores = jnp.einsum('bhqd,bhkd->bhqk', q, k) / math.sqrt(hd)
        w = jnp.square(jax.nn.relu(scores))
        w = jnp.where(mask, w, 0.0)
        denom = jnp.maximum(w.sum(-1, keepdims=True), EPS_DEN)
        out = jnp.einsum('bhqk,bhkd->bhqd', w / denom, v)
        out = out.transpose(0, 2, 1, 3).reshape(B, T, D)
        return x_tokens + out @ Wo.T
    x = _L0_xattn_ref(x, ctx_1024, L0_xattn_sa_in_w, L0_xattn_sa_in_b, L0_xattn_sa_out_w, L0_xattn_sa_out_b, L0_xattn_ca_q_w, L0_xattn_ca_q_b, L0_xattn_ca_k_w, L0_xattn_ca_k_b, L0_xattn_ca_v_w, L0_xattn_ca_v_b, L0_xattn_ca_o_w, L0_xattn_ca_o_b, L0_xattn_ffn_w1, L0_xattn_ffn_b1, L0_xattn_ffn_w2, L0_xattn_ffn_b2, L0_xattn_ln1_g, L0_xattn_ln1_b, L0_xattn_ln2_g, L0_xattn_ln2_b, L0_xattn_ln3_g, L0_xattn_ln3_b)
    x = _L1_xattn_ref(x, ctx_1024, mask_BxS2_bf1, L1_xattn_W_state, L1_xattn_b_state, L1_xattn_W_token, L1_xattn_b_token, L1_xattn_W_out, L1_xattn_b_out, L1_xattn_W_upd, L1_xattn_b_upd, L1_xattn_ln_gamma, L1_xattn_ln_beta)
    x = _L2_xattn_ref(x, ctx_1024, L2_xattn_Wq, L2_xattn_bq, L2_xattn_Wk, L2_xattn_bk, L2_xattn_Wv, L2_xattn_bv, L2_xattn_W1, L2_xattn_b1, L2_xattn_W2, L2_xattn_b2, L2_xattn_ln_g, L2_xattn_ln_b, 1)
    x = _L3_xattn_ref(x, ctx_1024, itok_BxS_0_255, L3_xattn_gamma_q, L3_xattn_gamma_kv, L3_xattn_Wq, L3_xattn_Wk, L3_xattn_Wv, L3_xattn_Wo)
    return x

_drawn_inputs = setup_inputs


def setup_inputs(seed=0):
    import zlib

    import numpy as np

    out = dict(_drawn_inputs(seed))
    spreads = {'L0_xattn_sa_in_b': (0.0, 0.1),
     'L0_xattn_sa_out_b': (0.0, 0.1),
     'L0_xattn_ca_q_b': (0.0, 0.8),
     'L0_xattn_ca_k_b': (0.0, 2.0),
     'L0_xattn_ca_v_b': (0.0, 0.1),
     'L0_xattn_ca_o_b': (0.0, 0.1),
     'L0_xattn_ffn_b1': (0.0, 0.1),
     'L0_xattn_ffn_b2': (0.0, 0.1),
     'L0_xattn_ln1_g': (1.0, 0.2),
     'L0_xattn_ln1_b': (0.0, 0.1),
     'L0_xattn_ln2_g': (1.0, 0.2),
     'L0_xattn_ln2_b': (0.0, 0.1),
     'L0_xattn_ln3_g': (1.0, 0.2),
     'L0_xattn_ln3_b': (0.0, 0.1),
     'L1_xattn_ln_gamma': (1.0, 0.2),
     'L1_xattn_ln_beta': (0.0, 0.1),
     'L2_xattn_bq': (0.0, 0.1),
     'L2_xattn_bk': (0.0, 2.0),
     'L2_xattn_bv': (0.0, 0.1),
     'L2_xattn_b1': (0.0, 0.1),
     'L2_xattn_b2': (0.0, 0.1),
     'L2_xattn_ln_g': (1.0, 0.2),
     'L2_xattn_ln_b': (0.0, 0.1),
     'L3_xattn_gamma_q': (1.0, 0.2),
     'L3_xattn_gamma_kv': (1.0, 0.2)}
    factors = {'L0_xattn_ca_q_w': 6.868,
     'L0_xattn_ca_k_w': 7.93,
     'L1_xattn_b_state': 5.452,
     'L0_xattn_sa_in_w': 2.668}
    for name, (base, spread) in spreads.items():
        noise = np.random.default_rng([zlib.crc32(name.encode()), seed]).standard_normal(out[name].shape)
        drawn = base * np.exp(spread * noise) if base else spread * noise
        out[name] = jnp.asarray(drawn.astype(out[name].dtype))
    for name, factor in factors.items():
        out[name] = (out[name] * factor).astype(out[name].dtype)
    return out
```

```python
import concourse.bass as bass
from concourse import mybir
from contextlib import ExitStack

B, T, D, H, DH = 16, 64, 128, 16, 8
TOK = B * T
G = 4
GB = B // G
GT = GB * T
NJ = GT // 128
SP_ = H // 2
TERMS = 6
Q_PART = (0, 0, 0, 1, 1, 2)
K_PART = (0, 1, 2, 0, 1, 0)
R_TERMS = TERMS * 16
R_MASK = R_TERMS + 2
R_ALL = R_MASK + 4
STRIDE = 4
K16 = T // STRIDE
F_CHUNKS = 4
EPS = 1e-5
EPS_RMS = 1.1920929e-07
EPS_DEN = 1e-6
SCALE = DH ** -0.5
BIG = 1e30
KEY_BIG = 3e38
CST = 397

MATS = ["ident", "center", "sa_q", "sa_k", "sa_v",
        "ca_q", "ca_k", "ca_v", "l1_q", "l1_k", "l1_v", "sa_o", "ca_o", "l1_updT", "l1_updsT", "l1_outT",
        "l2_q", "l2_k", "l2_v", "l3_q", "l3_k", "l3_v", "l3_o",
        "f_w1_0", "f_w1_1", "f_w1_2", "f_w1_3", "f_w2_0", "f_w2_1", "f_w2_2", "f_w2_3",
        "g_w1_0", "g_w1_1", "g_w1_2", "g_w1_3", "g_w2_0", "g_w2_1", "g_w2_2", "g_w2_3"]
FIRST_MATS = 5
COLS = ["sa_qb", "sa_kb", "ca_qb", "ca_kb", "l1_qb", "l1_kb", "l2_qb", "l2_kb",
        "sa_vb", "sa_ob", "ca_vb", "ca_ob", "f_b2", "l1_tb", "l1_ob", "l1_ub", "l2_vb", "g_b2",
        "sa_lg", "sa_lb", "ca_lg", "ca_lb", "f_lg", "f_lb", "l1_lg", "l1_lb", "l2_lg", "l2_lb",
        "l3_gq", "l3_gk", "f_b1_0", "f_b1_1", "f_b1_2", "f_b1_3", "g_b1_0", "g_b1_1", "g_b1_2", "g_b1_3"]
USES = ["mats", "sa_k", "sa_q", "sa_v", "ca_k", "ca_v",
        "sa_m", "sa_av", "sa_t", "sa_z", "sa_x",
        "l1_k", "l1_v", "ca_q", "ca_m", "ca_av", "ca_t", "ca_z", "ca_x",
        "l2_k", "l2_v", "l3_n", "f_h0", "f_h1", "f_z", "f_x",
        "l1_q", "l1_m", "l1_av", "l1_t", "l1_z", "l1_x",
        "l3_k", "l3_v", "l2_q", "l2_m", "l2_av", "l2_t", "l2_z", "l2_x",
        "g_h0", "g_h1", "g_y", "l3_q", "l3_ms", "l3_av", "l3_t", "l3_z"]
ATT = ["sa", "ca", "l1", "l2", "l3"]
NORMS = ["sa", "ca", "f", "l1", "l2"]
S_UNITS = {"sa": NJ * 2, "ca": 1, "l1": NJ * 2, "l2": NJ * 2}
T_UNITS = {"sa": GB, "ca": 1, "l1": GB, "l2": GB, "l3": GB}
LAG = 2
P_SLOTS = 4
STACK = {"sa": 0, "l1": 1, "l2": 0, "l3": 1}
V_BASE = {"sa": 1, "ca": 2, "l1": 1, "l2": 3, "l3": 1}
VALUES = {"sa": 0, "ca": 1, "l1": 0, "l2": 1, "l3": 0}
WC_OF = {"sa": 0, "ca": 1, "l1_upd": 2, "l1_res": 3, "f": 4, "l1": 8}
ROW_OF = {"sa": 0, "ca": 1, "f": 2, "l1": 3, "l2": 4}
X_OF = {"x0": 0, "x1": 1, "x2": 0, "x3": 1, "x4": 0, "x5": 1, "x6": 0}
X_FROM = {"x1": "sa", "x2": "ca", "x3": "f", "x4": "l1", "x5": "l2"}


def filled(use):
    return sum(not u.endswith("_av") for u in USES[:USES.index(use) + 1])


def attn(name, g=G - 1):
    return G * ATT.index(name) + g + 1


def norm(name, g=G - 1):
    return G * NORMS.index(name) + g + 1


def s_unit(name, g, i=0):
    return sum(G * S_UNITS[x] for x in ATT[:ATT.index(name)]) + g * S_UNITS[name] + i


def t_unit(name, g, i=0):
    return sum(G * T_UNITS[x] for x in ATT[:ATT.index(name)]) + g * T_UNITS[name] + i


def last_t(name, g):
    return t_unit(name, g, T_UNITS[name] - 1)


def last_read(use, g):
    name, step = use.split("_") if "_" in use else ("", use)
    if use == "mats":
        return [(f"mats_used{g}", 2 if g == 2 else 1)]
    if use == "ca_v":
        return [("v_even", attn(name, g))]
    if use == "l3_n":
        return [("ctx_normed_T", g + 1)]
    if use == "g_y":
        return [("x6", g + 1)]
    if use == "l3_ms":
        return [("l3_floor", g + 1)]
    if step in ("h0", "h1"):
        return [(f"{name}_gelu{step[1]}", 2 * (g + 1))]
    if step == "v":
        return [("v_even", attn(name, g)), ("v_odd", attn(name, g) - (G if name != "sa" else 0))]
    if step in ("z", "x"):
        return [({"z": "ln_scaled", "x": "ln_done"}[step], norm(name, g))]
    return [({"k": "k_first", "q": "q_first", "m": "m_row_ready", "av": "att_ready", "t": "attT_ready"}[step],
             attn(name, g))]


def build(nc, a, out):
    F, BF = mybir.dt.float32, mybir.dt.bfloat16
    ALU, ACT, AX = mybir.AluOpType, mybir.ActivationFunctionType, mybir.AxisListType
    ctx = ExitStack()
    with ctx:
        def sb(name, shape, dt=F):
            return ctx.enter_context(nc.sbuf_tensor(f"{name}_sb", shape, dt))

        sems = {}

        def sem(name):
            if name not in sems:
                sems[name] = ctx.enter_context(nc.semaphore(name))
            return sems[name]

        W = sb("W", [128, len(MATS), 128])
        V = sb("V", [128, len(COLS)])

        def mat(n):
            return W[:, MATS.index(n), :]

        def col(n):
            return V[:, COLS.index(n):COLS.index(n) + 1]

        x_buf = [sb("xa", [128, TOK]), sb("xb", [128, TOK])]
        ctxT = sb("ctxT", [128, TOK])
        hid = sb("hid", [128, F_CHUNKS, TOK])
        k_full = hid[:, 0, :].rearrange("p (g n) -> p g n", g=G)
        k_rest = hid[:, 1, :].rearrange("p (g n) -> p g n", g=G)
        k_ones = hid[0:4, 2, :].bitcast(BF).rearrange("p (e n) -> p e n", e=2)
        cn = hid[:, 3, :].rearrange("p (n d) -> p n d", d=128)
        q_full = sb("q_full", [128, G, GT])
        q_rest = sb("q_rest", [128, G, GT])
        q_part = sb("q_part", [128, 3, G, GT], BF)
        k_part = sb("k_part", [128, 3, TOK], BF)
        attT = q_full
        att = q_rest[:, :, :].rearrange("p g (j d) -> p g j d", j=NJ)
        y_tok = att
        fin = q_full
        q_stack = sb("q_stack", [128, G, SP_, GT], BF)
        k_stack = [sb(f"k_stack{i}", [128, SP_, 2, TOK], BF) for i in range(2)]
        kc_stack = sb("kc_stack", [128, SP_, 2, K16 * B], BF)
        ctx_rep = (k_stack[1][:, :, :, :].rearrange("p s e n -> p (s e n)").bitcast(F)[:, 0:4 * TOK]
                   .rearrange("p (b c a e k) -> p b c a e k", b=B, c=2, a=4, e=2))
        v_ext = [sb(f"v_ext{i}", [128, B, SP_, 2, DH + 1]) for i in range(2)]
        probs = sb("probs", [128, P_SLOTS, SP_ * T])
        relu = sb("relu", [128, 2, SP_ * T])
        idx = relu[0:64, :, :].bitcast(mybir.dt.int32).rearrange("p a n -> p (a n)")
        dist = probs[0:64, 0:2, :].rearrange("p a n -> p (a n)")
        m_col = sb("m_col", [128, G, NJ, SP_, 2])
        m_part = sb("m_part", [128, G, NJ, 2, 2, SP_], BF)
        m_row = sb("m_row", [32, G, GT], BF)
        rden = sb("rden", [128, G, NJ, H])
        var = sb("var", [128, G, NJ])
        vare = sb("vare", [128, G, NJ])
        rstd = sb("rstd", [128, G, NJ])
        half = sb("half", [128, 8])
        WC = sb("WC", [128, 9, 128])
        rows = sb("rows", [1, 5, 128])
        ones_row = sb("ones_row", [1, 128])
        ones_col = sb("ones_col", [128, 1])
        identb = sb("identb", [128, 128], BF)
        cst = sb("cst", [128, CST])
        two_i = sb("two_i", [64, 128], BF)
        causal = sb("causal", [64, 2, 64], BF)
        e_mask = cst[:, CST - 8:CST]
        q_ones = sb("q_ones", [2, GT], BF)
        km_u8 = sb("km_u8", [1, TOK], mybir.dt.uint8)
        km = sb("km", [1, TOK], BF)
        band = sb("band", [64, TOK], BF)
        cms = sb("cms", [128, B // 2])
        cmse = sb("cmse", [128, B // 2])
        crs = sb("crs", [128, B // 2])
        floor = sb("floor", [128, G, NJ])
        bank = [ctx.enter_context(nc.psum_tensor(f"bank{g}", [128, 512], F)) for g in range(G)]
        s_bank = [ctx.enter_context(nc.psum_tensor(f"s_bank{i}", [128, 512], F)) for i in range(2)]
        t_bank = [ctx.enter_context(nc.psum_tensor(f"t_bank{i}", [128, 512], F)) for i in range(2)]
        full = [sem(f"bank_full{g}") for g in range(G)]

        def X(x):
            return x_buf[X_OF[x]]

        def tok(g):
            return slice(g * GT, (g + 1) * GT)

        def keys(stack, rows_, s, b):
            return stack[0:rows_, s, :, :].rearrange("p e n -> p (e n)").rearrange("p (x b) -> p x b", b=B)[:, :, b]

        def use_full(eng, g, use):
            eng.wait_ge(full[g], filled(use))

        def stacked_k(eng, name):
            n = TERMS * (4 if name == "ca" else 2) + (2 if name == "l1" else 0)
            eng.wait_ge(sem(f"{name}_k_stacked"), 16 * n)

        def paired(name, side, t, g, x):
            if side == "q":
                return q_part[:, t, g, :], x
            if name == "ca":
                return (k_part[:, t, :].rearrange("p (r k b) -> p b k r", r=STRIDE, b=B)[:, g * GB:(g + 1) * GB],
                        x.rearrange("p (b k r) -> p b k r", b=GB, r=STRIDE))
            return (k_part[:, t, :].rearrange("p (k b) -> p b k", b=B)[:, g * GB:(g + 1) * GB],
                    x.rearrange("p (b k) -> p b k", b=GB))

        block = ctx.enter_context(nc.Block())

        @block.sync
        def _(sp):
            sp.dma_start(x_buf[0][:], a["xT"]).then_inc(sem("x_loaded"), 16)
            sp.dma_start(W[:, 0:FIRST_MATS, :], a["mats"][:, 0:FIRST_MATS, :]).then_inc(sem("w1_loaded"), 16)
            sp.dma_start(V[:], a["cols"]).then_inc(sem("v_loaded"), 16)
            sp.dma_start(cst[:], a["consts"]).then_inc(sem("cst_loaded"), 16)
            sp.dma_start(ctxT[:], a["ctxT"]).then_inc(sem("ctx_loaded"), 16)
            sp.dma_start(W[:, FIRST_MATS:, :], a["mats"][:, FIRST_MATS:, :]).then_inc(sem("w2_loaded"), 16)
            sp.dma_start(km_u8[:], a["key_mask"]).then_inc(sem("km_loaded"), 16)
            sp.dma_start(idx, a["idx"].to_broadcast([64, TOK])).then_inc(sem("idx_loaded"), 16)
            sp.dma_start(cn, a["ctx"].rearrange("(n p) d -> p n d", p=128)).then_inc(sem("cn_loaded"), 16)

            def stack_k(name):
                ks = k_stack[STACK[name]]
                sp.wait_ge(sem("k_low"), attn(name))
                sp.wait_ge(sem(f"k_zero{STACK[name]}"), 1 if STACK[name] else 2)
                if name in ("l2", "l3"):
                    sp.wait_ge(sem("t_full"), last_t({"l2": "sa", "l3": "l1"}[name], G - 1) + 1)
                for t in range(TERMS):
                    for e in range(2):
                        r = 16 * t + 8 * e
                        sp.dma_start(ks[r:r + 8, :, e, :], k_part[64 * e:64 * e + 64, K_PART[t], :]
                                     ).then_inc(sem(f"{name}_k_stacked"), 16)

            def constant_rows(i):
                sp.wait_ge(sem(f"k_zero{i}"), 1 if i else 2)
                sp.dma_start(k_stack[i][R_MASK:R_ALL, :, :, :].rearrange("r s e n -> r s (e n)"),
                             k_ones.rearrange("r e n -> r (e n)").unsqueeze(1).to_broadcast([4, SP_, 2 * TOK])
                             ).then_inc(sem(f"k_rows{i}"), 16)

            def stack_q(name):
                for g in range(G):
                    sp.wait_ge(sem("q_low"), attn(name, g))
                    if name != "sa":
                        sp.wait_ge(sem("t_full"), last_t(ATT[ATT.index(name) - 1], g) + 1)
                    for t in range(TERMS):
                        sp.dma_start(q_stack[16 * t:16 * t + 16, g, :, :], q_part[:, Q_PART[t], g, :]
                                     ).then_inc(sem(f"q_stacked{g}"), 16)

            def stack_m(name):
                for g in range(G):
                    sp.wait_ge(sem("m_row_ready"), attn(name, g))
                    sp.dma_start(q_stack[R_MASK:R_ALL, g, :, :], m_row[:, g, :]
                                 ).then_inc(sem(f"m_stacked{g}"), 16)

            stack_k("sa")
            stack_q("sa")
            sp.wait_ge(sem("const_ready"), 6)
            sp.dma_start(q_stack[R_TERMS:R_MASK, :, :, :].rearrange("r g s n -> r (g s) n"),
                         q_ones[:].unsqueeze(1).to_broadcast([2, G * SP_, GT])).then_inc(sem("q_ones_stacked"), 16)
            constant_rows(0)
            stack_m("sa")
            sp.wait_ge(sem("kc_zero"), 1)
            for e in range(2):
                sp.dma_start(kc_stack[R_MASK:R_ALL, :, e, :],
                             k_ones[:, e, 0:B * K16].unsqueeze(1).to_broadcast([4, SP_, B * K16])
                             ).then_inc(sem("kc_rows"), 16)
            sp.wait_ge(sem("k_low"), attn("ca"))
            for t in range(TERMS):
                for e in range(2):
                    for pi in range(2):
                        r, res = 16 * t + 8 * e, 2 * pi + e
                        sp.dma_start(kc_stack[r:r + 8, pi::2, e, :],
                                     k_part[64 * e + pi:64 * e + 64:2, K_PART[t], 256 * res:256 * res + 256]
                                     ).then_inc(sem("ca_k_stacked"), 16)
            stack_q("ca")
            constant_rows(1)
            stack_k("l1")
            sp.wait_ge(sem("km_ready"), 1)
            for e in range(2):
                sp.dma_start(k_stack[1][R_TERMS + e:R_TERMS + e + 1, :, e, :],
                             km[:].unsqueeze(1).to_broadcast([1, SP_, TOK])).then_inc(sem("l1_k_stacked"), 16)
            stack_m("ca")
            stack_k("l2")
            stack_q("l1")
            stack_m("l1")
            stack_q("l2")
            stack_k("l3")
            stack_m("l2")
            stack_q("l3")
            for g in range(G):
                sp.wait_ge(sem("fin_ready"), g + 1)
                sp.dma_start(out[g * GT:(g + 1) * GT, :].rearrange("(j p) d -> p j d", p=128),
                             fin[:, g, :].rearrange("p (j d) -> p j d", j=NJ)).then_inc(sem("stored"), 16)
            sp.wait_ge(sem("stored"), 16 * G)

        @block.tensor
        def _(pe):
            def take(g, use):
                if USES.index(use):
                    for name, n in last_read(USES[USES.index(use) - 1], g):
                        pe.wait_ge(sem(name), n)

            def mm(o, l, r, start=True, stop=True):
                return pe.matmul(o, l, r, start=start, stop=stop)

            def x_ready(x, g):
                if x == "x0":
                    pe.wait_ge(sem("x_loaded"), 16)
                elif x == "x6":
                    pe.wait_ge(sem("x6"), g + 1)
                else:
                    pe.wait_ge(sem("ln_done"), norm(X_FROM[x], g))

            def project(name, side, src, x=None):
                for g in range(G):
                    if x:
                        x_ready(x, g)
                    take(g, f"{name}_{side}")
                    mm(bank[g][:, 0:GT], mat(f"{name}_{side}"), src[:, tok(g)]).then_inc(full[g], 1)

            def values(name, src):
                for g in range(G):
                    take(g, f"{name}_v")
                    for i in range(GB):
                        b = g * GB + i
                        for e in range(2):
                            w = mat(f"{name}_v").rearrange("p (s e n) -> p s e n", e=2, n=DH)[:, :, e, :]
                            last = mm(bank[g][64 * e:64 * e + 64, i * 64:(i + 1) * 64].rearrange(
                                "p (s n) -> p s n", n=DH), src[:, b * T:(b + 1) * T], w)
                    last.then_inc(full[g], 1)

            def values_ca():
                for g in range(G):
                    take(g, "ca_v")
                    pe.wait_ge(sem("ctx_rep_ready"), 4)
                    for i in range(GB):
                        b = g * GB + i
                        for pi in range(2):
                            keys = ctx_rep[:, b, pi, :, :, :].rearrange("p a e k -> p (a e k)")
                            w = mat("ca_v").rearrange("p (a c n) -> p a c n", a=4, c=2)[:, :, pi, :]
                            o = (i * 2 + pi) * 64
                            last = mm(bank[g][:, o:o + 64].rearrange("p (a n) -> p a n", a=4), keys, w)
                    last.then_inc(full[g], 1)

            def scores(name, g, i):
                u = s_unit(name, g, i)
                if i == 0:
                    pe.wait_ge(sem(f"q_stacked{g}"), 16 * TERMS * (ATT.index(name) + 1))
                    stacked_k(pe, name)
                if u >= 2:
                    pe.wait_ge(sem("m_reduced"), u - 1)
                o = s_bank[u % 2]
                if name == "ca":
                    for ii in range(GB):
                        b, c = g * GB + ii, 64 * (ii % 2)
                        for s in range(SP_):
                            k = (ii // 2) * 256 + s * 32
                            last = mm(o[c:c + 64, k:k + 32], q_stack[0:R_TERMS, g, s, ii * T:(ii + 1) * T],
                                      keys(kc_stack, R_TERMS, s, b))
                    last.then_inc(sem("s_full"), 1)
                    return
                r = R_MASK if name == "l1" else R_TERMS
                j, hf = i // 2, i % 2
                if name == "l2":
                    mm(o[:, :].rearrange("p (c k) -> p c k", c=8), two_i[:, :],
                       causal[:, 0, :].unsqueeze(1).to_broadcast([64, 8, 64]))
                for c in range(2):
                    t = (2 * j + c) * T
                    b = g * GB + 2 * j + c
                    for s4 in range(4):
                        s = 4 * hf + s4
                        last = pe.matmul(o[64 * c:64 * c + 64, s4 * 128:(s4 + 1) * 128],
                                         q_stack[0:r, g, s, t:t + T],
                                         keys(k_stack[STACK[name]], r, s, b),
                                         start=name != "l2", stop=True, skip_group_check=name == "l2")
                last.then_inc(sem("s_full"), 1)

            def max_rows(name, g):
                take(g, f"{name}_m")
                pe.wait_ge(sem("m_lo"), attn(name, g))
                o = bank[g][0:32, 0:GT // 2].bitcast(BF)
                for j in range(NJ):
                    last = pe.transpose(o[:, j * 128:(j + 1) * 128],
                                        m_part[:, g, j, :, :, :].rearrange("p a e s -> p (a e s)"), identb[:, :])
                last.then_inc(full[g], 1)

            def scores_t(name, g, i):
                u = t_unit(name, g, i)
                if i == 0:
                    if name == "l3":
                        pe.wait_ge(sem(f"q_stacked{g}"), 16 * TERMS * (ATT.index(name) + 1))
                        stacked_k(pe, name)
                        pe.wait_ge(sem("band_ready"), 1)
                    else:
                        pe.wait_ge(sem(f"m_stacked{g}"), 16 * (ATT.index(name) + 1))
                        pe.wait_ge(sem("q_ones_stacked"), 16)
                        if name == "ca":
                            pe.wait_ge(sem("kc_rows"), 32)
                        else:
                            pe.wait_ge(sem(f"k_rows{STACK[name]}"), 16)
                n = u - t_unit("l3", 0)
                if n >= 2:
                    pe.wait_ge(sem("l3_relu"), n - 1)
                elif u >= 2:
                    pe.wait_ge(sem("p_ready"), u - 1)
                o = t_bank[u % 2]
                if name == "ca":
                    for ii in range(GB):
                        b = g * GB + ii
                        for s in range(SP_):
                            c, k = 32 * (s // 2), ii * 128 + (s % 2) * 64
                            last = mm(o[c:c + 32, k:k + 64], keys(kc_stack, R_ALL, s, b),
                                      q_stack[0:R_ALL, g, s, ii * T:(ii + 1) * T])
                    last.then_inc(sem("t_full"), 1)
                    return
                b = g * GB + i
                r = R_TERMS if name == "l3" else R_ALL
                masked = name in ("l2", "l3")
                if masked:
                    m = causal[:, 1, :] if name == "l2" else band[:, b * T:(b + 1) * T]
                    mm(o[:, :].rearrange("p (s q) -> p s q", s=SP_), two_i[:, :],
                       m.unsqueeze(1).to_broadcast([64, SP_, 64]))
                for s in range(SP_):
                    last = pe.matmul(o[:, s * T:(s + 1) * T], keys(k_stack[STACK[name]], r, s, b),
                                     q_stack[0:r, g, s, i * T:(i + 1) * T],
                                     start=not masked, stop=True, skip_group_check=masked)
                last.then_inc(sem("t_full"), 1)

            def attend(name, g, i):
                u = t_unit(name, g, i)
                if i == 0:
                    take(g, f"{name}_av")
                    pe.wait_ge(sem("v_even"), attn(name))
                    pe.wait_ge(sem("v_odd"), attn(name) - (G if name != "sa" else 0))
                    pe.wait_ge(sem("v_base"), V_BASE[name])
                pe.wait_ge(sem("p_ready"), u + 1)
                ve = v_ext[VALUES[name]]
                for ii in range(GB) if name == "ca" else (i,):
                    b = g * GB + ii
                    c = 64 * (ii % 2)
                    o = bank[g][c:c + 64, (ii // 2) * 144:(ii // 2) * 144 + 144]
                    if name == "ca":
                        for pi in range(2):
                            last = mm(o.rearrange("p (a c n) -> p a c n", a=4, c=2)[:, :, pi, :],
                                      probs[:, u % P_SLOTS, ii * 128 + pi * 64:ii * 128 + pi * 64 + 64],
                                      ve[:, b, :, :, :].rearrange("p s e n -> p (s e n)")[:, pi * 72:pi * 72 + 72]
                                      .rearrange("p (a n) -> p a n", a=4))
                    else:
                        for s in range(SP_):
                            last = mm(o[:, s * 18:s * 18 + 18], probs[:, u % P_SLOTS, s * T:(s + 1) * T],
                                      ve[:, b, s, :, :].rearrange("p e n -> p (e n)"))
                last.then_inc(sem("p_used"), 1)

            def attention(name):
                ns, nt = S_UNITS.get(name, 0), T_UNITS[name]
                for step in range(G + LAG):
                    for i in range(max(ns, nt)):
                        if step < G and i < ns:
                            scores(name, step, i)
                        if i == min(1, max(ns, nt) - 1) and 1 <= step <= G and ns:
                            max_rows(name, step - 1)
                        if step >= LAG and i < nt:
                            scores_t(name, step - LAG, i)
                            if i >= 1:
                                attend(name, step - LAG, i - 1)
                    if step >= LAG:
                        attend(name, step - LAG, nt - 1)

            def flip(use, src, signal, counts):
                for g in range(G):
                    take(g, use)
                    pe.wait_ge(sem(signal), counts(use.split("_")[0], g))
                    for j in range(NJ):
                        last = pe.transpose(bank[g][:, j * 128:(j + 1) * 128], src[:, g, j, :], mat("ident"))
                    last.then_inc(full[g], 1)

            def centred(name, x, res):
                for g in range(G):
                    take(g, f"{name}_z")
                    if name == "f":
                        pe.wait_ge(sem("f_gelu0"), 2 * (g + 1))
                        pe.wait_ge(sem("f_gelu1"), 2 * (g + 1))
                    else:
                        pe.wait_ge(sem("attT_ready"), attn(name, g))
                    for j in range(NJ):
                        o = bank[g][:, j * 128:(j + 1) * 128]
                        t = slice(g * GT + j * 128, g * GT + (j + 1) * 128)
                        mm(o, X(x)[:, t], res, stop=False)
                        if name == "f":
                            for c in range(F_CHUNKS):
                                mm(o, hid[:, c, t], WC[:, WC_OF["f"] + c, :], start=False, stop=False)
                        else:
                            w = mat("center") if name == "l2" else WC[:, WC_OF[name], :]
                            mm(o, attT[:, g, j * 128:(j + 1) * 128], w, start=False, stop=False)
                        last = mm(o, ones_row[:, :], rows[:, ROW_OF[name], :], start=False)
                    last.then_inc(full[g], 1)

            def finish(name, x, res):
                if name != "f":
                    flip(f"{name}_t", att, "att_ready", attn)
                centred(name, x, res)
                flip(f"{name}_x", y_tok, "ln_scaled", norm)

            def hidden(name, x):
                for hh in range(2):
                    for g in range(G):
                        x_ready(x, g)
                        take(g, f"{name}_h{hh}")
                        for c in range(2):
                            last = mm(bank[g][:, c * GT:(c + 1) * GT], mat(f"{name}_w1_{2 * hh + c}"),
                                      X(x)[:, tok(g)])
                        last.then_inc(full[g], 1)

            pe.wait_ge(sem("w1_loaded"), 16)
            pe.wait_ge(sem("w2_loaded"), 16)
            for c, n in enumerate(["sa_o", "ca_o", "l1_updT"]):
                mm(bank[0][:, c * 128:(c + 1) * 128], mat(n), mat("center"))
            mm(bank[0][:, 384:512], mat("l1_updsT"), mat("center"), stop=False)
            mm(bank[0][:, 384:512], mat("ident"), mat("center"), start=False).then_inc(full[0], 1)
            for c in range(F_CHUNKS):
                last = mm(bank[1][:, c * 128:(c + 1) * 128], mat(f"f_w2_{c}"), mat("center"))
            last.then_inc(full[1], 1)
            pe.wait_ge(sem("mats_used0"), 1)
            pe.wait_ge(sem("v_loaded"), 16)
            mm(bank[2][:, 0:128], mat("l1_outT"), WC[:, WC_OF["l1_upd"], :])
            mm(bank[2][0:1, 128:256], col("l2_vb"), mat("center")).then_inc(full[2], 1)
            pe.wait_ge(sem("mats_used2"), 2)
            for name, parts in (("sa", [("sa_vb", WC[:, 0, :]), ("sa_ob", mat("center"))]),
                                ("ca", [("ca_vb", WC[:, 1, :]), ("ca_ob", mat("center"))]),
                                ("f", [("f_b2", mat("center"))]),
                                ("l1", [("l1_tb", WC[:, 8, :]), ("l1_ob", WC[:, WC_OF["l1_upd"], :]),
                                        ("l1_ub", mat("center"))])):
                o = ROW_OF[name] * 128
                for n, (c, m) in enumerate(parts):
                    last = mm(bank[3][0:1, o:o + 128], col(c), m, start=n == 0, stop=n == len(parts) - 1)
            last.then_inc(full[3], 1)

            pe.wait_ge(sem("x_loaded"), 16)
            project("sa", "k", x_buf[0])
            project("sa", "q", x_buf[0])
            values("sa", x_buf[0])
            pe.wait_ge(sem("ctx_loaded"), 16)
            project("ca", "k", ctxT)
            values_ca()
            pe.wait_ge(sem("const_ready"), 6)
            attention("sa")
            finish("sa", "x0", mat("center"))
            project("l1", "k", ctxT)
            values("l1", ctxT)
            project("ca", "q", X("x1"), "x1")
            attention("ca")
            finish("ca", "x1", mat("center"))
            project("l2", "k", ctxT)
            values("l2", ctxT)
            pe.wait_ge(sem("cn_scaled"), 1)
            for g in range(G):
                take(g, "l3_n")
                for j in range(NJ):
                    last = pe.transpose(bank[g][:, j * 128:(j + 1) * 128], cn[:, g * NJ + j, :], mat("ident"))
                last.then_inc(full[g], 1)
            hidden("f", "x2")
            finish("f", "x2", mat("center"))
            project("l1", "q", X("x3"), "x3")
            attention("l1")
            finish("l1", "x3", WC[:, WC_OF["l1_res"], :])
            pe.wait_ge(sem("ctx_normed_T"), G)
            pe.wait_ge(sem("gamma_folded"), 3)
            project("l3", "k", ctxT)
            values("l3", ctxT)
            project("l2", "q", X("x4"), "x4")
            attention("l2")
            finish("l2", "x4", mat("center"))
            hidden("g", "x5")
            for g in range(G):
                take(g, "g_y")
                pe.wait_ge(sem("g_gelu0"), 2 * (g + 1))
                for c in range(F_CHUNKS):
                    last = mm(bank[g][:, 0:GT], mat(f"g_w2_{c}"), hid[:, c, tok(g)], start=c == 0,
                              stop=c == F_CHUNKS - 1)
                last.then_inc(full[g], 1)
            project("l3", "q", X("x6"), "x6")
            for g in range(G):
                take(g, "l3_ms")
                pe.wait_ge(sem("l3_sq"), g + 1)
                for j in range(NJ):
                    last = mm(bank[g][:, j:j + 1], k_full[:, g, j * 128:(j + 1) * 128], ones_col[:, :])
                last.then_inc(full[g], 1)
            for g in range(G):
                for i in range(GB):
                    scores_t("l3", g, i)
                    if i >= 1:
                        attend("l3", g, i - 1)
                attend("l3", g, GB - 1)
            flip("l3_t", att, "att_ready", attn)
            for g in range(G):
                take(g, "l3_z")
                for j in range(NJ):
                    o = bank[g][:, j * 128:(j + 1) * 128]
                    mm(o, X("x6")[:, g * GT + j * 128:g * GT + (j + 1) * 128], mat("ident"), stop=False)
                    last = mm(o, attT[:, g, j * 128:(j + 1) * 128], mat("l3_o"), start=False)
                last.then_inc(full[g], 1)

        @block.scalar
        def _(act):
            def parts(name, side):
                for g in range(G):
                    use_full(act, g, f"{name}_{side}")
                    if side == "q":
                        dst = q_full[:, g, :]
                        if name != "sa":
                            act.wait_ge(sem(f"q_stacked{g}"), 16 * TERMS * ATT.index(name))
                    else:
                        dst = k_full[:, g, :]
                        if name != "sa":
                            before = ATT[ATT.index(name) - 1]
                            stacked_k(act, before)
                            act.wait_ge(sem("k_low"), attn(before, g))
                    src = bank[g][:, 0:GT]
                    if name == "l3":
                        act.activation(dst, src, ACT.Copy).then_inc(sem(f"{side}_whole"), 1)
                        act.activation(*paired(name, side, 0, g, src), ACT.Copy).then_inc(sem(f"{side}_first"), 1)
                        continue
                    bias = col(f"{name}_{side}b")
                    act.activation(dst, src, ACT.Identity, bias=bias, scale=1.0).then_inc(sem(f"{side}_whole"), 1)
                    act.activation(*paired(name, side, 0, g, src), ACT.Identity, bias=bias, scale=1.0
                                   ).then_inc(sem(f"{side}_first"), 1)

            def value_half(name):
                for g in range(G):
                    use_full(act, g, f"{name}_v")
                    if g == 0:
                        act.wait_ge(sem("v_base"), V_BASE[name])
                        if name in ("l1", "l3"):
                            act.wait_ge(sem("p_used"), last_t({"l1": "sa", "l3": "l1"}[name], G - 1) + 1)
                    src = bank[g][64:128, 0:256].rearrange("p (c d) -> p c d", d=DH)
                    dst = v_ext[VALUES[name]][64:128, g * GB:(g + 1) * GB, :, :, :].rearrange("p b s e n -> p (b s) e n")
                    act.activation(dst[:, :, 1, 0:DH], src, ACT.Copy).then_inc(sem("v_odd"), 1)

            def exps(name, g, i):
                u = t_unit(name, g, i)
                act.wait_ge(sem("t_full"), u + 1)
                if u >= P_SLOTS:
                    act.wait_ge(sem("p_used"), u - P_SLOTS + 1)
                act.activation(probs[:, u % P_SLOTS, :], t_bank[u % 2][:, :], ACT.Exp, scale=SCALE
                               ).then_inc(sem("p_ready"), 1)

            def max_rows(name, g):
                use_full(act, g, f"{name}_m")
                if name != "sa":
                    act.wait_ge(sem(f"m_stacked{g}"), 16 * ATT.index(name))
                act.activation(m_row[:, g, :], bank[g][0:32, 0:GT // 2].bitcast(BF), ACT.Copy
                               ).then_inc(sem("m_row_ready"), 1)

            def attention(name):
                n = max(S_UNITS[name], T_UNITS[name])
                for step in range(G + LAG):
                    for i in range(n):
                        if i == min(1, n - 1) and 1 <= step <= G:
                            max_rows(name, step - 1)
                        if step >= LAG and i < T_UNITS[name]:
                            exps(name, step - LAG, i)

            def projected(name):
                for g in range(G):
                    use_full(act, g, f"{name}_t")
                    act.activation(attT[:, g, :], bank[g][:, 0:GT], ACT.Copy).then_inc(sem("attT_ready"), 1)

            def normalised(name, x):
                for g in range(G):
                    use_full(act, g, f"{name}_z")
                    if name == "f" and g == 0:
                        act.wait_ge(sem("attT_ready"), attn("ca"))
                    for j in range(NJ):
                        act.activation(att[:, g, j, :], bank[g][:, j * 128:(j + 1) * 128], ACT.Square,
                                       scale=D ** -0.5, accum_out=var[:, g, j:j + 1]).then_inc(sem("ln_var"), 1)
                for g in range(G):
                    use_full(act, g, f"{name}_x")
                    act.activation(X(x)[:, tok(g)], bank[g][:, 0:GT], ACT.Identity, bias=col(f"{name}_lb"),
                                   scale=col(f"{name}_lg")).then_inc(sem("ln_done"), 1)

            def gelu(name):
                for hh in range(2):
                    for g in range(G):
                        use_full(act, g, f"{name}_h{hh}")
                        for c in range(2):
                            cc = 2 * hh + c
                            act.activation(hid[:, cc, tok(g)], bank[g][:, c * GT:(c + 1) * GT], ACT.Gelu,
                                           bias=col(f"{name}_b1_{cc}"), scale=1.0).then_inc(sem(f"{name}_gelu{hh}"), 1)

            act.wait_ge(sem("v_loaded"), 16)
            parts("sa", "k")
            parts("sa", "q")
            value_half("sa")
            parts("ca", "k")
            act.wait_ge(sem("cn_loaded"), 16)
            for n in range(B // 2):
                act.activation(att[:, n // NJ, n % NJ, :], cn[:, n, :], ACT.Square, scale=D ** -0.5,
                               accum_out=cms[:, n:n + 1]).then_inc(sem("cms_ready"), 1)
            attention("sa")
            projected("sa")
            normalised("sa", "x1")
            parts("l1", "k")
            value_half("l1")
            parts("ca", "q")
            attention("ca")
            projected("ca")
            normalised("ca", "x2")
            parts("l2", "k")
            value_half("l2")
            for g in range(G):
                use_full(act, g, "l3_n")
                act.activation(ctxT[:, tok(g)], bank[g][:, 0:GT], ACT.Copy).then_inc(sem("ctx_normed_T"), 1)
            act.wait_ge(sem("k_low"), attn("l2"))
            gelu("f")
            normalised("f", "x3")
            parts("l1", "q")
            attention("l1")
            projected("l1")
            normalised("l1", "x4")
            parts("l3", "k")
            value_half("l3")
            parts("l2", "q")
            attention("l2")
            projected("l2")
            normalised("l2", "x5")
            act.wait_ge(sem("k_low"), attn("l3"))
            gelu("g")
            for g in range(G):
                act.wait_ge(sem("x6"), g + 1)
                act.activation(k_full[:, g, :], X("x6")[:, tok(g)], ACT.Square, scale=D ** -0.5
                               ).then_inc(sem("l3_sq"), 1)
            parts("l3", "q")
            for g in range(G):
                for i in range(GB):
                    u = t_unit("l3", g, i)
                    n = u - t_unit("l3", 0)
                    act.wait_ge(sem("t_full"), u + 1)
                    if n >= 2:
                        act.wait_ge(sem("p_ready"), u - 1)
                    act.activation(relu[:, n % 2, :], t_bank[u % 2][:, :], ACT.Relu).then_inc(sem("l3_relu"), 1)
            projected("l3")
            for g in range(G):
                use_full(act, g, "l3_z")
                act.activation(fin[:, g, :], bank[g][:, 0:GT], ACT.Copy).then_inc(sem("fin_ready"), 1)

        @block.vector
        def _(dve):
            def split(name, side):
                whole, rest = (q_full, q_rest) if side == "q" else (k_full, k_rest)
                for g in range(G):
                    dve.wait_ge(sem(f"{side}_first"), attn(name, g))
                    part, x = paired(name, side, 0, g, whole[:, g, :])
                    _, o = paired(name, side, 0, g, rest[:, g, :])
                    dve.tensor_tensor(o, x, part, ALU.subtract).then_inc(sem(f"{side}_rest"), 1)
                for g in range(G):
                    dve.wait_ge(sem(f"{side}_rest"), attn(name, g))
                    dve.tensor_copy(*paired(name, side, 1, g, rest[:, g, :])).then_inc(sem(f"{side}_mid"), 1)
                for g in range(G):
                    dve.wait_ge(sem(f"{side}_mid"), attn(name, g))
                    part, x = paired(name, side, 1, g, rest[:, g, :])
                    dve.tensor_tensor(paired(name, side, 2, g, rest[:, g, :])[0], x, part, ALU.subtract
                                      ).then_inc(sem(f"{side}_low"), 1)

            def value_half(name):
                for g in range(G):
                    use_full(dve, g, f"{name}_v")
                    if g == 0:
                        dve.wait_ge(sem("v_base"), V_BASE[name])
                        if name in ("l1", "l3"):
                            dve.wait_ge(sem("p_used"), last_t({"l1": "sa", "l3": "l1"}[name], G - 1) + 1)
                    src = bank[g][0:64, 0:256].rearrange("p (c d) -> p c d", d=DH)
                    dst = v_ext[VALUES[name]][0:64, g * GB:(g + 1) * GB, :, :, :].rearrange("p b s e n -> p (b s) e n")
                    dve.tensor_copy(dst[:, :, 0, 0:DH], src).then_inc(sem("v_even"), 1)

            def maxima(name, g, i):
                u = s_unit(name, g, i)
                dve.wait_ge(sem("s_full"), u + 1)
                if name == "ca":
                    o, w = m_col[:, g, :, :, :].rearrange("p j s e -> p (j s e)"), K16
                else:
                    o, w = m_col[:, g, i // 2, 4 * (i % 2):4 * (i % 2) + 4, :].rearrange("p s e -> p (s e)"), T
                dve.tensor_reduce(o, s_bank[u % 2][:, :].rearrange("p (c k) -> p c k", k=w), AX.X, ALU.max
                                  ).then_inc(sem("m_reduced"), 1)

            def max_parts(name, g):
                dve.wait_ge(sem("m_reduced"), s_unit(name, g, S_UNITS[name] - 1) + 1)
                src = m_col[:, g, :, :, :].rearrange("p j s e -> p j e s")
                dve.tensor_scalar(m_part[:, g, :, 0, :, :], src, -1.0, None, ALU.mult).then_inc(sem("m_hi"), 1)
                dve.wait_ge(sem("m_hi"), attn(name, g))
                dve.tensor_tensor(m_part[:, g, :, 1, :, :], src, m_part[:, g, :, 0, :, :], ALU.add
                                  ).then_inc(sem("m_lo"), 1)

            def divide(name, g):
                src = bank[g][:, 0:NJ * 144].rearrange("p (h n) -> p h n", n=DH + 1)
                rd = rden[:, g, :, :].rearrange("p j h -> p (j h)")
                dve.wait_ge(sem("p_used"), last_t(name, g) + 1)
                den = src[:, :, DH]
                if name == "l3":
                    dve.tensor_tensor(rden[:, g, :, :], den.rearrange("p (j h) -> p j h", j=NJ),
                                      floor[:, g, :].unsqueeze(2).to_broadcast([128, NJ, H]),
                                      ALU.max).then_inc(sem("l3_den"), 1)
                    dve.wait_ge(sem("l3_den"), g + 1)
                    den = rd
                dve.reciprocal(rd, den).then_inc(sem("rden_ready"), 1)
                dve.wait_ge(sem("rden_ready"), attn(name, g))
                dve.tensor_tensor(att[:, g, :, :].rearrange("p j (h n) -> p (j h) n", n=DH), src[:, :, 0:DH],
                                  rd.unsqueeze(2).to_broadcast([128, NJ * H, DH]), ALU.mult
                                  ).then_inc(sem("att_ready"), 1)

            def attention(name):
                n = S_UNITS[name]
                for step in range(G + LAG + 1):
                    for i in range(n):
                        if step < G:
                            maxima(name, step, i)
                        if i == 0 and step > LAG:
                            divide(name, step - LAG - 1)
                    if step < G:
                        max_parts(name, step)

            def scaled(name):
                for g in range(G):
                    dve.wait_ge(sem("ln_rstd"), norm(name, g))
                    dve.tensor_tensor(y_tok[:, g, :, :], bank[g][:, 0:GT].rearrange("p (j d) -> p j d", j=NJ),
                                      rstd[:, g, :].unsqueeze(2).to_broadcast([128, NJ, 128]), ALU.mult
                                      ).then_inc(sem("ln_scaled"), 1)

            dve.memset(k_stack[0][:, 0:4, :, :].bitcast(F), 0.0).then_inc(sem("k_zero0"), 1)
            dve.memset(ones_row[:], 1.0).then_inc(sem("const_ready"), 1)
            dve.memset(ones_col[:], 1.0).then_inc(sem("ones_col_ready"), 1)
            dve.memset(q_ones[:], 1.0).then_inc(sem("const_ready"), 1)
            dve.wait_ge(sem("cst_loaded"), 16)
            dve.tensor_copy(identb[:], cst[:, 0:128]).then_inc(sem("const_ready"), 1)
            dve.tensor_copy(two_i[:], cst[0:64, 128:256]).then_inc(sem("const_ready"), 1)
            dve.tensor_copy(causal[:], cst[0:64, 256:384].rearrange("p (a k) -> p a k", a=2)
                            ).then_inc(sem("const_ready"), 1)
            dve.tensor_copy(k_ones, cst[0:4, 384:386].unsqueeze(2).to_broadcast([4, 2, TOK])
                            ).then_inc(sem("const_ready"), 1)
            use_full(dve, 0, "mats")
            dve.tensor_copy(WC[:, 0:4, :].rearrange("p a n -> p (a n)"), bank[0][:, :]).then_inc(sem("mats_used0"), 1)
            use_full(dve, 1, "mats")
            dve.tensor_copy(WC[:, 4:8, :].rearrange("p a n -> p (a n)"), bank[1][:, :]).then_inc(sem("mats_used1"), 1)
            use_full(dve, 2, "mats")
            dve.tensor_copy(WC[:, 8, :], bank[2][:, 0:128]).then_inc(sem("mats_used2"), 1)
            dve.tensor_copy(rows[:, 4, :], bank[2][0:1, 128:256]).then_inc(sem("mats_used2"), 1)
            use_full(dve, 3, "mats")
            dve.tensor_copy(rows[:, 0:4, :].rearrange("p a n -> p (a n)"), bank[3][0:1, :]
                            ).then_inc(sem("mats_used3"), 1)

            split("sa", "k")
            split("sa", "q")
            value_half("sa")
            for g in range(G):
                use_full(dve, g, "ca_v")
                vc = v_ext[1][:, g * GB:(g + 1) * GB, :, :, :].rearrange("p b s e n -> p (b s e) n")
                vc = vc.rearrange("p (c a) n -> p c a n", a=8)
                dve.tensor_tensor(vc[:, :, :, 0:DH], bank[g][:, :].rearrange("p (c a n) -> p c a n", a=8, n=DH),
                                  e_mask.unsqueeze(1).unsqueeze(3).to_broadcast([128, 2 * GB, 8, DH]), ALU.mult
                                  ).then_inc(sem("v_even"), 1)
            dve.wait_ge(sem("km_loaded"), 16)
            dve.tensor_scalar(km[:].rearrange("p (k b) -> p b k", b=B), km_u8[:].rearrange("p (b k) -> p b k", b=B), -1.0, KEY_BIG, ALU.add, ALU.mult).then_inc(sem("km_ready"), 1)
            dve.wait_ge(sem("idx_loaded"), 16)
            dve.tensor_scalar(dist, idx, cst[0:64, 386:387], None, ALU.subtract).then_inc(sem("dist_ready"), 1)
            dve.wait_ge(sem("dist_ready"), 1)
            dve.tensor_tensor(dist, dist, dist, ALU.mult).then_inc(sem("dist_ready"), 1)
            dve.wait_ge(sem("dist_ready"), 2)
            dve.tensor_scalar(band[:], dist, 1.0, -BIG, ALU.is_gt, ALU.mult).then_inc(sem("band_ready"), 1)
            dve.wait_ge(sem("band_ready"), 1)
            dve.wait_ge(sem("v_loaded"), 16)
            for n, c in (("l3_q", "l3_gq"), ("l3_k", "l3_gk"), ("l3_v", "l3_gk")):
                dve.tensor_scalar(mat(n), mat(n), col(c), None, ALU.mult).then_inc(sem("gamma_folded"), 1)
            dve.wait_ge(sem("crs_ready"), 1)
            dve.tensor_tensor(cn, cn, crs[:].unsqueeze(2).to_broadcast([128, B // 2, 128]), ALU.mult
                              ).then_inc(sem("cn_scaled"), 1)

            attention("sa")
            scaled("sa")
            value_half("l1")
            split("ca", "q")
            attention("ca")
            scaled("ca")
            value_half("l2")
            scaled("f")
            split("l1", "q")
            attention("l1")
            scaled("l1")
            value_half("l3")
            split("l2", "q")
            attention("l2")
            scaled("l2")
            for g in range(G):
                use_full(dve, g, "g_y")
                dve.scalar_tensor_tensor(X("x6")[:, tok(g)], bank[g][:, 0:GT], col("g_b2"), X("x5")[:, tok(g)],
                                         ALU.add, ALU.add).then_inc(sem("x6"), 1)
            split("l3", "q")
            for g in range(G):
                use_full(dve, g, "l3_ms")
                dve.tensor_scalar(floor[:, g, :], bank[g][:, 0:NJ], EPS_DEN / SCALE ** 2,
                                  EPS_RMS * EPS_DEN / SCALE ** 2, ALU.mult, ALU.add).then_inc(sem("l3_floor"), 1)
            dve.wait_ge(sem("l3_floor"), G)
            for g in range(G):
                for i in range(GB):
                    u = t_unit("l3", g, i)
                    n = u - t_unit("l3", 0)
                    dve.wait_ge(sem("l3_relu"), n + 1)
                    dve.wait_ge(sem("p_used"), u - P_SLOTS + 1)
                    dve.tensor_tensor(probs[:, u % P_SLOTS, :], relu[:, n % 2, :], relu[:, n % 2, :], ALU.mult
                                      ).then_inc(sem("p_ready"), 1)
                    if i == 1 and g >= 1:
                        divide("l3", g - 1)
            divide("l3", G - 1)

        @block.gpsimd
        def _(pool):
            def v_base(i, ca):
                n = B * SP_
                ve = v_ext[i][:, :, :, :, :].rearrange("p b s e n -> p (b s) e n")
                if ca:
                    pool.wait_ge(sem("cst_loaded"), 16)
                    flat = v_ext[i][:, :, :, :, :].rearrange("p b s e n -> p (b s e) n")
                    pool.tensor_copy(flat[:, :, DH].rearrange("p (c a) -> p c a", a=8),
                                     e_mask.unsqueeze(1).to_broadcast([128, 2 * B, 8])).then_inc(sem("v_base"), 1)
                    return
                pool.memset(v_ext[i][:], 0.0).then_inc(sem("v_zero"), 1)
                pool.wait_ge(sem("v_zero"), i + 1)
                pool.wait_ge(sem("cst_loaded"), 16)
                pool.tensor_copy(ve[:, :, :, DH], cst[:, 387:389].unsqueeze(1).to_broadcast([128, n, 2])
                                 ).then_inc(sem("v_base"), 1)

            def split_k(name):
                for g in range(G):
                    pool.wait_ge(sem("k_first"), attn(name, g))
                    part, x = paired(name, "k", 0, g, k_full[:, g, :])
                    pool.tensor_tensor(paired(name, "k", 0, g, k_rest[:, g, :])[1], x, part, ALU.subtract
                                       ).then_inc(sem("k_rest"), 1)
                for g in range(G):
                    pool.wait_ge(sem("k_rest"), attn(name, g))
                    pool.tensor_copy(*paired(name, "k", 1, g, k_rest[:, g, :])).then_inc(sem("k_mid"), 1)
                for g in range(G):
                    pool.wait_ge(sem("k_mid"), attn(name, g))
                    part, x = paired(name, "k", 1, g, k_rest[:, g, :])
                    pool.tensor_tensor(paired(name, "k", 2, g, k_rest[:, g, :])[0], x, part, ALU.subtract
                                       ).then_inc(sem("k_low"), 1)

            def inverse_root(name):
                for g in range(G):
                    pool.wait_ge(sem("ln_var"), NJ * norm(name, g))
                    pool.tensor_scalar(vare[:, g, :], var[:, g, :], EPS, None, ALU.add).then_inc(sem("ln_var_eps"), 1)
                    pool.wait_ge(sem("ln_var_eps"), norm(name, g))
                    pool.tensor_tensor(rstd[:, g, :], vare[:, g, :], half[:, 0:NJ], ALU.pow
                                       ).then_inc(sem("ln_rstd"), 1)

            pool.memset(k_stack[0][:, 4:8, :, :].bitcast(F), 0.0).then_inc(sem("k_zero0"), 1)
            pool.memset(half[:], -0.5).then_inc(sem("half_ready"), 1)
            v_base(0, False)
            v_base(1, True)
            pool.wait_ge(sem("ctx_loaded"), 16)
            for pi in range(2):
                for e in range(2):
                    pool.tensor_copy(ctx_rep[:, :, pi, :, e, :],
                                     ctxT[:].rearrange("p (b k r) -> p b k r", b=B, r=STRIDE)[:, :, :, 2 * pi + e]
                                     .unsqueeze(2).to_broadcast([128, B, 4, K16])).then_inc(sem("ctx_rep_ready"), 1)
            pool.memset(kc_stack[:].bitcast(F), 0.0).then_inc(sem("kc_zero"), 1)
            split_k("ca")
            pool.wait_ge(sem("v_even"), attn("ca"))
            pool.memset(k_stack[1][:].bitcast(F), 0.0).then_inc(sem("k_zero1"), 1)
            pool.wait_ge(sem("half_ready"), 1)
            pool.wait_ge(sem("cms_ready"), B // 2)
            pool.tensor_scalar(cmse[:], cms[:], EPS_RMS, None, ALU.add).then_inc(sem("cmse_ready"), 1)
            pool.wait_ge(sem("cmse_ready"), 1)
            pool.tensor_tensor(crs[:], cmse[:], half[:], ALU.pow).then_inc(sem("crs_ready"), 1)
            inverse_root("sa")
            split_k("l1")
            inverse_root("ca")
            pool.wait_ge(sem("p_used"), last_t("ca", G - 1) + 1)
            v_base(1, False)
            split_k("l2")
            inverse_root("f")
            inverse_root("l1")
            split_k("l3")
            inverse_root("l2")


def constants():
    import numpy as np
    c = np.zeros((128, CST), np.float32)
    c[:, 0:128] = np.eye(128)
    c[0:64, 128:192] = np.eye(64)
    c[0:64, 192:256] = np.eye(64)
    later = np.triu(np.ones((64, 64)), 1) * -BIG
    c[0:64, 256:320] = later
    c[0:64, 320:384] = later.T
    for hl in range(2):
        for e in range(2):
            c[2 * hl + e, 384 + e] = 1 - 2 * hl
    c[:, 386] = np.arange(128)
    c[0:64, 387] = c[64:128, 388] = 1
    for p in range(4):
        for e in range(2):
            c[32 * p + 16 * e:32 * p + 16 * e + 16, CST - 8 + 2 * p + e] = 1
    return c


def kernel(**inp):
    import numpy as np
    import concourse.bacc as bacc
    from concourse.bass_utils import run_bass_kernel_spmd

    def arr(n):
        return np.asarray(inp[n])

    def by_feature(w):
        return w.reshape(w.shape[:-1] + (SP_, 2, DH)).swapaxes(-3, -2).swapaxes(-2, -1).reshape(w.shape)

    L0, L1, L2, L3 = "L0_xattn_", "L1_xattn_", "L2_xattn_", "L3_xattn_"
    sa_w, sa_b = arr(L0 + "sa_in_w"), arr(L0 + "sa_in_b")
    upd, tokw = arr(L1 + "W_upd"), arr(L1 + "W_token")
    f1, f2 = arr(L0 + "ffn_w1").T, arr(L0 + "ffn_w2")
    g1, g2 = arr(L2 + "W1").T, arr(L2 + "W2").T
    m = {
        "ident": np.eye(D, dtype=np.float32),
        "center": np.eye(D, dtype=np.float32) - np.float32(1 / D),
        "sa_q": by_feature(sa_w[0:D].T), "sa_k": by_feature(sa_w[D:2 * D].T), "sa_v": sa_w[2 * D:].T,
        "ca_q": by_feature(arr(L0 + "ca_q_w").T), "ca_k": by_feature(arr(L0 + "ca_k_w").T),
        "ca_v": arr(L0 + "ca_v_w").T,
        "l1_q": by_feature(arr(L1 + "W_state")), "l1_k": by_feature(tokw), "l1_v": tokw,
        "sa_o": arr(L0 + "sa_out_w"), "ca_o": arr(L0 + "ca_o_w"),
        "l1_updT": upd[D:].T, "l1_updsT": upd[:D].T, "l1_outT": arr(L1 + "W_out").T,
        "l2_q": by_feature(arr(L2 + "Wq").T), "l2_k": by_feature(arr(L2 + "Wk").T), "l2_v": arr(L2 + "Wv").T,
        "l3_q": by_feature(arr(L3 + "Wq").T), "l3_k": by_feature(arr(L3 + "Wk").T), "l3_v": arr(L3 + "Wv").T,
        "l3_o": arr(L3 + "Wo").T,
    }
    for c in range(F_CHUNKS):
        s = slice(c * D, (c + 1) * D)
        m[f"f_w1_{c}"], m[f"f_w2_{c}"] = f1[:, s], f2[:, s]
        m[f"g_w1_{c}"], m[f"g_w2_{c}"] = g1[:, s], g2[s, :]
    v = {
        "sa_qb": by_feature(sa_b[0:D]), "sa_kb": by_feature(sa_b[D:2 * D]), "sa_vb": sa_b[2 * D:],
        "ca_qb": by_feature(arr(L0 + "ca_q_b")), "ca_kb": by_feature(arr(L0 + "ca_k_b")),
        "l1_qb": by_feature(arr(L1 + "b_state")), "l1_kb": by_feature(arr(L1 + "b_token")),
        "l2_qb": by_feature(arr(L2 + "bq")), "l2_kb": by_feature(arr(L2 + "bk")),
        "sa_ob": arr(L0 + "sa_out_b"), "ca_vb": arr(L0 + "ca_v_b"), "ca_ob": arr(L0 + "ca_o_b"),
        "f_b2": arr(L0 + "ffn_b2"), "l1_tb": arr(L1 + "b_token"), "l1_ob": arr(L1 + "b_out"),
        "l1_ub": arr(L1 + "b_upd"), "l2_vb": arr(L2 + "bv"), "g_b2": arr(L2 + "b2"),
        "sa_lg": arr(L0 + "ln1_g"), "sa_lb": arr(L0 + "ln1_b"), "ca_lg": arr(L0 + "ln2_g"), "ca_lb": arr(L0 + "ln2_b"),
        "f_lg": arr(L0 + "ln3_g"), "f_lb": arr(L0 + "ln3_b"), "l1_lg": arr(L1 + "ln_gamma"),
        "l1_lb": arr(L1 + "ln_beta"), "l2_lg": arr(L2 + "ln_g"), "l2_lb": arr(L2 + "ln_b"),
        "l3_gq": arr(L3 + "gamma_q"), "l3_gk": arr(L3 + "gamma_kv"),
    }
    for c in range(F_CHUNKS):
        v[f"f_b1_{c}"] = arr(L0 + "ffn_b1")[c * D:(c + 1) * D]
        v[f"g_b1_{c}"] = arr(L2 + "b1")[c * D:(c + 1) * D]
    arrays = {
        "xT": arr("x").reshape(TOK, D).T,
        "ctxT": arr("ctx_1024").reshape(TOK, D).T,
        "ctx": arr("ctx_1024").reshape(TOK, D),
        "idx": arr("itok_BxS_0_255").reshape(1, TOK),
        "key_mask": arr("mask_BxS2_bf1").reshape(1, TOK).view(np.uint8),
        "mats": np.stack([m[n] for n in MATS], axis=1),
        "cols": np.stack([v[n] for n in COLS], axis=1),
        "consts": constants(),
    }
    arrays = {n: np.ascontiguousarray(x) for n, x in arrays.items()}
    nc = bacc.Bacc("TRN2", target_bir_lowering=False, num_devices=1)
    a = {n: nc.dram_tensor(f"in_{n}", x.shape, mybir.dt.from_np(x.dtype), kind="ExternalInput").ap()
         for n, x in arrays.items()}
    out = nc.dram_tensor("out", (TOK, D), mybir.dt.float32, kind="ExternalOutput").ap()
    build(nc, a, out)
    r = run_bass_kernel_spmd(nc, [{f"in_{n}": x for n, x in arrays.items()}], core_ids=[0])
    return r.results[0]["out"].reshape(B, T, D)
```

```python
import concourse.bass as bass
from concourse import mybir
from contextlib import ExitStack

B, T, D, H, DH = 16, 64, 128, 16, 8
TOK = B * T
G = 4
GB = B // G
GT = GB * T
NJ = GT // 128
SP_ = H // 2
TERMS = 6
Q_PART = (0, 0, 0, 1, 1, 2)
K_PART = (0, 1, 2, 0, 1, 0)
R_TERMS = TERMS * 16
R_MASK = R_TERMS + 2
R_ALL = R_MASK + 4
STRIDE = 4
K16 = T // STRIDE
F_CHUNKS = 4
EPS = 1e-5
EPS_RMS = 1.1920929e-07
EPS_DEN = 1e-6
SCALE = DH ** -0.5
BIG = 1e30
KEY_BIG = 3e38
CST = 397

MATS = ["ident", "center", "sa_q", "sa_k", "sa_v",
        "ca_q", "ca_k", "ca_v", "l1_q", "l1_k", "l1_v", "sa_o", "ca_o", "l1_updT", "l1_updsT", "l1_outT",
        "l2_q", "l2_k", "l2_v", "l3_q", "l3_k", "l3_v", "l3_o",
        "f_w1_0", "f_w1_1", "f_w1_2", "f_w1_3", "f_w2_0", "f_w2_1", "f_w2_2", "f_w2_3",
        "g_w1_0", "g_w1_1", "g_w1_2", "g_w1_3", "g_w2_0", "g_w2_1", "g_w2_2", "g_w2_3"]
FIRST_MATS = 5
NEXT_MATS = 23
COLS = ["sa_qb", "sa_kb", "ca_qb", "ca_kb", "l1_qb", "l1_kb", "l2_qb", "l2_kb",
        "sa_vb", "sa_ob", "ca_vb", "ca_ob", "f_b2", "l1_tb", "l1_ob", "l1_ub", "l2_vb", "g_b2",
        "sa_lg", "sa_lb", "ca_lg", "ca_lb", "f_lg", "f_lb", "l1_lg", "l1_lb", "l2_lg", "l2_lb",
        "l3_gq", "l3_gk", "f_b1_0", "f_b1_1", "f_b1_2", "f_b1_3", "g_b1_0", "g_b1_1", "g_b1_2", "g_b1_3"]
ATT = ["sa", "ca", "l1", "l2", "l3"]
S_UNITS = {"sa": NJ * 2, "ca": 1, "l1": NJ * 2, "l2": NJ * 2, "l3": 0}
T_UNITS = {"sa": GB, "ca": 1, "l1": GB, "l2": GB, "l3": GB}
P_SLOTS = 4
STACK = {"sa": 0, "l1": 1, "l2": 0, "l3": 1}
V_BASE = {"sa": 0, "ca": 1, "l1": 0, "l2": 2, "l3": 0}
VALUES = {"sa": 0, "ca": 1, "l1": 0, "l2": 1, "l3": 0}
V_BEFORE = {"l1": "sa", "l3": "l1"}
WC_OF = {"sa": 0, "ca": 1, "l1_upd": 2, "l1_res": 3, "f": 4, "l1": 8}
ROW_OF = {"sa": 0, "ca": 1, "f": 2, "l1": 3, "l2": 4}
X_OF = {"x0": 0, "x1": 1, "x2": 0, "x3": 1, "x4": 0, "x5": 1, "x6": 0}
X_FROM = {"x1": "sa", "x2": "ca", "x3": "f", "x4": "l1", "x5": "l2"}
X_IN = {"sa": "x0", "ca": "x1", "f": "x2", "l1": "x3", "l2": "x4", "g": "x5", "l3": "x6"}
X_OUT = {"sa": "x1", "ca": "x2", "f": "x3", "l1": "x4", "l2": "x5"}

OWN = {"q": ["q_parts"], "m": ["m_row"], "av": ["divide"], "flip": ["attT"], "z": ["scale"], "flip_x": ["ln"],
       "h": ["gelu"], "y": ["x6"], "ms": ["floor"], "out": ["fin"]}
TURNS = {"s": ["max"], "k": ["k_parts"], "v": ["v_even", "v_odd"], "ctx_rows": ["ctx_normed"],
         "weights": ["weights_kept"]}


def timetable():
    jobs, tail = {}, {}

    def add(engine, cost, step, name="", g=0, i=0, after=()):
        jobs[step, name, g, i] = (engine, cost, [k if len(k) == 4 else k + (0,) * (4 - len(k)) for k in after])
        return (step, name, g, i)

    groups = range(G)
    for n, (name, t) in enumerate((("x", 3), ("w1", 4), ("cols", 5), ("consts", 6), ("ctx", 8), ("w2", 12), ("w3", 16),
                                   ("rest", 18))):
        add(f"load{n}", t, "load", name)

    def load(name):
        return ("load", name, 0, 0)

    w0 = add("pe", 2.6, "weights", i=0, after=[load("w2")])
    w0k = add("dve", .6, "weights_kept", i=0, after=[w0])
    w1 = add("pe", 2.0, "weights", i=1, after=[load("w3")])
    add("dve", .6, "weights_kept", i=1, after=[w1])
    w2 = add("pe", .8, "weights", i=2, after=[w0k, load("w3")])
    w2k = add("dve", .3, "weights_kept", i=2, after=[w2])
    w3 = add("pe", 1.8, "weights", i=3, after=[w2k])
    add("dve", .6, "weights_kept", i=3, after=[w3])
    z0 = [add("dve", 4.4, "k_zero_first", i=0), add("pool", 4.4, "k_zero_first", i=1)]
    constants_ready = add("dve", 1.6, "constants", after=[load("consts")])
    ck = add("dve", .5, "ca_k_split", after=[load("w2")])
    add("pool", 2.4, "v_base", i=0, after=[load("consts")])
    add("pool", .6, "v_base", i=1, after=[load("consts")])
    rep = add("pool", 5., "ctx_rep", after=[load("ctx"), ("v_base", "", 0, 1)])
    kcz = add("pool", 3., "kc_zero", after=[rep])
    add("sp", 1.3, "kc_rows", after=[kcz, constants_ready])
    add("sp", 1.3, "k_rows", i=0, after=[constants_ready] + z0)
    zs = []
    for i in range(4):
        zs.append(add("pool", 2.2, "k_zero", i=i, after=[("v_even", "ca", g) for g in groups] + zs[-1:]))
    add("sp", .7, "k_rows", i=1, after=[zs[-1]])
    add("dve", .9, "key_mask", after=[load("rest")])
    add("sp", 1.3, "km_stack", after=[("key_mask", ""), zs[-1]])
    band = add("dve", 3.3, "band", after=[load("rest")])
    add("dve", 1., "gammas", after=[load("w3")])
    cms = add("act", 2., "ctx_ms", after=[load("rest")])
    crs = add("pool", .4, "ctx_rs", after=[cms])
    ctx_scaled = add("dve", 1.2, "ctx_scale", after=[crs])
    add("pool", 2.8, "v_base", i=2, after=[("av", "ca", g) for g in groups])

    def keys_of(name, k_free, v_free):
        prev = {"l1": "sa", "l2": "l1", "l3": "l2"}.get(name)
        lows = []
        low = "k0_low" if name == "sa" else "k_low"
        if name == "ca":
            k = add("pe", .45, "k", name, after=[load("ctx"), ck, ("k0_low", "sa", 0)])
            for e, cost, step in (("act", .75, "k_parts"), ("pool", .4, "k_rest"), ("pool", .4, "k_mid"),
                                  ("pool", .4, "k_low")):
                k = add(e, cost, step, name, after=[k])
            lows = [k]
        for g in groups if name != "ca" else ():
            after = [load("w1"), load("x")] if name == "sa" else [load("w2"), load("ctx")]
            if name != "sa":
                after += [("k_stack", prev, 0, t) for t in range(TERMS)]
                after += [("k_low", "ca", 0) if name == "l1" else ("k_low", prev, g)]
            if name == "l3":
                after += [("ctx_normed", "", g), ("z", "f", g), ("gammas", "")]
            k = add("pe", .45, "k", name, g, after=after)
            k = add("act", .75, "k_parts", name, g, after=[k])
            if name == "sa":
                k = add("dve", .35, "k0_rest", name, g, after=[k] + z0[:1])
                k = add("dve", .35, "k0_mid", name, g, after=[k])
                lows.append(add("dve", .35, "k0_low", name, g, after=[k]))
                continue
            k = add("pool", .6, "k_rest", name, g, after=[k])
            k = add("pool", .6, "k_mid", name, g, after=[k])
            lows.append(add("pool", .6, "k_low", name, g, after=[k]))
        for t in range(TERMS):
            add("sp", 1.3, "k_stack", name, 0, t, after=lows + k_free)
        for g in groups:
            after = [load("w1"), load("x")] if name == "sa" else [load("w2"), load("ctx")]
            if name == "l3":
                after += [("ctx_normed", "", g)]
            if name == "ca":
                after += [rep]
            v = add("pe", .9, "v", name, g, after=after + v_free + [("v_base", "", 0, V_BASE[name])])
            add("dve", .35, "v_even", name, g, after=[v])
            if name != "ca":
                add("act", .35, "v_odd", name, g, after=[v])

    keys_of("sa", z0, [])
    keys_of("ca", [kcz], [])
    keys_of("l1", [zs[-1]], [("av", "sa", g, GB - 1) for g in groups])
    keys_of("l2", [("t", "sa", g, GB - 1) for g in groups], [("av", "ca", g) for g in groups])
    for g in groups:
        k = add("pe", .45, "ctx_rows", "", g, after=[ctx_scaled, ("v", "l2", g), ("k", "l2", g)])
        add("act", .3, "ctx_normed", "", g, after=[k])
    keys_of("l3", [("t", "l1", g, GB - 1) for g in groups], [("av", "l1", g, GB - 1) for g in groups])

    for g in groups:
        k = load("x")

        def attention(name, k):
            k = add("pe", .45, "q", name, g, after=[k, load("w2" if name != "sa" else "w1")])
            q_parts = k = add("act", .75, "q_parts", name, g, after=[k])
            k = add("dve", .35, "q_rest", name, g, after=[k])
            k = add("dve", .35, "q_mid", name, g, after=[k])
            k = add("dve", .35, "q_low", name, g, after=[k])
            k = add("sp", 4., "q_stack", name, g, after=[k])
            stacked = [k] + [("k_stack", name, 0, t) for t in range(TERMS)]
            k_rows = {"sa": ("k_rows", "", 0, 0), "l1": ("k_rows", "", 0, 1), "ca": ("kc_rows", "")}
            if name == "l1":
                stacked.append(("km_stack", ""))
            if name == "l3":
                stacked.append(band)
                sq = add("act", .35, "x_sq", name, g, after=[("x6", "g", g)])
                ms = add("pe", .2, "ms", name, g, after=[sq, q_parts])
                floored = [add("dve", .2, "floor", name, g, after=[ms])]
            else:
                floored, maxes = [], []
                for i in range(S_UNITS[name]):
                    s = add("pe", 1.7 if name == "ca" else .7, "s", name, g, i, after=stacked)
                    maxes.append(add("dve", .65, "max", name, g, i, after=[s]))
                k = add("dve", .3, "max_parts", name, g, after=maxes)
                k = add("pe", .2, "m", name, g, after=[k])
                k = add("act", .2, "m_row", name, g, after=[k])
                stacked = [add("sp", .7, "m_stack", name, g, after=[k])] + ([k_rows[name]] if name in k_rows else [])
            avs = []
            for i in range(T_UNITS[name]):
                t = add("pe", {"ca": 1.7, "l2": .7, "l3": .7}.get(name, .45), "t", name, g, i, after=stacked)
                p = add("act", .5, "exp", name, g, i, after=[t] + ([band, cms] if name == "sa" else []))
                if name == "l3":
                    p = add("dve", .6, "square", name, g, i, after=[p])
                avs.append(add("pe", .9, "av", name, g, i, after=[p, ("v_even", name, g)]
                               + ([("v_odd", name, g)] if name != "ca" else []) + (avs[-1:] or floored)))
            k = add("dve", .6, "divide", name, g, after=avs)
            k = add("pe", .45, "flip", name, g, after=[k])
            return add("act", .3, "attT", name, g, after=[k])

        def norm(name, k):
            k = add("pe", 2.6 if name == "f" else 1.3, "z", name, g, after=[k, ("weights_kept", "", 0, 3)])
            k = add("act", .4, "var", name, g, after=[k])
            k = add("pool", .4, "rstd", name, g, after=[k])
            k = add("dve", .35, "scale", name, g, after=[k])
            k = add("pe", .45, "flip_x", name, g, after=[k])
            return add("act", .5, "ln", name, g, after=[k] + ([("k", "ca", 0)] if name == "sa" else []))

        def hidden(name, k):
            for i in range(2):
                h = add("pe", .9, "h", name, g, i, after=[k])
                k = add("act", .8, "gelu", name, g, i, after=[h] + (
                    [("k_low", "l2", gg) for gg in groups] + [("ctx_normed", "", gg) for gg in groups]
                    + [("kc_rows", ""), ("k_rows", "", 0, 1)] if name == "f" else [("k_low", "l3", g)]))
            return k

        k = norm("sa", attention("sa", k))
        k = norm("ca", attention("ca", k))
        k = norm("f", hidden("f", k))
        k = norm("l1", attention("l1", k))
        k = norm("l2", attention("l2", k))
        k = hidden("g", k)
        k = add("pe", 1.8, "y", "g", g, after=[k])
        k = add("dve", .4, "x6", "g", g, after=[k])
        k = attention("l3", k)
        k = add("pe", .9, "out", "", g, after=[k])
        k = add("act", .3, "fin", "", g, after=[k])
        add("sp", .7, "store", "", g, after=[k])

    users = {}
    for k, (_, _, after) in jobs.items():
        for x in after:
            users.setdefault(x, []).append(k)

    def way(k):
        if k not in tail:
            tail[k] = jobs[k][1] + HOP + max([way(u) for u in users.get(k, [])], default=0)
        return tail[k]

    end, free, order, turns, ts, table = {}, {}, [], [], [], "exp"
    waiting = set(jobs)
    ready = {k for k in waiting if not jobs[k][2]}
    while waiting:
        best = None
        for k in ready:
            step, name, g, i = k
            engine, cost, after = jobs[k]
            need = list(after)
            if step in TURNS and len(turns) >= 2:
                need += [(r,) + turns[-2][1:] for r in TURNS[turns[-2][0]] if (r,) + turns[-2][1:] in jobs]
            if step == "t" and len(ts) >= 2:
                need.append(("exp",) + ts[-2][1:])
            if step == ("square" if name == "l3" else "exp"):
                u = ts.index(("t",) + k[1:])
                if u >= P_SLOTS:
                    need.append(("av",) + ts[u - P_SLOTS][1:])
            if step == "exp":
                same = [x for x in ts if x[1] == "l3"]
                u = same.index(("t",) + k[1:]) if name == "l3" else 0
                if u >= 2:
                    need.append(("square",) + same[u - 2][1:])
            if any(x not in end for x in need):
                continue
            start = max([free.get(engine, 0)] + [end[x] for x in need])
            kind = {"exp": "relu" if name == "l3" else "exp", "gelu": "gelu"}.get(step)
            if kind in ("exp", "gelu") and kind != table:
                start += TABLE_LOAD
            rank = (start, -(way(k) - LEAD * g), k)
            if best is None or rank < best[0]:
                best = (rank, k)
        (start, _, _), k = best
        engine, cost, _ = jobs[k]
        free[engine] = start + cost
        if k[0] == "gelu" or k[0] == "exp" and k[1] != "l3":
            table = k[0]
        end[k] = start + cost + (DMA_HOP if engine == "sp" else HOP)
        order.append(k)
        waiting.remove(k)
        ready.remove(k)
        ready |= {u for u in users.get(k, []) if u in waiting and all(x in end for x in jobs[u][2])}
        if k[0] in TURNS:
            turns.append(k)
        if k[0] == "t":
            ts.append(k)
    return order


HOP, DMA_HOP, LEAD, TABLE_LOAD = .2, 2., 10., 1.3
ORDER = timetable()
SEEN = {}
NTH = {}
for k_ in ORDER:
    SEEN[k_[0]] = NTH[k_] = SEEN.get(k_[0], 0) + 1
TURN = [k_ for k_ in ORDER if k_[0] in TURNS]
T_ORDER = [k_ for k_ in ORDER if k_[0] == "t"]
L3_ORDER = [k_ for k_ in T_ORDER if k_[1] == "l3"]


def nth(step, name="", g=0, i=0):
    return NTH[step, name, g, i]


def nth_all(step, name=""):
    return max(n for k, n in NTH.items() if k[:2] == (step, name))


def nth_of_layer(step, name, g, i=0):
    return sum(k[:2] == (step, name) and n <= NTH[step, name, g, i] for k, n in NTH.items())


def readers(key):
    return [(r, NTH[(r,) + key[1:]]) for r in {**OWN, **TURNS}[key[0]] if (r,) + key[1:] in NTH]


def own_before(step, name, g, i=0):
    mine = [k for k in ORDER if k[0] in OWN and k[2] == g and not (k[0] == "av" and k[3])]
    n = mine.index((step, name, g, i))
    if not n:
        return []
    k = mine[n - 1]
    return readers(k) if k[0] != "av" else [("divide", NTH["divide", k[1], g, 0])]


def turn(step, name, g, i=0):
    n = TURN.index((step, name, g, i))
    return n % 2, (readers(TURN[n - 2]) if n >= 2 else [])


def build(nc, a, out):
    F, BF = mybir.dt.float32, mybir.dt.bfloat16
    ALU, ACT, AX = mybir.AluOpType, mybir.ActivationFunctionType, mybir.AxisListType
    ctx = ExitStack()
    with ctx:
        def sb(name, shape, dt=F):
            return ctx.enter_context(nc.sbuf_tensor(f"{name}_sb", shape, dt))

        sems = {}

        def sem(name):
            if name not in sems:
                sems[name] = ctx.enter_context(nc.semaphore(name))
            return sems[name]

        W = sb("W", [128, len(MATS), 128])
        V = sb("V", [128, len(COLS)])

        def mat(n):
            return W[:, MATS.index(n), :]

        def col(n):
            return V[:, COLS.index(n):COLS.index(n) + 1]

        x_buf = [sb("xa", [128, TOK]), sb("xb", [128, TOK])]
        ctxT = sb("ctxT", [128, TOK])
        hid = sb("hid", [128, F_CHUNKS, TOK])
        k_full = hid[:, 0, :].rearrange("p (g n) -> p g n", g=G)
        k_rest = hid[:, 1, :].rearrange("p (g n) -> p g n", g=G)
        k_ones = hid[0:4, 2, :].bitcast(BF).rearrange("p (e n) -> p e n", e=2)
        cn = hid[:, 3, :].rearrange("p (n d) -> p n d", d=128)
        q_full = sb("q_full", [128, G, GT])
        q_rest = sb("q_rest", [128, G, GT])
        q_part = sb("q_part", [128, 3, G, GT], BF)
        kc_part = sb("kc_part", [128, 3, B * K16], BF)
        k_part = sb("k_part", [128, 3, TOK], BF)
        attT = q_full
        att = q_rest[:, :, :].rearrange("p g (j d) -> p g j d", j=NJ)
        fin = q_full
        q_stack = sb("q_stack", [128, G, SP_, GT], BF)
        k_stack = [sb(f"k_stack{i}", [128, SP_, 2, TOK], BF) for i in range(2)]
        kc_stack = sb("kc_stack", [128, SP_, 2, K16 * B], BF)
        ctx_rep = (k_stack[1][:, :, :, :].rearrange("p s e n -> p (s e n)").bitcast(F)[:, 0:4 * TOK]
                   .rearrange("p (b c a e k) -> p b c a e k", b=B, c=2, a=4, e=2))
        v_ext = [sb(f"v_ext{i}", [128, B, SP_, 2, DH + 1]) for i in range(2)]
        probs = sb("probs", [128, P_SLOTS, SP_ * T])
        ctx_sq = probs[:, 2:4, :].rearrange("p a n -> p (a n)")
        ca_k_split = x_buf[1][:, 0:STRIDE * 128].rearrange("p (r n) -> p r n", r=STRIDE)
        relu = sb("relu", [128, 2, SP_ * T])
        idx = relu[0:64, :, :].bitcast(mybir.dt.int32).rearrange("p a n -> p (a n)")
        dist = probs[0:64, 0:2, :].rearrange("p a n -> p (a n)")
        m_col = sb("m_col", [128, G, NJ, SP_, 2])
        m_part = sb("m_part", [128, G, NJ, 2, 2, SP_], BF)
        m_row = sb("m_row", [32, G, GT], BF)
        rden = sb("rden", [128, G, NJ, H])
        var = sb("var", [128, G, NJ])
        vare = sb("vare", [128, G, NJ])
        rstd = sb("rstd", [128, G, NJ])
        half = sb("half", [128, 8])
        WC = sb("WC", [128, 9, 128])
        rows = sb("rows", [1, 5, 128])
        ones_row = sb("ones_row", [1, 128])
        ones_col = sb("ones_col", [128, 1])
        identb = sb("identb", [128, 128], BF)
        cst = sb("cst", [128, CST])
        two_i = sb("two_i", [64, 128], BF)
        causal = sb("causal", [64, 2, 64], BF)
        e_mask = cst[:, CST - 8:CST]
        q_ones = sb("q_ones", [2, GT], BF)
        km_u8 = sb("km_u8", [1, TOK], mybir.dt.uint8)
        km = sb("km", [1, TOK], BF)
        band = sb("band", [64, TOK], BF)
        cms = sb("cms", [128, B // 2])
        cmse = sb("cmse", [128, B // 2])
        crs = sb("crs", [128, B // 2])
        floor = sb("floor", [128, G, NJ])
        bank = [ctx.enter_context(nc.psum_tensor(f"bank{g}", [128, 512], F)) for g in range(G)]
        s_bank = [ctx.enter_context(nc.psum_tensor(f"s_bank{i}", [128, 512], F)) for i in range(2)]
        t_bank = [ctx.enter_context(nc.psum_tensor(f"t_bank{i}", [128, 512], F)) for i in range(2)]

        def X(x):
            return x_buf[X_OF[x]]

        def tok(g):
            return slice(g * GT, (g + 1) * GT)

        def keys(stack, rows_, s, b):
            return stack[0:rows_, s, :, :].rearrange("p e n -> p (e n)").rearrange("p (x b) -> p x b", b=B)[:, :, b]

        def stacked_k(eng, name):
            n = TERMS * 2 + (2 if name == "l1" else 0)
            eng.wait_ge(sem(f"{name}_k_stacked"), 16 * n)

        def paired(name, side, t, g, x):
            if side == "q":
                return q_part[:, t, g, :], x
            if name == "ca":
                return kc_part[:, t, :], x
            return (k_part[:, t, :].rearrange("p (k b) -> p b k", b=B)[:, g * GB:(g + 1) * GB],
                    x.rearrange("p (b k) -> p b k", b=GB))
        block = ctx.enter_context(nc.Block())

        @block.sync
        def _(sp):
            sp.dma_start(x_buf[0][:], a["xT"]).then_inc(sem("x_loaded"), 16)
            sp.dma_start(W[:, 0:FIRST_MATS, :], a["mats"][:, 0:FIRST_MATS, :]).then_inc(sem("w1_loaded"), 16)
            sp.dma_start(V[:], a["cols"]).then_inc(sem("v_loaded"), 16)
            sp.dma_start(cst[:], a["consts"]).then_inc(sem("cst_loaded"), 16)
            sp.dma_start(ctxT[:], a["ctxT"]).then_inc(sem("ctx_loaded"), 16)
            sp.dma_start(W[:, FIRST_MATS:NEXT_MATS, :], a["mats"][:, FIRST_MATS:NEXT_MATS, :]
                         ).then_inc(sem("w2_loaded"), 16)
            sp.dma_start(W[:, NEXT_MATS:, :], a["mats"][:, NEXT_MATS:, :]).then_inc(sem("w3_loaded"), 16)
            sp.dma_start(cn, a["ctx"].rearrange("(n p) d -> p n d", p=128)).then_inc(sem("cn_loaded"), 16)
            sp.dma_start(idx, a["idx"].to_broadcast([64, TOK])).then_inc(sem("idx_loaded"), 16)
            sp.dma_start(km_u8[:], a["key_mask"]).then_inc(sem("km_loaded"), 16)

            def k_stack_term(name, t):
                low = "k0_low" if name == "sa" else "k_low"
                sp.wait_ge(sem(low), nth_all(low, name))
                if name == "ca":
                    ks, part = kc_stack, kc_part
                    sp.wait_ge(sem("kc_zero"), nth("kc_zero"))
                elif STACK[name]:
                    ks, part = k_stack[1], k_part
                    sp.wait_ge(sem("k_zero"), nth_all("k_zero"))
                else:
                    ks, part = k_stack[0], k_part
                    sp.wait_ge(sem("k_zero_first"), 2)
                if name in ("l2", "l3"):
                    sp.wait_ge(sem("t"), nth_all("t", {"l2": "sa", "l3": "l1"}[name]))
                for e in range(2):
                    r = 16 * t + 8 * e
                    sp.dma_start(ks[r:r + 8, :, e, :], part[64 * e:64 * e + 64, K_PART[t], :]
                                 ).then_inc(sem(f"{name}_k_stacked"), 16)

            def k_rows(i):
                sp.wait_ge(sem("const_ready"), 5)
                if i:
                    sp.wait_ge(sem("k_zero"), nth_all("k_zero"))
                else:
                    sp.wait_ge(sem("k_zero_first"), 2)
                    sp.dma_start(q_stack[R_TERMS:R_MASK, :, :, :].rearrange("r g s n -> r (g s) n"),
                                 q_ones[:].unsqueeze(1).to_broadcast([2, G * SP_, GT])
                                 ).then_inc(sem("q_ones_stacked"), 16)
                sp.dma_start(k_stack[i][R_MASK:R_ALL, :, :, :].rearrange("r s e n -> r s (e n)"),
                             k_ones.rearrange("r e n -> r (e n)").unsqueeze(1).to_broadcast([4, SP_, 2 * TOK])
                             ).then_inc(sem(f"k_rows{i}"), 16)

            def kc_rows():
                sp.wait_ge(sem("kc_zero"), nth("kc_zero"))
                sp.wait_ge(sem("const_ready"), 5)
                for e in range(2):
                    sp.dma_start(kc_stack[R_MASK:R_ALL, :, e, :],
                                 k_ones[:, e, 0:B * K16].unsqueeze(1).to_broadcast([4, SP_, B * K16])
                                 ).then_inc(sem("kc_rows"), 16)

            def km_stack():
                sp.wait_ge(sem("key_mask"), nth("key_mask"))
                sp.wait_ge(sem("k_zero"), nth_all("k_zero"))
                for e in range(2):
                    sp.dma_start(k_stack[1][R_TERMS + e:R_TERMS + e + 1, :, e, :],
                                 km[:].unsqueeze(1).to_broadcast([1, SP_, TOK])).then_inc(sem("l1_k_stacked"), 16)

            def q_to_stack(name, g):
                sp.wait_ge(sem("q_low"), nth("q_low", name, g))
                if name != "sa":
                    before = ATT[ATT.index(name) - 1]
                    sp.wait_ge(sem("t"), nth("t", before, g, T_UNITS[before] - 1))
                for t in range(TERMS):
                    sp.dma_start(q_stack[16 * t:16 * t + 16, g, :, :], q_part[:, Q_PART[t], g, :]
                                 ).then_inc(sem(f"q_stacked{g}"), 16)

            for step, name, g, i in ORDER:
                if step == "k_stack":
                    k_stack_term(name, i)
                elif step == "k_rows":
                    k_rows(i)
                elif step == "kc_rows":
                    kc_rows()
                elif step == "km_stack":
                    km_stack()
                elif step == "q_stack":
                    q_to_stack(name, g)
                elif step == "m_stack":
                    sp.wait_ge(sem("m_row"), nth("m_row", name, g))
                    sp.dma_start(q_stack[R_MASK:R_ALL, g, :, :], m_row[:, g, :]).then_inc(sem(f"m_stacked{g}"), 16)
                elif step == "store":
                    sp.wait_ge(sem("fin"), nth("fin", "", g))
                    sp.dma_start(out[g * GT:(g + 1) * GT, :].rearrange("(j p) d -> p j d", p=128),
                                 fin[:, g, :].rearrange("p (j d) -> p j d", j=NJ)).then_inc(sem("stored"), 16)
            sp.wait_ge(sem("stored"), 16 * G)

        @block.tensor
        def _(pe):
            def take(step, name, g, i=0):
                for reader, n in own_before(step, name, g, i):
                    pe.wait_ge(sem(reader), n)
                return bank[g]

            def take_turn(step, name, g, i=0):
                which, before = turn(step, name, g, i)
                for reader, n in before:
                    pe.wait_ge(sem(reader), n)
                return s_bank[which]

            def mm(o, l, r, start=True, stop=True):
                return pe.matmul(o, l, r, start=start, stop=stop)

            def x_ready(name, g):
                x = X_IN[name]
                if x == "x0":
                    pe.wait_ge(sem("x_loaded"), 16)
                elif x == "x6":
                    pe.wait_ge(sem("x6"), nth("x6", "g", g))
                else:
                    pe.wait_ge(sem("ln"), nth("ln", X_FROM[x], g))

            def weights(i):
                o = take_turn("weights", "", 0, i)
                if i == 0:
                    pe.wait_ge(sem("w1_loaded"), 16)
                    pe.wait_ge(sem("w2_loaded"), 16)
                    for c, n in enumerate(["sa_o", "ca_o", "l1_updT"]):
                        mm(o[:, c * 128:(c + 1) * 128], mat(n), mat("center"))
                    mm(o[:, 384:512], mat("l1_updsT"), mat("center"), stop=False)
                    last = mm(o[:, 384:512], mat("ident"), mat("center"), start=False)
                elif i == 1:
                    pe.wait_ge(sem("w3_loaded"), 16)
                    for c in range(F_CHUNKS):
                        last = mm(o[:, c * 128:(c + 1) * 128], mat(f"f_w2_{c}"), mat("center"))
                elif i == 2:
                    pe.wait_ge(sem("weights_kept"), nth("weights_kept", i=0))
                    pe.wait_ge(sem("v_loaded"), 16)
                    mm(o[:, 0:128], mat("l1_outT"), WC[:, WC_OF["l1_upd"], :])
                    last = mm(o[0:1, 128:256], col("l2_vb"), mat("center"))
                else:
                    pe.wait_ge(sem("weights_kept"), nth("weights_kept", i=2))
                    for name, terms in (("sa", [("sa_vb", WC[:, 0, :]), ("sa_ob", mat("center"))]),
                                        ("ca", [("ca_vb", WC[:, 1, :]), ("ca_ob", mat("center"))]),
                                        ("f", [("f_b2", mat("center"))]),
                                        ("l1", [("l1_tb", WC[:, 8, :]), ("l1_ob", WC[:, WC_OF["l1_upd"], :]),
                                                ("l1_ub", mat("center"))])):
                        c = ROW_OF[name] * 128
                        for n, (b, m) in enumerate(terms):
                            last = mm(o[0:1, c:c + 128], col(b), m, start=n == 0, stop=n == len(terms) - 1)
                last.then_inc(sem("weights"), 1)

            def keys_of(name, g):
                o = take_turn("k", name, g)
                pe.wait_ge(sem("w1_loaded" if name == "sa" else "w2_loaded"), 16)
                pe.wait_ge(sem("x_loaded" if name == "sa" else "ctx_loaded"), 16)
                if name == "ca":
                    pe.wait_ge(sem("ca_k_split"), 1)
                    for r in range(STRIDE):
                        last = mm(o[:, 0:B * K16].rearrange("p (k b) -> p k b", b=B), ca_k_split[:, r, :],
                                  ctxT[:].rearrange("p (b k r) -> p k b r", b=B, r=STRIDE)[:, :, :, r],
                                  start=r == 0, stop=r == STRIDE - 1)
                    last.then_inc(sem("k"), 1)
                    return
                if name == "l3":
                    pe.wait_ge(sem("ctx_normed"), nth("ctx_normed", g=g))
                    pe.wait_ge(sem("gammas"), 1)
                mm(o[:, 0:GT], mat(f"{name}_k"), (x_buf[0] if name == "sa" else ctxT)[:, tok(g)]
                   ).then_inc(sem("k"), 1)

            def values(name, g):
                o = take_turn("v", name, g)
                src = x_buf[0] if name == "sa" else ctxT
                pe.wait_ge(sem("w1_loaded" if name == "sa" else "w2_loaded"), 16)
                pe.wait_ge(sem("x_loaded" if name == "sa" else "ctx_loaded"), 16)
                if name == "l3":
                    pe.wait_ge(sem("ctx_normed"), nth("ctx_normed", g=g))
                    pe.wait_ge(sem("gammas"), 1)
                for i in range(GB):
                    b = g * GB + i
                    for e in range(2):
                        w = mat(f"{name}_v").rearrange("p (s e n) -> p s e n", e=2, n=DH)[:, :, e, :]
                        last = mm(o[64 * e:64 * e + 64, i * 64:(i + 1) * 64].rearrange("p (s n) -> p s n", n=DH),
                                  src[:, b * T:(b + 1) * T], w)
                last.then_inc(sem("v"), 1)

            def values_ca(g):
                o = take_turn("v", "ca", g)
                pe.wait_ge(sem("w2_loaded"), 16)
                pe.wait_ge(sem("ctx_rep"), 1)
                for i in range(GB):
                    b = g * GB + i
                    for pi in range(2):
                        rows_ = ctx_rep[:, b, pi, :, :, :].rearrange("p a e k -> p (a e k)")
                        w = mat("ca_v").rearrange("p (a c n) -> p a c n", a=4, c=2)[:, :, pi, :]
                        c = (i * 2 + pi) * 64
                        last = mm(o[:, c:c + 64].rearrange("p (a n) -> p a n", a=4), rows_, w)
                last.then_inc(sem("v"), 1)

            def scores(name, g, i):
                o = take_turn("s", name, g, i)
                if i == 0:
                    pe.wait_ge(sem(f"q_stacked{g}"), 16 * TERMS * (ATT.index(name) + 1))
                    stacked_k(pe, name)
                if name == "ca":
                    for ii in range(GB):
                        b, c = g * GB + ii, 64 * (ii % 2)
                        for s in range(SP_):
                            k = (ii // 2) * 256 + s * 32
                            last = mm(o[c:c + 64, k:k + 32], q_stack[0:R_TERMS, g, s, ii * T:(ii + 1) * T],
                                      keys(kc_stack, R_TERMS, s, b))
                    last.then_inc(sem("s"), 1)
                    return
                if name == "l1" and i == 0:
                    pe.wait_ge(sem("q_ones_stacked"), 16)
                r = R_MASK if name == "l1" else R_TERMS
                j, hf = i // 2, i % 2
                if name == "l2":
                    pe.wait_ge(sem("const_ready"), 5)
                    mm(o[:, :].rearrange("p (c k) -> p c k", c=8), two_i[:, :],
                       causal[:, 0, :].unsqueeze(1).to_broadcast([64, 8, 64]))
                for c in range(2):
                    t = (2 * j + c) * T
                    b = g * GB + 2 * j + c
                    for s4 in range(4):
                        s = 4 * hf + s4
                        last = pe.matmul(o[64 * c:64 * c + 64, s4 * 128:(s4 + 1) * 128],
                                         q_stack[0:r, g, s, t:t + T],
                                         keys(k_stack[STACK[name]], r, s, b),
                                         start=name != "l2", stop=True, skip_group_check=name == "l2")
                last.then_inc(sem("s"), 1)

            def max_rows(name, g):
                o = take("m", name, g)[0:32, 0:GT // 2].bitcast(BF)
                pe.wait_ge(sem("max_parts"), nth("max_parts", name, g))
                pe.wait_ge(sem("const_ready"), 5)
                for j in range(NJ):
                    last = pe.transpose(o[:, j * 128:(j + 1) * 128],
                                        m_part[:, g, j, :, :, :].rearrange("p a e s -> p (a e s)"), identb[:, :])
                last.then_inc(sem("m"), 1)

            def scores_t(name, g, i):
                u = T_ORDER.index(("t", name, g, i))
                if i == 0:
                    if name == "l3":
                        pe.wait_ge(sem(f"q_stacked{g}"), 16 * TERMS * (ATT.index(name) + 1))
                        stacked_k(pe, name)
                        pe.wait_ge(sem("band"), 1)
                    else:
                        pe.wait_ge(sem(f"m_stacked{g}"), 16 * (ATT.index(name) + 1))
                        pe.wait_ge(sem("q_ones_stacked"), 16)
                        if name == "ca":
                            pe.wait_ge(sem("kc_rows"), 32)
                        else:
                            pe.wait_ge(sem(f"k_rows{STACK[name]}"), 16)
                if u >= 2:
                    pe.wait_ge(sem("exp"), nth(*("exp",) + T_ORDER[u - 2][1:]))
                o = t_bank[u % 2]
                if name == "ca":
                    for ii in range(GB):
                        b = g * GB + ii
                        for s in range(SP_):
                            c, k = 32 * (s // 2), ii * 128 + (s % 2) * 64
                            last = mm(o[c:c + 32, k:k + 64], keys(kc_stack, R_ALL, s, b),
                                      q_stack[0:R_ALL, g, s, ii * T:(ii + 1) * T])
                    last.then_inc(sem("t"), 1)
                    return
                b = g * GB + i
                r = R_TERMS if name == "l3" else R_ALL
                masked = name in ("l2", "l3")
                if masked:
                    m = causal[:, 1, :] if name == "l2" else band[:, b * T:(b + 1) * T]
                    mm(o[:, :].rearrange("p (s q) -> p s q", s=SP_), two_i[:, :],
                       m.unsqueeze(1).to_broadcast([64, SP_, 64]))
                for s in range(SP_):
                    last = pe.matmul(o[:, s * T:(s + 1) * T], keys(k_stack[STACK[name]], r, s, b),
                                     q_stack[0:r, g, s, i * T:(i + 1) * T],
                                     start=not masked, stop=True, skip_group_check=masked)
                last.then_inc(sem("t"), 1)

            def attend(name, g, i):
                u = T_ORDER.index(("t", name, g, i))
                if i == 0:
                    take("av", name, g)
                    pe.wait_ge(sem("v_even"), nth("v_even", name, g))
                    if name != "ca":
                        pe.wait_ge(sem("v_odd"), nth("v_odd", name, g))
                    pe.wait_ge(sem("v_base"), nth("v_base", i=V_BASE[name]))
                if name == "l3":
                    pe.wait_ge(sem("square"), nth("square", name, g, i))
                else:
                    pe.wait_ge(sem("exp"), nth("exp", name, g, i))
                ve = v_ext[VALUES[name]]
                for ii in range(GB) if name == "ca" else (i,):
                    b = g * GB + ii
                    c = 64 * (ii % 2)
                    o = bank[g][c:c + 64, (ii // 2) * 144:(ii // 2) * 144 + 144]
                    if name == "ca":
                        for pi in range(2):
                            last = mm(o.rearrange("p (a c n) -> p a c n", a=4, c=2)[:, :, pi, :],
                                      probs[:, u % P_SLOTS, ii * 128 + pi * 64:ii * 128 + pi * 64 + 64],
                                      ve[:, b, :, :, :].rearrange("p s e n -> p (s e n)")[:, pi * 72:pi * 72 + 72]
                                      .rearrange("p (a n) -> p a n", a=4))
                    else:
                        for s in range(SP_):
                            last = mm(o[:, s * 18:s * 18 + 18], probs[:, u % P_SLOTS, s * T:(s + 1) * T],
                                      ve[:, b, s, :, :].rearrange("p e n -> p (e n)"))
                last.then_inc(sem("av"), 1)

            def flip(step, name, g, signal):
                o = take(step, name, g)
                pe.wait_ge(sem(signal), nth(signal, name, g))
                for j in range(NJ):
                    last = pe.transpose(o[:, j * 128:(j + 1) * 128], att[:, g, j, :], mat("ident"))
                last.then_inc(sem(step), 1)

            def centred(name, g):
                bank_ = take("z", name, g)
                if name == "f":
                    pe.wait_ge(sem("gelu"), nth("gelu", "f", g, 1))
                else:
                    pe.wait_ge(sem("attT"), nth("attT", name, g))
                pe.wait_ge(sem("weights_kept"), nth_all("weights_kept"))
                res = WC[:, WC_OF["l1_res"], :] if name == "l1" else mat("center")
                for j in range(NJ):
                    o = bank_[:, j * 128:(j + 1) * 128]
                    t = slice(g * GT + j * 128, g * GT + (j + 1) * 128)
                    mm(o, X(X_IN[name])[:, t], res, stop=False)
                    mm(o, ones_row[:, :], rows[:, ROW_OF[name], :], start=False, stop=False)
                    if name == "f":
                        for c in range(F_CHUNKS):
                            last = mm(o, hid[:, c, t], WC[:, WC_OF["f"] + c, :], start=False, stop=c == F_CHUNKS - 1)
                    else:
                        w = mat("center") if name == "l2" else WC[:, WC_OF[name], :]
                        last = mm(o, attT[:, g, j * 128:(j + 1) * 128], w, start=False)
                last.then_inc(sem("z"), 1)

            def hidden(name, g, i):
                x_ready(name, g)
                o = take("h", name, g, i)
                for c in range(2):
                    last = mm(o[:, c * GT:(c + 1) * GT], mat(f"{name}_w1_{2 * i + c}"), X(X_IN[name])[:, tok(g)])
                last.then_inc(sem("h"), 1)

            for step, name, g, i in ORDER:
                if step == "weights":
                    weights(i)
                elif step == "k":
                    keys_of(name, g)
                elif step == "v" and name == "ca":
                    values_ca(g)
                elif step == "v":
                    values(name, g)
                elif step == "ctx_rows":
                    o = take_turn("ctx_rows", "", g)
                    pe.wait_ge(sem("ctx_scale"), 1)
                    for j in range(NJ):
                        last = pe.transpose(o[:, j * 128:(j + 1) * 128], cn[:, g * NJ + j, :], mat("ident"))
                    last.then_inc(sem("ctx_rows"), 1)
                elif step == "q":
                    x_ready(name, g)
                    pe.wait_ge(sem("w1_loaded" if name == "sa" else "w2_loaded"), 16)
                    if name == "l3":
                        pe.wait_ge(sem("gammas"), 1)
                    o = take("q", name, g)
                    mm(o[:, 0:GT], mat(f"{name}_q"), X(X_IN[name])[:, tok(g)]).then_inc(sem("q"), 1)
                elif step == "s":
                    scores(name, g, i)
                elif step == "m":
                    max_rows(name, g)
                elif step == "t":
                    scores_t(name, g, i)
                elif step == "av":
                    attend(name, g, i)
                elif step == "flip":
                    flip("flip", name, g, "divide")
                elif step == "z":
                    centred(name, g)
                elif step == "flip_x":
                    flip("flip_x", name, g, "scale")
                elif step == "h":
                    hidden(name, g, i)
                elif step == "y":
                    o = take("y", "g", g)
                    pe.wait_ge(sem("gelu"), nth("gelu", "g", g, 1))
                    for c in range(F_CHUNKS):
                        last = mm(o[:, 0:GT], mat(f"g_w2_{c}"), hid[:, c, tok(g)], start=c == 0,
                                  stop=c == F_CHUNKS - 1)
                    last.then_inc(sem("y"), 1)
                elif step == "ms":
                    o = take("ms", name, g)
                    pe.wait_ge(sem("x_sq"), nth("x_sq", name, g))
                    for j in range(NJ):
                        last = mm(o[:, j:j + 1], k_full[:, g, j * 128:(j + 1) * 128], ones_col[:, :])
                    last.then_inc(sem("ms"), 1)
                elif step == "out":
                    o = take("out", "", g)
                    pe.wait_ge(sem("attT"), nth("attT", "l3", g))
                    for j in range(NJ):
                        oj = o[:, j * 128:(j + 1) * 128]
                        mm(oj, X("x6")[:, g * GT + j * 128:g * GT + (j + 1) * 128], mat("ident"), stop=False)
                        last = mm(oj, attT[:, g, j * 128:(j + 1) * 128], mat("l3_o"), start=False)
                    last.then_inc(sem("out"), 1)

        @block.scalar
        def _(act):
            def parts(name, side, g):
                act.wait_ge(sem(side), nth(side, name, g))
                if side == "q":
                    dst, src = q_full[:, g, :], bank[g][:, 0:GT]
                    if name != "sa":
                        act.wait_ge(sem(f"q_stacked{g}"), 16 * TERMS * ATT.index(name))
                else:
                    dst, src = k_full[:, g, :], s_bank[turn("k", name, g)[0]][:, 0:GT]
                    if name == "ca":
                        act.wait_ge(sem("k0_low"), nth("k0_low", "sa", g))
                    elif name == "l1":
                        stacked_k(act, "sa")
                        act.wait_ge(sem("k_low"), nth("k_low", "ca"))
                    elif name != "sa":
                        before = ATT[ATT.index(name) - 1]
                        stacked_k(act, before)
                        act.wait_ge(sem("k_low"), nth("k_low", before, g))
                    if name == "l3":
                        act.wait_ge(sem("z"), nth("z", "f", g))
                if name == "l3":
                    act.activation(dst, src, ACT.Copy)
                    act.activation(*paired(name, side, 0, g, src), ACT.Copy).then_inc(sem(f"{side}_parts"), 1)
                    return
                bias = col(f"{name}_{side}b")
                act.activation(dst, src, ACT.Identity, bias=bias, scale=1.0)
                act.activation(*paired(name, side, 0, g, src), ACT.Identity, bias=bias, scale=1.0
                               ).then_inc(sem(f"{side}_parts"), 1)

            def value_half(name, g):
                act.wait_ge(sem("v"), nth("v", name, g))
                act.wait_ge(sem("v_base"), nth("v_base", i=V_BASE[name]))
                if name in V_BEFORE:
                    act.wait_ge(sem("av"), nth_all("av", V_BEFORE[name]))
                src = s_bank[turn("v", name, g)[0]][64:128, 0:256].rearrange("p (c d) -> p c d", d=DH)
                dst = v_ext[VALUES[name]][64:128, g * GB:(g + 1) * GB, :, :, :].rearrange("p b s e n -> p (b s) e n")
                act.activation(dst[:, :, 1, 0:DH], src, ACT.Copy).then_inc(sem("v_odd"), 1)

            def exps(name, g, i):
                u = T_ORDER.index(("t", name, g, i))
                act.wait_ge(sem("t"), nth("t", name, g, i))
                if name == "l3":
                    n = L3_ORDER.index(("t", name, g, i))
                    if n >= 2:
                        act.wait_ge(sem("square"), nth(*("square",) + L3_ORDER[n - 2][1:]))
                    act.activation(relu[:, n % 2, :], t_bank[u % 2][:, :], ACT.Relu).then_inc(sem("exp"), 1)
                    return
                if u >= P_SLOTS:
                    act.wait_ge(sem("av"), nth(*("av",) + T_ORDER[u - P_SLOTS][1:]))
                else:
                    act.wait_ge(sem("band"), 1)
                    act.wait_ge(sem("ctx_ms"), 1)
                act.activation(probs[:, u % P_SLOTS, :], t_bank[u % 2][:, :], ACT.Exp, scale=SCALE
                               ).then_inc(sem("exp"), 1)

            act.wait_ge(sem("v_loaded"), 16)
            for step, name, g, i in ORDER:
                if step == "k_parts":
                    parts(name, "k", g)
                elif step == "q_parts":
                    parts(name, "q", g)
                elif step == "v_odd":
                    value_half(name, g)
                elif step == "ctx_ms":
                    act.wait_ge(sem("cn_loaded"), 16)
                    for n in range(B // 2):
                        last = act.activation(ctx_sq[:, n * 128:(n + 1) * 128], cn[:, n, :], ACT.Square,
                                              scale=D ** -0.5, accum_out=cms[:, n:n + 1])
                    last.then_inc(sem("ctx_ms"), 1)
                elif step == "ctx_normed":
                    act.wait_ge(sem("ctx_rows"), nth("ctx_rows", g=g))
                    act.activation(ctxT[:, tok(g)], s_bank[turn("ctx_rows", "", g)[0]][:, 0:GT], ACT.Copy
                                   ).then_inc(sem("ctx_normed"), 1)
                elif step == "m_row":
                    act.wait_ge(sem("m"), nth("m", name, g))
                    if name != "sa":
                        act.wait_ge(sem(f"m_stacked{g}"), 16 * ATT.index(name))
                    act.activation(m_row[:, g, :], bank[g][0:32, 0:GT // 2].bitcast(BF), ACT.Copy
                                   ).then_inc(sem("m_row"), 1)
                elif step == "exp":
                    exps(name, g, i)
                elif step == "attT":
                    act.wait_ge(sem("flip"), nth("flip", name, g))
                    act.activation(attT[:, g, :], bank[g][:, 0:GT], ACT.Copy).then_inc(sem("attT"), 1)
                elif step == "var":
                    act.wait_ge(sem("z"), nth("z", name, g))
                    for j in range(NJ):
                        last = act.activation(att[:, g, j, :], bank[g][:, j * 128:(j + 1) * 128], ACT.Square,
                                              scale=D ** -0.5, accum_out=var[:, g, j:j + 1])
                    last.then_inc(sem("var"), 1)
                elif step == "ln":
                    act.wait_ge(sem("flip_x"), nth("flip_x", name, g))
                    if name == "sa":
                        act.wait_ge(sem("k"), nth("k", "ca"))
                    act.activation(X(X_OUT[name])[:, tok(g)], bank[g][:, 0:GT], ACT.Identity,
                                   bias=col(f"{name}_lb"), scale=col(f"{name}_lg")).then_inc(sem("ln"), 1)
                elif step == "gelu":
                    act.wait_ge(sem("h"), nth("h", name, g, i))
                    if name == "f" and i == 0:
                        act.wait_ge(sem("k_low"), nth_all("k_low", "l2"))
                        act.wait_ge(sem("ctx_rows"), nth_all("ctx_rows"))
                        act.wait_ge(sem("kc_rows"), 32)
                        act.wait_ge(sem("k_rows1"), 16)
                    elif i == 0:
                        act.wait_ge(sem("k_low"), nth("k_low", "l3", g))
                    for c in range(2):
                        cc = 2 * i + c
                        last = act.activation(hid[:, cc, tok(g)], bank[g][:, c * GT:(c + 1) * GT], ACT.Gelu,
                                              bias=col(f"{name}_b1_{cc}"), scale=1.0)
                    last.then_inc(sem("gelu"), 1)
                elif step == "x_sq":
                    act.wait_ge(sem("x6"), nth("x6", "g", g))
                    act.activation(k_full[:, g, :], X("x6")[:, tok(g)], ACT.Square, scale=D ** -0.5
                                   ).then_inc(sem("x_sq"), 1)
                elif step == "fin":
                    act.wait_ge(sem("out"), nth("out", "", g))
                    act.activation(fin[:, g, :], bank[g][:, 0:GT], ACT.Copy).then_inc(sem("fin"), 1)

        @block.vector
        def _(dve):
            def weights_kept(i):
                dve.wait_ge(sem("weights"), nth("weights", i=i))
                o = s_bank[turn("weights", "", 0, i)[0]]
                if i < 2:
                    last = dve.tensor_copy(WC[:, 4 * i:4 * i + 4, :].rearrange("p a n -> p (a n)"), o[:, :])
                elif i == 2:
                    dve.tensor_copy(WC[:, 8, :], o[:, 0:128])
                    last = dve.tensor_copy(rows[:, 4, :], o[0:1, 128:256])
                else:
                    last = dve.tensor_copy(rows[:, 0:4, :].rearrange("p a n -> p (a n)"), o[0:1, :])
                last.then_inc(sem("weights_kept"), 1)

            def value_half(name, g):
                dve.wait_ge(sem("v"), nth("v", name, g))
                dve.wait_ge(sem("v_base"), nth("v_base", i=V_BASE[name]))
                o = s_bank[turn("v", name, g)[0]]
                if name == "ca":
                    vc = v_ext[1][:, g * GB:(g + 1) * GB, :, :, :].rearrange("p b s e n -> p (b s e) n")
                    vc = vc.rearrange("p (c a) n -> p c a n", a=8)
                    dve.tensor_tensor(vc[:, :, :, 0:DH], o[:, :].rearrange("p (c a n) -> p c a n", a=8, n=DH),
                                      e_mask.unsqueeze(1).unsqueeze(3).to_broadcast([128, 2 * GB, 8, DH]), ALU.mult
                                      ).then_inc(sem("v_even"), 1)
                    return
                if name in V_BEFORE:
                    dve.wait_ge(sem("av"), nth_all("av", V_BEFORE[name]))
                src = o[0:64, 0:256].rearrange("p (c d) -> p c d", d=DH)
                dst = v_ext[VALUES[name]][0:64, g * GB:(g + 1) * GB, :, :, :].rearrange("p b s e n -> p (b s) e n")
                dve.tensor_copy(dst[:, :, 0, 0:DH], src).then_inc(sem("v_even"), 1)

            def key_mask():
                dve.wait_ge(sem("km_loaded"), 16)
                dve.tensor_scalar(km[:].rearrange("p (k b) -> p b k", b=B),
                                  km_u8[:].rearrange("p (b k) -> p b k", b=B), -1.0, KEY_BIG, ALU.add, ALU.mult
                                  ).then_inc(sem("key_mask"), 1)

            def band_mask():
                dve.wait_ge(sem("idx_loaded"), 16)
                dve.tensor_scalar(dist, idx, cst[0:64, 386:387], None, ALU.subtract).then_inc(sem("distance"), 1)
                dve.wait_ge(sem("distance"), 1)
                dve.tensor_tensor(dist, dist, dist, ALU.mult).then_inc(sem("distance"), 1)
                dve.wait_ge(sem("distance"), 2)
                dve.tensor_scalar(band[:], dist, 1.0, -BIG, ALU.is_gt, ALU.mult).then_inc(sem("band"), 1)

            def maxima(name, g, i):
                dve.wait_ge(sem("s"), nth("s", name, g, i))
                if name == "ca":
                    o, w = m_col[:, g, :, :, :].rearrange("p j s e -> p (j s e)"), K16
                else:
                    o, w = m_col[:, g, i // 2, 4 * (i % 2):4 * (i % 2) + 4, :].rearrange("p s e -> p (s e)"), T
                dve.tensor_reduce(o, s_bank[turn("s", name, g, i)[0]][:, :].rearrange("p (c k) -> p c k", k=w),
                                  AX.X, ALU.max).then_inc(sem("max"), 1)

            def max_parts(name, g):
                dve.wait_ge(sem("max"), max(nth("max", name, g, i) for i in range(S_UNITS[name])))
                src = m_col[:, g, :, :, :].rearrange("p j s e -> p j e s")
                dve.tensor_scalar(m_part[:, g, :, 0, :, :], src, -1.0, None, ALU.mult).then_inc(sem("max_hi"), 1)
                dve.wait_ge(sem("max_hi"), nth("max_parts", name, g))
                dve.tensor_tensor(m_part[:, g, :, 1, :, :], src, m_part[:, g, :, 0, :, :], ALU.add
                                  ).then_inc(sem("max_parts"), 1)

            def divide(name, g):
                src = bank[g][:, 0:NJ * 144].rearrange("p (h n) -> p h n", n=DH + 1)
                rd = rden[:, g, :, :].rearrange("p j h -> p (j h)")
                dve.wait_ge(sem("av"), nth("av", name, g, T_UNITS[name] - 1))
                den = src[:, :, DH]
                if name == "l3":
                    dve.wait_ge(sem("floor"), nth("floor", name, g))
                    dve.tensor_tensor(rden[:, g, :, :], den.rearrange("p (j h) -> p j h", j=NJ),
                                      floor[:, g, :].unsqueeze(2).to_broadcast([128, NJ, H]),
                                      ALU.max).then_inc(sem("den_floored"), 1)
                    dve.wait_ge(sem("den_floored"), nth_of_layer("divide", name, g))
                    den = rd
                dve.reciprocal(rd, den).then_inc(sem("rden"), 1)
                dve.wait_ge(sem("rden"), nth("divide", name, g))
                dve.tensor_tensor(att[:, g, :, :].rearrange("p j (h n) -> p (j h) n", n=DH), src[:, :, 0:DH],
                                  rd.unsqueeze(2).to_broadcast([128, NJ * H, DH]), ALU.mult
                                  ).then_inc(sem("divide"), 1)

            dve.memset(k_stack[0][:, 0:4, :, :].bitcast(F), 0.0).then_inc(sem("k_zero_first"), 1)
            dve.memset(ones_row[:], 1.0)
            dve.memset(ones_col[:], 1.0)
            dve.memset(q_ones[:], 1.0).then_inc(sem("const_ready"), 1)
            for step, name, g, i in ORDER:
                if step == "weights_kept":
                    weights_kept(i)
                elif step == "constants":
                    dve.wait_ge(sem("cst_loaded"), 16)
                    dve.tensor_copy(identb[:], cst[:, 0:128]).then_inc(sem("const_ready"), 1)
                    dve.tensor_copy(two_i[:], cst[0:64, 128:256]).then_inc(sem("const_ready"), 1)
                    dve.tensor_copy(causal[:], cst[0:64, 256:384].rearrange("p (a k) -> p a k", a=2)
                                    ).then_inc(sem("const_ready"), 1)
                    dve.tensor_copy(k_ones, cst[0:4, 384:386].unsqueeze(2).to_broadcast([4, 2, TOK])
                                    ).then_inc(sem("const_ready"), 1)
                elif step == "ca_k_split":
                    dve.memset(ca_k_split[:], 0.0).then_inc(sem("ca_k_zero"), 1)
                    dve.wait_ge(sem("ca_k_zero"), 1)
                    dve.wait_ge(sem("w2_loaded"), 16)
                    for r in range(STRIDE):
                        pi, e = r // 2, r % 2
                        of_e = slice(64 * e, 64 * e + 64)
                        last = dve.tensor_copy(
                            ca_k_split[:, r, of_e].rearrange("p (a c) -> p a c", c=2)[:, :, pi],
                            mat("ca_k")[:, of_e].rearrange("p (a c) -> p a c", c=2)[:, :, pi])
                    last.then_inc(sem("ca_k_split"), 1)
                elif step == "k0_rest":
                    dve.wait_ge(sem("k_parts"), nth("k_parts", name, g))
                    part, x = paired(name, "k", 0, g, k_full[:, g, :])
                    dve.tensor_tensor(paired(name, "k", 0, g, k_rest[:, g, :])[1], x, part, ALU.subtract
                                      ).then_inc(sem("k0_rest"), 1)
                elif step == "k0_mid":
                    dve.wait_ge(sem("k0_rest"), nth("k0_rest", name, g))
                    dve.tensor_copy(*paired(name, "k", 1, g, k_rest[:, g, :])).then_inc(sem("k0_mid"), 1)
                elif step == "k0_low":
                    dve.wait_ge(sem("k0_mid"), nth("k0_mid", name, g))
                    part, x = paired(name, "k", 1, g, k_rest[:, g, :])
                    dve.tensor_tensor(paired(name, "k", 2, g, k_rest[:, g, :])[0], x, part, ALU.subtract
                                      ).then_inc(sem("k0_low"), 1)
                elif step == "v_even":
                    value_half(name, g)
                elif step == "key_mask":
                    key_mask()
                elif step == "band":
                    band_mask()
                elif step == "gammas":
                    dve.wait_ge(sem("w3_loaded"), 16)
                    dve.wait_ge(sem("v_loaded"), 16)
                    for n, c in (("l3_q", "l3_gq"), ("l3_k", "l3_gk"), ("l3_v", "l3_gk")):
                        last = dve.tensor_scalar(mat(n), mat(n), col(c), None, ALU.mult)
                    last.then_inc(sem("gammas"), 1)
                elif step == "ctx_scale":
                    dve.wait_ge(sem("ctx_rs"), 1)
                    dve.tensor_tensor(cn, cn, crs[:].unsqueeze(2).to_broadcast([128, B // 2, 128]), ALU.mult
                                      ).then_inc(sem("ctx_scale"), 1)
                elif step == "q_rest":
                    dve.wait_ge(sem("q_parts"), nth("q_parts", name, g))
                    dve.tensor_tensor(q_rest[:, g, :], q_full[:, g, :], q_part[:, 0, g, :], ALU.subtract
                                      ).then_inc(sem("q_rest"), 1)
                elif step == "q_mid":
                    dve.wait_ge(sem("q_rest"), nth("q_rest", name, g))
                    dve.tensor_copy(q_part[:, 1, g, :], q_rest[:, g, :]).then_inc(sem("q_mid"), 1)
                elif step == "q_low":
                    dve.wait_ge(sem("q_mid"), nth("q_mid", name, g))
                    dve.tensor_tensor(q_part[:, 2, g, :], q_rest[:, g, :], q_part[:, 1, g, :], ALU.subtract
                                      ).then_inc(sem("q_low"), 1)
                elif step == "max":
                    maxima(name, g, i)
                elif step == "max_parts":
                    max_parts(name, g)
                elif step == "divide":
                    divide(name, g)
                elif step == "scale":
                    dve.wait_ge(sem("rstd"), nth("rstd", name, g))
                    dve.tensor_tensor(att[:, g, :, :], bank[g][:, 0:GT].rearrange("p (j d) -> p j d", j=NJ),
                                      rstd[:, g, :].unsqueeze(2).to_broadcast([128, NJ, 128]), ALU.mult
                                      ).then_inc(sem("scale"), 1)
                elif step == "x6":
                    dve.wait_ge(sem("y"), nth("y", "g", g))
                    dve.scalar_tensor_tensor(X("x6")[:, tok(g)], bank[g][:, 0:GT], col("g_b2"), X("x5")[:, tok(g)],
                                             ALU.add, ALU.add).then_inc(sem("x6"), 1)
                elif step == "floor":
                    dve.wait_ge(sem("ms"), nth("ms", name, g))
                    dve.tensor_scalar(floor[:, g, :], bank[g][:, 0:NJ], EPS_DEN / SCALE ** 2,
                                      EPS_RMS * EPS_DEN / SCALE ** 2, ALU.mult, ALU.add).then_inc(sem("floor"), 1)
                elif step == "square":
                    u = T_ORDER.index(("t", name, g, i))
                    n = L3_ORDER.index(("t", name, g, i))
                    dve.wait_ge(sem("exp"), nth("exp", name, g, i))
                    dve.wait_ge(sem("av"), nth(*("av",) + T_ORDER[u - P_SLOTS][1:]))
                    dve.tensor_tensor(probs[:, u % P_SLOTS, :], relu[:, n % 2, :], relu[:, n % 2, :], ALU.mult
                                      ).then_inc(sem("square"), 1)

        @block.gpsimd
        def _(pool):
            def v_base(i):
                n = B * SP_
                which = 0 if i == 0 else 1
                pool.wait_ge(sem("cst_loaded"), 16)
                if i == 1:
                    flat = v_ext[1][:, :, :, :, :].rearrange("p b s e n -> p (b s e) n")
                    pool.tensor_copy(flat[:, :, DH].rearrange("p (c a) -> p c a", a=8),
                                     e_mask.unsqueeze(1).to_broadcast([128, 2 * B, 8])).then_inc(sem("v_base"), 1)
                    return
                if i == 2:
                    pool.wait_ge(sem("av"), nth_all("av", "ca"))
                pool.memset(v_ext[which][:], 0.0).then_inc(sem("v_zero"), 1)
                pool.wait_ge(sem("v_zero"), 1 if i == 0 else 2)
                ve = v_ext[which][:, :, :, :, :].rearrange("p b s e n -> p (b s) e n")
                pool.tensor_copy(ve[:, :, :, DH], cst[:, 387:389].unsqueeze(1).to_broadcast([128, n, 2])
                                 ).then_inc(sem("v_base"), 1)

            pool.memset(k_stack[0][:, 4:8, :, :].bitcast(F), 0.0).then_inc(sem("k_zero_first"), 1)
            pool.memset(half[:], -0.5).then_inc(sem("half_ready"), 1)
            for step, name, g, i in ORDER:
                if step == "v_base":
                    v_base(i)
                elif step == "ctx_rep":
                    pool.wait_ge(sem("ctx_loaded"), 16)
                    for pi in range(2):
                        for e in range(2):
                            last = pool.tensor_copy(
                                ctx_rep[:, :, pi, :, e, :],
                                ctxT[:].rearrange("p (b k r) -> p b k r", b=B, r=STRIDE)[:, :, :, 2 * pi + e]
                                .unsqueeze(2).to_broadcast([128, B, 4, K16]))
                    last.then_inc(sem("ctx_rep"), 1)
                elif step == "kc_zero":
                    pool.memset(kc_stack[:].bitcast(F), 0.0).then_inc(sem("kc_zero"), 1)
                elif step == "k_zero":
                    if i == 0:
                        pool.wait_ge(sem("v"), nth_all("v", "ca"))
                    pool.memset(k_stack[1][:, 2 * i:2 * i + 2, :, :].bitcast(F), 0.0).then_inc(sem("k_zero"), 1)
                elif step == "ctx_rs":
                    pool.wait_ge(sem("half_ready"), 1)
                    pool.wait_ge(sem("ctx_ms"), 1)
                    pool.tensor_scalar(cmse[:], cms[:], EPS_RMS, None, ALU.add).then_inc(sem("ctx_ms_eps"), 1)
                    pool.wait_ge(sem("ctx_ms_eps"), 1)
                    pool.tensor_tensor(crs[:], cmse[:], half[:], ALU.pow).then_inc(sem("ctx_rs"), 1)
                elif step == "k_rest":
                    pool.wait_ge(sem("k_parts"), nth("k_parts", name, g))
                    part, x = paired(name, "k", 0, g, k_full[:, g, :])
                    pool.tensor_tensor(paired(name, "k", 0, g, k_rest[:, g, :])[1], x, part, ALU.subtract
                                       ).then_inc(sem("k_rest"), 1)
                elif step == "k_mid":
                    pool.wait_ge(sem("k_rest"), nth("k_rest", name, g))
                    pool.tensor_copy(*paired(name, "k", 1, g, k_rest[:, g, :])).then_inc(sem("k_mid"), 1)
                elif step == "k_low":
                    pool.wait_ge(sem("k_mid"), nth("k_mid", name, g))
                    part, x = paired(name, "k", 1, g, k_rest[:, g, :])
                    pool.tensor_tensor(paired(name, "k", 2, g, k_rest[:, g, :])[0], x, part, ALU.subtract
                                       ).then_inc(sem("k_low"), 1)
                elif step == "rstd":
                    pool.wait_ge(sem("half_ready"), 1)
                    pool.wait_ge(sem("var"), nth("var", name, g))
                    pool.tensor_scalar(vare[:, g, :], var[:, g, :], EPS, None, ALU.add).then_inc(sem("var_eps"), 1)
                    pool.wait_ge(sem("var_eps"), nth("rstd", name, g))
                    pool.tensor_tensor(rstd[:, g, :], vare[:, g, :], half[:, 0:NJ], ALU.pow
                                       ).then_inc(sem("rstd"), 1)


def constants():
    import numpy as np
    c = np.zeros((128, CST), np.float32)
    c[:, 0:128] = np.eye(128)
    c[0:64, 128:192] = np.eye(64)
    c[0:64, 192:256] = np.eye(64)
    later = np.triu(np.ones((64, 64)), 1) * -BIG
    c[0:64, 256:320] = later
    c[0:64, 320:384] = later.T
    for hl in range(2):
        for e in range(2):
            c[2 * hl + e, 384 + e] = 1 - 2 * hl
    c[:, 386] = np.arange(128)
    c[0:64, 387] = c[64:128, 388] = 1
    for p in range(4):
        for e in range(2):
            c[32 * p + 16 * e:32 * p + 16 * e + 16, CST - 8 + 2 * p + e] = 1
    return c


def kernel(**inp):
    import numpy as np
    import concourse.bacc as bacc
    from concourse.bass_utils import run_bass_kernel_spmd

    def arr(n):
        return np.asarray(inp[n])

    def by_feature(w):
        return w.reshape(w.shape[:-1] + (SP_, 2, DH)).swapaxes(-3, -2).swapaxes(-2, -1).reshape(w.shape)

    L0, L1, L2, L3 = "L0_xattn_", "L1_xattn_", "L2_xattn_", "L3_xattn_"
    sa_w, sa_b = arr(L0 + "sa_in_w"), arr(L0 + "sa_in_b")
    upd, tokw = arr(L1 + "W_upd"), arr(L1 + "W_token")
    f1, f2 = arr(L0 + "ffn_w1").T, arr(L0 + "ffn_w2")
    g1, g2 = arr(L2 + "W1").T, arr(L2 + "W2").T
    m = {
        "ident": np.eye(D, dtype=np.float32),
        "center": np.eye(D, dtype=np.float32) - np.float32(1 / D),
        "sa_q": by_feature(sa_w[0:D].T), "sa_k": by_feature(sa_w[D:2 * D].T), "sa_v": sa_w[2 * D:].T,
        "ca_q": by_feature(arr(L0 + "ca_q_w").T), "ca_k": by_feature(arr(L0 + "ca_k_w").T),
        "ca_v": arr(L0 + "ca_v_w").T,
        "l1_q": by_feature(arr(L1 + "W_state")), "l1_k": by_feature(tokw), "l1_v": tokw,
        "sa_o": arr(L0 + "sa_out_w"), "ca_o": arr(L0 + "ca_o_w"),
        "l1_updT": upd[D:].T, "l1_updsT": upd[:D].T, "l1_outT": arr(L1 + "W_out").T,
        "l2_q": by_feature(arr(L2 + "Wq").T), "l2_k": by_feature(arr(L2 + "Wk").T), "l2_v": arr(L2 + "Wv").T,
        "l3_q": by_feature(arr(L3 + "Wq").T), "l3_k": by_feature(arr(L3 + "Wk").T), "l3_v": arr(L3 + "Wv").T,
        "l3_o": arr(L3 + "Wo").T,
    }
    for c in range(F_CHUNKS):
        s = slice(c * D, (c + 1) * D)
        m[f"f_w1_{c}"], m[f"f_w2_{c}"] = f1[:, s], f2[:, s]
        m[f"g_w1_{c}"], m[f"g_w2_{c}"] = g1[:, s], g2[s, :]
    v = {
        "sa_qb": by_feature(sa_b[0:D]), "sa_kb": by_feature(sa_b[D:2 * D]), "sa_vb": sa_b[2 * D:],
        "ca_qb": by_feature(arr(L0 + "ca_q_b")), "ca_kb": by_feature(arr(L0 + "ca_k_b")),
        "l1_qb": by_feature(arr(L1 + "b_state")), "l1_kb": by_feature(arr(L1 + "b_token")),
        "l2_qb": by_feature(arr(L2 + "bq")), "l2_kb": by_feature(arr(L2 + "bk")),
        "sa_ob": arr(L0 + "sa_out_b"), "ca_vb": arr(L0 + "ca_v_b"), "ca_ob": arr(L0 + "ca_o_b"),
        "f_b2": arr(L0 + "ffn_b2"), "l1_tb": arr(L1 + "b_token"), "l1_ob": arr(L1 + "b_out"),
        "l1_ub": arr(L1 + "b_upd"), "l2_vb": arr(L2 + "bv"), "g_b2": arr(L2 + "b2"),
        "sa_lg": arr(L0 + "ln1_g"), "sa_lb": arr(L0 + "ln1_b"), "ca_lg": arr(L0 + "ln2_g"), "ca_lb": arr(L0 + "ln2_b"),
        "f_lg": arr(L0 + "ln3_g"), "f_lb": arr(L0 + "ln3_b"), "l1_lg": arr(L1 + "ln_gamma"),
        "l1_lb": arr(L1 + "ln_beta"), "l2_lg": arr(L2 + "ln_g"), "l2_lb": arr(L2 + "ln_b"),
        "l3_gq": arr(L3 + "gamma_q"), "l3_gk": arr(L3 + "gamma_kv"),
    }
    for c in range(F_CHUNKS):
        v[f"f_b1_{c}"] = arr(L0 + "ffn_b1")[c * D:(c + 1) * D]
        v[f"g_b1_{c}"] = arr(L2 + "b1")[c * D:(c + 1) * D]
    arrays = {
        "xT": arr("x").reshape(TOK, D).T,
        "ctxT": arr("ctx_1024").reshape(TOK, D).T,
        "ctx": arr("ctx_1024").reshape(TOK, D),
        "idx": arr("itok_BxS_0_255").reshape(1, TOK),
        "key_mask": arr("mask_BxS2_bf1").reshape(1, TOK).view(np.uint8),
        "mats": np.stack([m[n] for n in MATS], axis=1),
        "cols": np.stack([v[n] for n in COLS], axis=1),
        "consts": constants(),
    }
    arrays = {n: np.ascontiguousarray(x) for n, x in arrays.items()}
    nc = bacc.Bacc("TRN2", target_bir_lowering=False, num_devices=1)
    a = {n: nc.dram_tensor(f"in_{n}", x.shape, mybir.dt.from_np(x.dtype), kind="ExternalInput").ap()
         for n, x in arrays.items()}
    out = nc.dram_tensor("out", (TOK, D), mybir.dt.float32, kind="ExternalOutput").ap()
    build(nc, a, out)
    r = run_bass_kernel_spmd(nc, [{f"in_{n}": x for n, x in arrays.items()}], core_ids=[0])
    return r.results[0]["out"].reshape(B, T, D)
```

```python
import concourse.bass as bass
from concourse import mybir
from contextlib import ExitStack

B, T, D, H, DH = 16, 64, 128, 16, 8
TOK = B * T
G = 4
GB = B // G
GT = GB * T
NJ = GT // 128
SP_ = H // 2
TERMS = 6
Q_PART = (0, 0, 0, 1, 1, 2)
K_PART = (0, 1, 2, 0, 1, 0)
R_TERMS = TERMS * 16
R_MASK = R_TERMS + 2
R_ALL = R_MASK + 4
STRIDE = 4
K16 = T // STRIDE
F_CHUNKS = 4
EPS = 1e-5
EPS_RMS = 1.1920929e-07
EPS_DEN = 1e-6
SCALE = DH ** -0.5
BIG = 1e30
KEY_BIG = 3e38
CST = 397

MATS = ["ident", "center", "sa_q", "sa_k", "sa_v",
        "ca_q", "ca_k", "ca_v", "l1_q", "l1_k", "l1_v", "sa_o", "ca_o", "l1_updT", "l1_updsT", "l1_outT",
        "l2_q", "l2_k", "l2_v", "l3_q", "l3_k", "l3_v", "l3_o",
        "f_w1_0", "f_w1_1", "f_w1_2", "f_w1_3", "f_w2_0", "f_w2_1", "f_w2_2", "f_w2_3",
        "g_w1_0", "g_w1_1", "g_w1_2", "g_w1_3", "g_w2_0", "g_w2_1", "g_w2_2", "g_w2_3"]
FIRST_MATS, NEXT_MATS = 5, 23
COLS = ["sa_qb", "sa_kb", "ca_qb", "ca_kb", "l1_qb", "l1_kb", "l2_qb", "l2_kb",
        "sa_vb", "sa_ob", "ca_vb", "ca_ob", "f_b2", "l1_tb", "l1_ob", "l1_ub", "l2_vb", "g_b2",
        "sa_lg", "sa_lb", "ca_lg", "ca_lb", "f_lg", "f_lb", "l1_lg", "l1_lb", "l2_lg", "l2_lb",
        "l3_gq", "l3_gk", "f_b1_0", "f_b1_1", "f_b1_2", "f_b1_3", "g_b1_0", "g_b1_1", "g_b1_2", "g_b1_3"]
ATT = ["sa", "ca", "l1", "l2", "l3"]
S_UNITS = {"sa": NJ * 2, "ca": 1, "l1": NJ * 2, "l2": NJ * 2, "l3": 0}
T_UNITS = {"sa": GB, "ca": 1, "l1": GB, "l2": GB, "l3": GB}
P_SLOTS = 4
POOL_STACKS = ('ca',)
STACK = {"sa": 0, "l1": 1, "l2": 0, "l3": 1}
V_BASE = {"sa": 0, "ca": 1, "l1": 0, "l2": 2, "l3": 0}
VALUES = {"sa": 0, "ca": 1, "l1": 0, "l2": 1, "l3": 0}
V_BEFORE = {"l1": "sa", "l3": "l1"}
WC_OF = {"sa": 0, "ca": 1, "l1_upd": 2, "l1_res": 3, "f": 4, "l1": 8}
ROW_OF = {"sa": 0, "ca": 1, "f": 2, "l1": 3, "l2": 4}
X_OF = {"x0": 0, "x1": 1, "x2": 0, "x3": 1, "x4": 0, "x5": 1, "x6": 0}
X_FROM = {"x1": "sa", "x2": "ca", "x3": "f", "x4": "l1", "x5": "l2"}
X_IN = {"sa": "x0", "ca": "x1", "f": "x2", "l1": "x3", "l2": "x4", "g": "x5", "l3": "x6"}
X_OUT = {"sa": "x1", "ca": "x2", "f": "x3", "l1": "x4", "l2": "x5"}

OWN = {"q": ["q_parts"], "m": ["m_row"], "av": ["divide"], "flip": ["attT"], "z": ["scale"], "flip_x": ["ln"],
       "h": ["gelu"], "y": ["x6"], "ms": ["floor"], "out": ["fin"]}
TURNS = {"s": ["max"], "k": ["k_parts"], "v": ["v_even", "v_odd"], "ctx_rows": ["ctx_normed"],
         "weights": ["weights_kept"]}


def timetable():
    jobs, tail = {}, {}

    def add(engine, cost, step, name="", g=0, i=0, after=()):
        after = [k + (0,) * (4 - len(k)) for k in after]
        jobs[step, name, g, i] = (engine, cost * SLOW if engine == "pe" else cost, after)
        return (step, name, g, i)

    groups = range(G)
    for n, (name, t) in enumerate((("x", 4), ("w1", 4.5), ("cols", 5), ("consts", 6), ("ctx", 9), ("w2", 14), ("w3", 18),
                                   ("rest", 19))):
        add(f"load{n}", t, "load", name)

    def load(name):
        return ("load", name, 0, 0)

    w0 = add("pe", 2.6, "weights", i=0, after=[load("w2")])
    w0k = add("dve", .6, "weights_kept", i=0, after=[w0])
    w1 = add("pe", 2.0, "weights", i=1, after=[load("w3")])
    add("dve", .6, "weights_kept", i=1, after=[w1])
    w2 = add("pe", .8, "weights", i=2, after=[w0k, load("w3")])
    w2k = add("dve", .3, "weights_kept", i=2, after=[w2])
    w3 = add("pe", 3., "weights", i=3, after=[w2k])
    w3 = add("dve", .7, "weights_kept", i=3, after=[w3])
    w3 = add("pe", .3, "weights", i=4, after=[w3])
    add("dve", .7, "weights_kept", i=4, after=[w3])
    z0 = [add("dve", 4.4, "k_zero_first", i=0), add("pool", 4.4, "k_zero_first", i=1)]
    constants_ready = add("dve", 1.6, "constants", after=[load("consts")])
    ck = add("dve", .5, "ca_k_split", after=[load("w2")])
    add("pool", 2.4, "v_base", i=0, after=[load("consts")])
    add("pool", .6, "v_base", i=1, after=[load("consts")])
    rep = add("act", 4., "ctx_rep", after=[load("ctx")])
    kcz = add("pool", 1.8, "kc_zero")
    add("pool", 2.1, "kc_rows", after=[kcz, constants_ready])
    add("pool", 2.1, "k_rows", i=0, after=[constants_ready] + z0)
    zs = []
    for i in range(4):
        zs.append(add("pool", 1.8, "k_zero", i=i, after=[("v_even", "ca", g) for g in groups] + zs[-1:]))
    add("pool", 1.1, "k_rows", i=1, after=[zs[-1]])
    add("dve", .9, "key_mask", after=[load("rest")])
    add("sp", 1.3, "km_stack", after=[("key_mask", ""), zs[-1]])
    band = add("dve", 3.3, "band", after=[load("rest")])
    add("dve", 1., "gammas", after=[load("w3")])
    cms = add("act", 2., "ctx_ms", after=[load("rest")])
    crs = add("pool", 1.9, "ctx_rs", after=[cms])
    ctx_scaled = add("dve", 1.2, "ctx_scale", after=[crs])
    add("pool", 2.8, "v_base", i=2, after=[("av", "ca", g) for g in groups])

    def keys_of(name, k_free, v_free):
        prev = {"l1": "sa", "l2": "l1", "l3": "l2"}.get(name)
        lows = []
        if name == "ca":
            k = add("pe", 1.7, "k", name, after=[load("ctx"), ck, ("k_low", "sa", 0)])
            for e, cost, step in (("act", .75, "k_parts"), ("dve", .35, "k_rest"), ("dve", .35, "k_mid"),
                                  ("dve", .35, "k_low")):
                k = add(e, cost, step, name, after=[k])
            lows = [k]
        for g in groups if name != "ca" else ():
            after = [load("w1"), load("x")] if name == "sa" else [load("w2"), load("ctx")]
            if name != "sa":
                after += [("k_stack", prev, 0, t) for t in range(TERMS)]
                after += [("k_low", "ca", 0) if name == "l1" else ("k_low", prev, g)]
            if name == "l3":
                after += [("ctx_normed", "", g), ("z", "f", g), ("gammas", "")]
            k = add("pe", .45, "k", name, g, after=after)
            k = add("act", .75, "k_parts", name, g, after=[k])
            k = add("dve", .35, "k_rest", name, g, after=[k] + (z0[:1] if name == "sa" else []))
            k = add("dve", .2, "k_mid", name, g, after=[k])
            lows.append(add("dve", .35, "k_low", name, g, after=[k]))
        for t in range(TERMS):
            engine, cost = ("pool", 2.) if name in POOL_STACKS else ("sp", 1.3)
            add(engine, cost, "k_stack", name, 0, t, after=lows + k_free)
        for g in groups:
            after = [load("w1"), load("x")] if name == "sa" else [load("w2"), load("ctx")]
            if name == "l3":
                after += [("ctx_normed", "", g)]
            if name == "ca":
                after += [rep]
            v = add("pe", .85 if name == "ca" else .45, "v", name, g,
                    after=after + v_free + [("v_base", "", 0, V_BASE[name])])
            add("dve", .6 if name == "ca" else .42, "v_even", name, g, after=[v])
            if name != "ca":
                add("act", .35, "v_odd", name, g, after=[v])

    keys_of("sa", z0, [])
    keys_of("ca", [kcz], [])
    keys_of("l1", [zs[-1]], [("av", "sa", g, GB - 1) for g in groups])
    keys_of("l2", [("t", "sa", g, GB - 1) for g in groups], [("av", "ca", g) for g in groups])
    for g in groups:
        k = add("pe", .25, "ctx_rows", "", g, 
                after=[ctx_scaled, ("k", "ca", 0)] + [(x, name, g) for x in ("k", "v") for name in ("l1", "l2")])
        add("act", .3, "ctx_normed", "", g, after=[k])
    keys_of("l3", [("t", "l1", g, GB - 1) for g in groups], [("av", "l1", g, GB - 1) for g in groups])

    for g in groups:
        k = load("x")

        def attention(name, k):
            k = add("pe", .45, "q", name, g, after=[k, load("w2" if name != "sa" else "w1")])
            q_parts = k = add("act", .75, "q_parts", name, g, after=[k])
            k = add("dve", .35, "q_rest", name, g, after=[k])
            k = add("dve", .2, "q_mid", name, g, after=[k])
            k = add("dve", .35, "q_low", name, g, after=[k])
            k = add("sp", 4., "q_stack", name, g, after=[k])
            stacked = [k] + [("k_stack", name, 0, t) for t in range(TERMS)]
            k_rows = {"sa": ("k_rows", "", 0, 0), "l1": ("k_rows", "", 0, 1), "ca": ("kc_rows", "")}
            if name == "l1":
                stacked.append(("km_stack", ""))
            if name == "l3":
                stacked.append(band)
                sq = add("act", .35, "x_sq", name, g, after=[("x6", "g", g)])
                ms = add("pe", .2, "ms", name, g, after=[sq, q_parts])
                floored = [add("dve", .2, "floor", name, g, after=[ms])]
            else:
                floored, maxes = [], []
                for i in range(S_UNITS[name]):
                    s = add("pe", {"ca": 1.6, "l2": .75}.get(name, .5), "s", name, g, i, after=stacked)
                    maxes.append(add("dve", .65, "max", name, g, i, after=[s]))
                k = add("dve", .3, "max_parts", name, g, after=maxes)
                k = add("pe", .2, "m", name, g, after=[k])
                k = add("act", .2, "m_row", name, g, after=[k])
                stacked = [add("sp", .7, "m_stack", name, g, after=[k])] + ([k_rows[name]] if name in k_rows else [])
            avs = []
            for i in range(T_UNITS[name]):
                t = add("pe", {"ca": 1.3, "l2": .6, "l3": .6}.get(name, .4), "t", name, g, i, after=stacked)
                p = add("act", .5, "exp", name, g, i, after=[t] + ([band, cms] if name == "sa" else []))
                if name == "l3":
                    p = add("dve", .6, "square", name, g, i, after=[p])
                avs.append(add("pe", .82, "av", name, g, i, after=[p, ("v_even", name, g)]
                               + ([("v_odd", name, g)] if name != "ca" else []) + (avs[-1:] or floored)))
            k = add("dve", .6, "divide", name, g, after=avs)
            k = add("pe", .25, "flip", name, g, after=[k])
            return add("act", .3, "attT", name, g, after=[k])

        def norm(name, k):
            k = add("pe", 2.2 if name == "f" else .95, "z", name, g,
                    after=[k, ("weights_kept", "", 0, 1), ("weights_kept", "", 0, 4)])
            k = add("act", .4, "var", name, g, after=[k])
            k = add("pool", .8, "rstd", name, g, after=[k])
            k = add("dve", .35, "scale", name, g, after=[k])
            k = add("pe", .25, "flip_x", name, g, after=[k])
            return add("act", .5, "ln", name, g, after=[k] + ([("k", "ca", 0)] if name == "sa" else []))

        def hidden(name, k):
            for i in range(2):
                h = add("pe", .9, "h", name, g, i, after=[k])
                k = add("act", .8, "gelu", name, g, i, after=[h] + (
                    [("k_low", "l2", gg) for gg in groups] + [("ctx_normed", "", gg) for gg in groups]
                    + [("kc_rows", ""), ("k_rows", "", 0, 1)] if name == "f" else [("k_low", "l3", g)]))
            return k

        k = norm("sa", attention("sa", k))
        k = norm("ca", attention("ca", k))
        k = norm("f", hidden("f", k))
        k = norm("l1", attention("l1", k))
        k = norm("l2", attention("l2", k))
        k = hidden("g", k)
        k = add("pe", 1.8, "y", "g", g, after=[k])
        k = add("dve", .4, "x6", "g", g, after=[k])
        k = attention("l3", k)
        k = add("pe", 1.1, "out", "", g, after=[k])
        k = add("act", .3, "fin", "", g, after=[k])
        add("sp", .7, "store", "", g, after=[k])

    users = {}
    for k, (_, _, after) in jobs.items():
        for x in after:
            users.setdefault(x, []).append(k)

    def way(k):
        if k not in tail:
            tail[k] = jobs[k][1] + HOP + max([way(u) for u in users.get(k, [])], default=0)
        return tail[k]

    end, free, order, turns, ts, table = {}, {}, [], [], [], "exp"
    waiting = set(jobs)
    ready = {k for k in waiting if not jobs[k][2]}
    while waiting:
        best = None
        for k in ready:
            step, name, g, i = k
            engine, cost, after = jobs[k]
            need = list(after)
            if step in TURNS and len(turns) >= 2:
                need += [(r,) + turns[-2][1:] for r in TURNS[turns[-2][0]] if (r,) + turns[-2][1:] in jobs]
            if step == "t" and len(ts) >= 2:
                need.append(("exp",) + ts[-2][1:])
            if step == ("square" if name == "l3" else "exp"):
                u = ts.index(("t",) + k[1:])
                if u >= P_SLOTS:
                    need.append(("av",) + ts[u - P_SLOTS][1:])
            if step == "exp":
                same = [x for x in ts if x[1] == "l3"]
                u = same.index(("t",) + k[1:]) if name == "l3" else 0
                if u >= 2:
                    need.append(("square",) + same[u - 2][1:])
            if any(x not in end for x in need):
                continue
            start = max([free.get(engine, 0)] + [end[x] for x in need])
            kind = {"exp": "relu" if name == "l3" else "exp", "gelu": "gelu"}.get(step)
            if kind in ("exp", "gelu") and kind != table:
                start += TABLE_LOAD
            urgency = way(k) - LEAD * g + AHEAD.get(step, 0) + AHEAD.get(f"{step} {name}", 0)
            rank = (start - WORTH * urgency, -urgency, k)
            if best is None or rank < best_rank:
                best, best_rank = (start, k), rank
        start, k = best
        engine, cost, _ = jobs[k]
        free[engine] = start + cost
        if k[0] == "gelu" or k[0] == "exp" and k[1] != "l3":
            table = k[0]
        end[k] = start + cost + (DMA_HOP if engine == "sp" or k[0] in ("k_stack", "k_rows", "kc_rows") else HOP)
        order.append(k)
        waiting.remove(k)
        ready.remove(k)
        ready |= {u for u in users.get(k, []) if u in waiting and all(x in end for x in jobs[u][2])}
        if k[0] in TURNS:
            turns.append(k)
        if k[0] == "t":
            ts.append(k)
    return order


HOP, DMA_HOP = 0.2, 2.0
LEAD = 5.0
TABLE_LOAD = 1.5
WORTH = 0.01
SLOW = 0.9
AHEAD = {"ln": 10, "flip_x": 30, "weights_kept": 30, "m_row": 4, "q_stack sa": -30, "t ca": -10, "attT": -30,
         "h": 4, "divide": -10}
ORDER = timetable()
SEEN, NTH = {}, {}
for k_ in ORDER:
    SEEN[k_[0]] = NTH[k_] = SEEN.get(k_[0], 0) + 1
TURN = [k_ for k_ in ORDER if k_[0] in TURNS]
T_ORDER = [k_ for k_ in ORDER if k_[0] == "t"]
L3_ORDER = [k_ for k_ in T_ORDER if k_[1] == "l3"]


def nth(step, name="", g=0, i=0):
    return NTH[step, name, g, i]


def nth_all(step, name=""):
    return max(n for k, n in NTH.items() if k[:2] == (step, name))


def nth_of_layer(step, name, g, i=0):
    return sum(k[:2] == (step, name) and n <= NTH[step, name, g, i] for k, n in NTH.items())


def readers(key):
    return [(r, NTH[(r,) + key[1:]]) for r in {**OWN, **TURNS}[key[0]] if (r,) + key[1:] in NTH]


def own_before(step, name, g, i=0):
    mine = [k for k in ORDER if k[0] in OWN and k[2] == g and not (k[0] == "av" and k[3])]
    n = mine.index((step, name, g, i))
    if not n:
        return []
    k = mine[n - 1]
    return readers(k) if k[0] != "av" else [("divide", NTH["divide", k[1], g, 0])]


def turn(step, name, g, i=0):
    n = TURN.index((step, name, g, i))
    return n % 2, (readers(TURN[n - 2]) if n >= 2 else [])


def build(nc, a, out):
    F, BF = mybir.dt.float32, mybir.dt.bfloat16
    ALU, ACT, AX = mybir.AluOpType, mybir.ActivationFunctionType, mybir.AxisListType
    ctx = ExitStack()
    with ctx:
        def sb(name, shape, dt=F):
            return ctx.enter_context(nc.sbuf_tensor(f"{name}_sb", shape, dt))

        sems = {}

        def sem(name):
            if name not in sems:
                sems[name] = ctx.enter_context(nc.semaphore(name))
            return sems[name]

        W = sb("W", [128, len(MATS), 128])
        V = sb("V", [128, len(COLS)])

        def mat(n):
            return W[:, MATS.index(n), :]

        def col(n):
            return V[:, COLS.index(n):COLS.index(n) + 1]

        x_buf = [sb("xa", [128, TOK]), sb("xb", [128, TOK])]
        ctxT = sb("ctxT", [128, TOK])
        hid = sb("hid", [128, F_CHUNKS, TOK])
        k_full = hid[:, 0, :].rearrange("p (g n) -> p g n", g=G)
        k_rest = hid[:, 1, :].rearrange("p (g n) -> p g n", g=G)
        k_ones = hid[0:4, 2, :].bitcast(BF).rearrange("p (e n) -> p e n", e=2)
        cn = hid[:, 3, :].rearrange("p (n d) -> p n d", d=128)
        q_full = sb("q_full", [128, G, GT])
        q_rest = sb("q_rest", [128, G, GT])
        q_part = sb("q_part", [128, 3, G, GT], BF)
        kc_part = sb("kc_part", [128, 3, B * K16], BF)
        k_part = sb("k_part", [128, 3, TOK], BF)
        attT = q_full
        att = q_rest[:, :, :].rearrange("p g (j d) -> p g j d", j=NJ)
        fin = q_full
        q_stack = sb("q_stack", [128, G, SP_, GT], BF)
        k_stack = [sb(f"k_stack{i}", [128, SP_, 2, TOK], BF) for i in range(2)]
        kc_stack = sb("kc_stack", [128, SP_, 2, K16 * B], BF)
        ctx_rep = (k_stack[1][:, :, :, :].rearrange("p s e n -> p (s e n)").bitcast(F)[:, 0:4 * TOK]
                   .rearrange("p (b c a e k) -> p b c a e k", b=B, c=2, a=4, e=2))
        v_ext = [sb(f"v_ext{i}", [128, B, SP_, 2, DH + 1]) for i in range(2)]
        probs = sb("probs", [128, P_SLOTS, SP_ * T])
        ctx_sq = probs[:, 2:4, :].rearrange("p a n -> p (a n)")
        ca_k_split = x_buf[1][:, 0:STRIDE * 128].rearrange("p (r n) -> p r n", r=STRIDE)
        relu = sb("relu", [128, 2, SP_ * T])
        idx = relu[0:64, :, :].bitcast(mybir.dt.int32).rearrange("p a n -> p (a n)")
        dist = probs[0:64, 0:2, :].rearrange("p a n -> p (a n)")
        m_col = sb("m_col", [128, G, NJ, SP_, 2])
        m_part = sb("m_part", [128, G, NJ, 2, 2, SP_], BF)
        m_row = sb("m_row", [32, G, GT], BF)
        rden = sb("rden", [128, G, NJ, H])
        var = sb("var", [128, G, NJ])
        vare = sb("vare", [128, G, NJ])
        rstd = sb("rstd", [128, G, NJ])
        half = sb("half", [128, 8])
        WC = sb("WC", [128, 9, 128])
        rows = sb("rows", [3, 5 * 128], BF)
        row_part = sb("row_part", [128, 3, 5], BF)
        row_rest = sb("row_rest", [128, 5])
        ones_row = sb("ones_row", [3, 128], BF)
        ones_col = sb("ones_col", [128, 1])
        identb = sb("identb", [128, 128], BF)
        cst = sb("cst", [128, CST])
        two_i = sb("two_i", [64, 128], BF)
        causal = sb("causal", [64, 2, 64], BF)
        e_mask = cst[:, CST - 8:CST]
        q_ones = sb("q_ones", [2, GT], BF)
        km_u8 = sb("km_u8", [1, TOK], mybir.dt.uint8)
        km = sb("km", [1, TOK], BF)
        band = sb("band", [64, TOK], BF)
        cms = sb("cms", [128, B // 2])
        cmse = sb("cmse", [128, B // 2])
        crs = sb("crs", [128, B // 2])
        floor = sb("floor", [128, G, NJ])
        bank = [ctx.enter_context(nc.psum_tensor(f"bank{g}", [128, 512], F)) for g in range(G)]
        s_bank = [ctx.enter_context(nc.psum_tensor(f"s_bank{i}", [128, 512], F)) for i in range(2)]
        t_bank = [ctx.enter_context(nc.psum_tensor(f"t_bank{i}", [128, 512], F)) for i in range(2)]

        def X(x):
            return x_buf[X_OF[x]]

        def tok(g):
            return slice(g * GT, (g + 1) * GT)

        def keys(stack, rows_, s, b):
            return stack[0:rows_, s, :, :].rearrange("p e n -> p (e n)").rearrange("p (x b) -> p x b", b=B)[:, :, b]

        def stacked_k(eng, name):
            n = TERMS * 2 + (2 if name == "l1" else 0)
            eng.wait_ge(sem(f"{name}_k_stacked"), 16 * n)

        def paired(name, side, t, g, x):
            if side == "q":
                return q_part[:, t, g, :], x
            if name == "ca":
                return kc_part[:, t, :], x
            return (k_part[:, t, :].rearrange("p (k b) -> p b k", b=B)[:, g * GB:(g + 1) * GB],
                    x.rearrange("p (b k) -> p b k", b=GB))
        def k_stack_term(dma, name, t):
            dma.wait_ge(sem("k_low"), nth_all("k_low", name))
            if name == "ca":
                ks, part = kc_stack, kc_part
                dma.wait_ge(sem("kc_zero"), nth("kc_zero"))
            elif STACK[name]:
                ks, part = k_stack[1], k_part
                dma.wait_ge(sem("k_zero"), nth_all("k_zero"))
            else:
                ks, part = k_stack[0], k_part
                dma.wait_ge(sem("k_zero_first"), 2)
            if name in ("l2", "l3"):
                dma.wait_ge(sem("t"), nth_all("t", {"l2": "sa", "l3": "l1"}[name]))
            for e in range(2):
                r = 16 * t + 8 * e
                dma.dma_start(ks[r:r + 8, :, e, :], part[64 * e:64 * e + 64, K_PART[t], :]
                             ).then_inc(sem(f"{name}_k_stacked"), 16)

        block = ctx.enter_context(nc.Block())

        @block.sync
        def _(sp):
            sp.dma_start(x_buf[0][:, tok(0)], a["xT"][:, tok(0)]).then_inc(sem("x_first"), 16)
            sp.dma_start(W[:, 0:FIRST_MATS, :], a["mats"][:, 0:FIRST_MATS, :]).then_inc(sem("w1_loaded"), 16)
            sp.dma_start(V[:], a["cols"]).then_inc(sem("v_loaded"), 16)
            sp.dma_start(x_buf[0][:, GT:TOK], a["xT"][:, GT:TOK]).then_inc(sem("x_loaded"), 16)
            sp.dma_start(cst[:], a["consts"]).then_inc(sem("cst_loaded"), 16)
            sp.dma_start(ctxT[:], a["ctxT"]).then_inc(sem("ctx_loaded"), 16)
            sp.dma_start(W[:, FIRST_MATS:NEXT_MATS, :], a["mats"][:, FIRST_MATS:NEXT_MATS, :]
                         ).then_inc(sem("w2_loaded"), 16)
            sp.dma_start(W[:, NEXT_MATS:, :], a["mats"][:, NEXT_MATS:, :]).then_inc(sem("w3_loaded"), 16)
            sp.dma_start(cn, a["ctx"].rearrange("(n p) d -> p n d", p=128)).then_inc(sem("cn_loaded"), 16)
            sp.dma_start(idx, a["idx"].to_broadcast([64, TOK])).then_inc(sem("idx_loaded"), 16)
            sp.dma_start(km_u8[:], a["key_mask"]).then_inc(sem("km_loaded"), 16)

            def km_stack():
                sp.wait_ge(sem("key_mask"), nth("key_mask"))
                sp.wait_ge(sem("k_zero"), nth_all("k_zero"))
                for e in range(2):
                    sp.dma_start(k_stack[1][R_TERMS + e:R_TERMS + e + 1, :, e, :],
                                 km[:].unsqueeze(1).to_broadcast([1, SP_, TOK])).then_inc(sem("l1_k_stacked"), 16)

            def q_to_stack(name, g):
                sp.wait_ge(sem("q_low"), nth("q_low", name, g))
                if name != "sa":
                    before = ATT[ATT.index(name) - 1]
                    sp.wait_ge(sem("t"), nth("t", before, g, T_UNITS[before] - 1))
                for t in range(TERMS):
                    sp.dma_start(q_stack[16 * t:16 * t + 16, g, :, :], q_part[:, Q_PART[t], g, :]
                                 ).then_inc(sem(f"q_stacked{g}"), 16)

            for step, name, g, i in ORDER:
                if step == "k_stack" and name not in POOL_STACKS:
                    k_stack_term(sp, name, i)
                elif step == "km_stack":
                    km_stack()
                elif step == "q_stack":
                    q_to_stack(name, g)
                elif step == "m_stack":
                    sp.wait_ge(sem("m_row"), nth("m_row", name, g))
                    sp.dma_start(q_stack[R_MASK:R_ALL, g, :, :], m_row[:, g, :]).then_inc(sem(f"m_stacked{g}"), 16)
                elif step == "store":
                    sp.wait_ge(sem("fin"), nth("fin", "", g))
                    sp.dma_start(out[g * GT:(g + 1) * GT, :].rearrange("(j p) d -> p j d", p=128),
                                 fin[:, g, :].rearrange("p (j d) -> p j d", j=NJ)).then_inc(sem("stored"), 16)
            sp.wait_ge(sem("stored"), 16 * G)

        @block.tensor
        def _(pe):
            def take(step, name, g, i=0):
                for reader, n in own_before(step, name, g, i):
                    pe.wait_ge(sem(reader), n)
                return bank[g]

            def take_turn(step, name, g, i=0):
                which, before = turn(step, name, g, i)
                for reader, n in before:
                    pe.wait_ge(sem(reader), n)
                return s_bank[which]

            def mm(o, l, r, start=True, stop=True):
                return pe.matmul(o, l, r, start=start, stop=stop)

            def x_ready(name, g):
                x = X_IN[name]
                if x == "x0":
                    pe.wait_ge(sem("x_loaded" if g else "x_first"), 16)
                elif x == "x6":
                    pe.wait_ge(sem("x6"), nth("x6", "g", g))
                else:
                    pe.wait_ge(sem("ln"), nth("ln", X_FROM[x], g))

            def weights(i):
                o = take_turn("weights", "", 0, i)
                if i == 0:
                    pe.wait_ge(sem("w1_loaded"), 16)
                    pe.wait_ge(sem("w2_loaded"), 16)
                    for c, n in enumerate(["sa_o", "ca_o", "l1_updT"]):
                        mm(o[:, c * 128:(c + 1) * 128], mat(n), mat("center"))
                    mm(o[:, 384:512], mat("l1_updsT"), mat("center"), stop=False)
                    last = mm(o[:, 384:512], mat("ident"), mat("center"), start=False)
                elif i == 1:
                    pe.wait_ge(sem("w3_loaded"), 16)
                    for c in range(F_CHUNKS):
                        last = mm(o[:, c * 128:(c + 1) * 128], mat(f"f_w2_{c}"), mat("center"))
                elif i == 2:
                    pe.wait_ge(sem("weights_kept"), nth("weights_kept", i=0))
                    pe.wait_ge(sem("v_loaded"), 16)
                    last = mm(o[:, 0:128], mat("l1_outT"), WC[:, WC_OF["l1_upd"], :])
                elif i == 3:
                    pe.wait_ge(sem("weights_kept"), nth("weights_kept", i=2))
                    for name, terms in (("sa", [("sa_vb", WC[:, 0, :]), ("sa_ob", mat("center"))]),
                                        ("ca", [("ca_vb", WC[:, 1, :]), ("ca_ob", mat("center"))]),
                                        ("f", [("f_b2", mat("center"))]),
                                        ("l1", [("l1_tb", WC[:, 8, :]), ("l1_ob", WC[:, WC_OF["l1_upd"], :]),
                                                ("l1_ub", mat("center"))]),
                                        ("l2", [("l2_vb", mat("center"))])):
                        c = ROW_OF[name]
                        for n, (b, m) in enumerate(terms):
                            last = mm(o[:, c:c + 1], m, col(b), start=n == 0, stop=n == len(terms) - 1)
                else:
                    pe.wait_ge(sem("weights_kept"), nth("weights_kept", i=3))
                    for c in range(5):
                        last = pe.transpose(o[0:3, 0:320].bitcast(BF)[:, c * 128:(c + 1) * 128],
                                            row_part[:, :, c], identb[:, :])
                last.then_inc(sem("weights"), 1)

            def keys_of(name, g):
                o = take_turn("k", name, g)
                pe.wait_ge(sem("w1_loaded" if name == "sa" else "w2_loaded"), 16)
                pe.wait_ge(sem("ctx_loaded" if name != "sa" else "x_loaded" if g else "x_first"), 16)
                if name == "ca":
                    pe.wait_ge(sem("ca_k_split"), 1)
                    for r in range(STRIDE):
                        last = mm(o[:, 0:B * K16].rearrange("p (k b) -> p k b", b=B), ca_k_split[:, r, :],
                                  ctxT[:].rearrange("p (b k r) -> p k b r", b=B, r=STRIDE)[:, :, :, r],
                                  start=r == 0, stop=r == STRIDE - 1)
                    last.then_inc(sem("k"), 1)
                    return
                if name == "l3":
                    pe.wait_ge(sem("ctx_normed"), nth("ctx_normed", g=g))
                    pe.wait_ge(sem("gammas"), 1)
                mm(o[:, 0:GT], mat(f"{name}_k"), (x_buf[0] if name == "sa" else ctxT)[:, tok(g)]
                   ).then_inc(sem("k"), 1)

            def values(name, g):
                o = take_turn("v", name, g)
                src = x_buf[0] if name == "sa" else ctxT
                pe.wait_ge(sem("w1_loaded" if name == "sa" else "w2_loaded"), 16)
                pe.wait_ge(sem("ctx_loaded" if name != "sa" else "x_loaded" if g else "x_first"), 16)
                if name == "l3":
                    pe.wait_ge(sem("ctx_normed"), nth("ctx_normed", g=g))
                    pe.wait_ge(sem("gammas"), 1)
                for j in range(NJ):
                    t = g * GT + j * 128
                    last = mm(o[:, j * 128:(j + 1) * 128], src[:, t:t + 128], mat(f"{name}_v"))
                last.then_inc(sem("v"), 1)

            def values_ca(g):
                o = take_turn("v", "ca", g)
                pe.wait_ge(sem("w2_loaded"), 16)
                pe.wait_ge(sem("ctx_rep"), 1)
                for i in range(GB):
                    b = g * GB + i
                    for pi in range(2):
                        rows_ = ctx_rep[:, b, pi, :, :, :].rearrange("p a e k -> p (a e k)")
                        w = mat("ca_v").rearrange("p (a c n) -> p a c n", a=4, c=2)[:, :, pi, :]
                        c = (i * 2 + pi) * 64
                        last = mm(o[:, c:c + 64].rearrange("p (a n) -> p a n", a=4), rows_, w)
                last.then_inc(sem("v"), 1)

            def scores(name, g, i):
                o = take_turn("s", name, g, i)
                if i == 0:
                    pe.wait_ge(sem(f"q_stacked{g}"), 16 * TERMS * (ATT.index(name) + 1))
                    stacked_k(pe, name)
                if name == "ca":
                    for ii in range(GB):
                        b, c = g * GB + ii, 64 * (ii % 2)
                        for s in range(SP_):
                            k = (ii // 2) * 256 + s * 32
                            last = mm(o[c:c + 64, k:k + 32], q_stack[0:R_TERMS, g, s, ii * T:(ii + 1) * T],
                                      keys(kc_stack, R_TERMS, s, b))
                    last.then_inc(sem("s"), 1)
                    return
                if name == "l1" and i == 0:
                    pe.wait_ge(sem("q_ones_stacked"), 16)
                r = R_MASK if name == "l1" else R_TERMS
                j, hf = i // 2, i % 2
                if name == "l2":
                    pe.wait_ge(sem("const_ready"), 5)
                    mm(o[:, :].rearrange("p (c k) -> p c k", c=8), two_i[:, :],
                       causal[:, 0, :].unsqueeze(1).to_broadcast([64, 8, 64]))
                for c in range(2):
                    t = (2 * j + c) * T
                    b = g * GB + 2 * j + c
                    for s4 in range(4):
                        s = 4 * hf + s4
                        last = pe.matmul(o[64 * c:64 * c + 64, s4 * 128:(s4 + 1) * 128],
                                         q_stack[0:r, g, s, t:t + T],
                                         keys(k_stack[STACK[name]], r, s, b),
                                         start=name != "l2", stop=True, skip_group_check=name == "l2")
                last.then_inc(sem("s"), 1)

            def max_rows(name, g):
                o = take("m", name, g)[0:32, 0:GT // 2].bitcast(BF)
                pe.wait_ge(sem("max_parts"), nth("max_parts", name, g))
                pe.wait_ge(sem("const_ready"), 5)
                for j in range(NJ):
                    last = pe.transpose(o[:, j * 128:(j + 1) * 128],
                                        m_part[:, g, j, :, :, :].rearrange("p a e s -> p (a e s)"), identb[:, :])
                last.then_inc(sem("m"), 1)

            def scores_t(name, g, i):
                u = T_ORDER.index(("t", name, g, i))
                if i == 0:
                    if name == "l3":
                        pe.wait_ge(sem(f"q_stacked{g}"), 16 * TERMS * (ATT.index(name) + 1))
                        stacked_k(pe, name)
                        pe.wait_ge(sem("band"), 1)
                    else:
                        pe.wait_ge(sem(f"m_stacked{g}"), 16 * (ATT.index(name) + 1))
                        pe.wait_ge(sem("q_ones_stacked"), 16)
                        if name == "ca":
                            pe.wait_ge(sem("kc_rows"), 32)
                        else:
                            pe.wait_ge(sem(f"k_rows{STACK[name]}"), 16)
                if u >= 2:
                    pe.wait_ge(sem("exp"), nth(*("exp",) + T_ORDER[u - 2][1:]))
                o = t_bank[u % 2]
                if name == "ca":
                    for ii in range(GB):
                        b = g * GB + ii
                        for s in range(SP_):
                            c, k = 32 * (s // 2), ii * 128 + (s % 2) * 64
                            last = mm(o[c:c + 32, k:k + 64], keys(kc_stack, R_ALL, s, b),
                                      q_stack[0:R_ALL, g, s, ii * T:(ii + 1) * T])
                    last.then_inc(sem("t"), 1)
                    return
                b = g * GB + i
                r = R_TERMS if name == "l3" else R_ALL
                masked = name in ("l2", "l3")
                if masked:
                    m = causal[:, 1, :] if name == "l2" else band[:, b * T:(b + 1) * T]
                    mm(o[:, :].rearrange("p (s q) -> p s q", s=SP_), two_i[:, :],
                       m.unsqueeze(1).to_broadcast([64, SP_, 64]))
                for s in range(SP_):
                    last = pe.matmul(o[:, s * T:(s + 1) * T], keys(k_stack[STACK[name]], r, s, b),
                                     q_stack[0:r, g, s, i * T:(i + 1) * T],
                                     start=not masked, stop=True, skip_group_check=masked)
                last.then_inc(sem("t"), 1)

            def attend(name, g, i):
                u = T_ORDER.index(("t", name, g, i))
                if i == 0:
                    take("av", name, g)
                    pe.wait_ge(sem("v_even"), nth("v_even", name, g))
                    if name != "ca":
                        pe.wait_ge(sem("v_odd"), nth("v_odd", name, g))
                    pe.wait_ge(sem("v_base"), nth("v_base", i=V_BASE[name]))
                if name == "l3":
                    pe.wait_ge(sem("square"), nth("square", name, g, i))
                else:
                    pe.wait_ge(sem("exp"), nth("exp", name, g, i))
                ve = v_ext[VALUES[name]]
                for ii in range(GB) if name == "ca" else (i,):
                    b = g * GB + ii
                    c = 64 * (ii % 2)
                    o = bank[g][c:c + 64, (ii // 2) * 144:(ii // 2) * 144 + 144]
                    if name == "ca":
                        for pi in range(2):
                            last = mm(o.rearrange("p (a c n) -> p a c n", a=4, c=2)[:, :, pi, :],
                                      probs[:, u % P_SLOTS, ii * 128 + pi * 64:ii * 128 + pi * 64 + 64],
                                      ve[:, b, :, :, :].rearrange("p s e n -> p (s e n)")[:, pi * 72:pi * 72 + 72]
                                      .rearrange("p (a n) -> p a n", a=4))
                    else:
                        for s in range(SP_):
                            last = mm(o[:, s * 18:s * 18 + 18], probs[:, u % P_SLOTS, s * T:(s + 1) * T],
                                      ve[:, b, s, :, :].rearrange("p e n -> p (e n)"))
                last.then_inc(sem("av"), 1)

            def flip(step, name, g, signal):
                o = take(step, name, g)
                pe.wait_ge(sem(signal), nth(signal, name, g))
                for j in range(NJ):
                    last = pe.transpose(o[:, j * 128:(j + 1) * 128], att[:, g, j, :], mat("ident"))
                last.then_inc(sem(step), 1)

            def centred(name, g):
                bank_ = take("z", name, g)
                if name == "f":
                    pe.wait_ge(sem("gelu"), nth("gelu", "f", g, 1))
                else:
                    pe.wait_ge(sem("attT"), nth("attT", name, g))
                pe.wait_ge(sem("weights_kept"), nth_all("weights_kept"))
                res = WC[:, WC_OF["l1_res"], :] if name == "l1" else mat("center")
                bias = rows[:, ROW_OF[name] * 128:(ROW_OF[name] + 1) * 128]
                mm(bank_[:, 0:GT].rearrange("p (j d) -> p j d", j=NJ), ones_row[:, :],
                   bias.unsqueeze(1).to_broadcast([3, NJ, 128]))
                w = mat("center") if name == "l2" else None if name == "f" else WC[:, WC_OF[name], :]
                for j in range(NJ):
                    t = slice(g * GT + j * 128, g * GT + (j + 1) * 128)
                    terms = [(X(X_IN[name])[:, t], res)]
                    if name == "f":
                        terms += [(hid[:, c, t], WC[:, WC_OF["f"] + c, :]) for c in range(F_CHUNKS)]
                    else:
                        terms.append((attT[:, g, j * 128:(j + 1) * 128], w))
                    for rows_, m in terms:
                        last = pe.matmul(bank_[:, j * 128:(j + 1) * 128], rows_, m, start=False, stop=True,
                                         skip_group_check=True)
                last.then_inc(sem("z"), 1)

            def hidden(name, g, i):
                x_ready(name, g)
                o = take("h", name, g, i)
                for c in range(2):
                    last = mm(o[:, c * GT:(c + 1) * GT], mat(f"{name}_w1_{2 * i + c}"), X(X_IN[name])[:, tok(g)])
                last.then_inc(sem("h"), 1)

            for step, name, g, i in ORDER:
                if step == "weights":
                    weights(i)
                elif step == "k":
                    keys_of(name, g)
                elif step == "v" and name == "ca":
                    values_ca(g)
                elif step == "v":
                    values(name, g)
                elif step == "ctx_rows":
                    o = take_turn("ctx_rows", "", g)
                    pe.wait_ge(sem("ctx_scale"), 1)
                    for j in range(NJ):
                        last = pe.transpose(o[:, j * 128:(j + 1) * 128], cn[:, g * NJ + j, :], mat("ident"))
                    last.then_inc(sem("ctx_rows"), 1)
                elif step == "q":
                    x_ready(name, g)
                    pe.wait_ge(sem("w1_loaded" if name == "sa" else "w2_loaded"), 16)
                    if name == "l3":
                        pe.wait_ge(sem("gammas"), 1)
                    o = take("q", name, g)
                    mm(o[:, 0:GT], mat(f"{name}_q"), X(X_IN[name])[:, tok(g)]).then_inc(sem("q"), 1)
                elif step == "s":
                    scores(name, g, i)
                elif step == "m":
                    max_rows(name, g)
                elif step == "t":
                    scores_t(name, g, i)
                elif step == "av":
                    attend(name, g, i)
                elif step == "flip":
                    flip("flip", name, g, "divide")
                elif step == "z":
                    centred(name, g)
                elif step == "flip_x":
                    flip("flip_x", name, g, "scale")
                elif step == "h":
                    hidden(name, g, i)
                elif step == "y":
                    o = take("y", "g", g)
                    pe.wait_ge(sem("gelu"), nth("gelu", "g", g, 1))
                    for c in range(F_CHUNKS):
                        last = mm(o[:, 0:GT], mat(f"g_w2_{c}"), hid[:, c, tok(g)], start=c == 0,
                                  stop=c == F_CHUNKS - 1)
                    last.then_inc(sem("y"), 1)
                elif step == "ms":
                    o = take("ms", name, g)
                    pe.wait_ge(sem("x_sq"), nth("x_sq", name, g))
                    for j in range(NJ):
                        last = mm(o[:, j:j + 1], k_full[:, g, j * 128:(j + 1) * 128], ones_col[:, :])
                    last.then_inc(sem("ms"), 1)
                elif step == "out":
                    o = take("out", "", g)
                    pe.wait_ge(sem("attT"), nth("attT", "l3", g))
                    for j in range(NJ):
                        oj = o[:, j * 128:(j + 1) * 128]
                        mm(oj, X("x6")[:, g * GT + j * 128:g * GT + (j + 1) * 128], mat("ident"), stop=False)
                        last = mm(oj, attT[:, g, j * 128:(j + 1) * 128], mat("l3_o"), start=False)
                    last.then_inc(sem("out"), 1)

        @block.scalar
        def _(act):
            def parts(name, side, g):
                act.wait_ge(sem(side), nth(side, name, g))
                if side == "q":
                    dst, src = q_full[:, g, :], bank[g][:, 0:GT]
                    if name != "sa":
                        act.wait_ge(sem(f"q_stacked{g}"), 16 * TERMS * ATT.index(name))
                else:
                    dst, src = k_full[:, g, :], s_bank[turn("k", name, g)[0]][:, 0:GT]
                    if name == "ca":
                        act.wait_ge(sem("k_low"), nth("k_low", "sa", g))
                    elif name == "l1":
                        stacked_k(act, "sa")
                        act.wait_ge(sem("k_low"), nth("k_low", "ca"))
                    elif name != "sa":
                        before = ATT[ATT.index(name) - 1]
                        stacked_k(act, before)
                        act.wait_ge(sem("k_low"), nth("k_low", before, g))
                    if name == "l3":
                        act.wait_ge(sem("z"), nth("z", "f", g))
                if name == "l3":
                    act.activation(dst, src, ACT.Copy)
                    act.activation(*paired(name, side, 0, g, src), ACT.Copy).then_inc(sem(f"{side}_parts"), 1)
                    return
                bias = col(f"{name}_{side}b")
                act.activation(dst, src, ACT.Identity, bias=bias, scale=1.0)
                act.activation(*paired(name, side, 0, g, src), ACT.Identity, bias=bias, scale=1.0
                               ).then_inc(sem(f"{side}_parts"), 1)

            def value_half(name, g):
                act.wait_ge(sem("v"), nth("v", name, g))
                act.wait_ge(sem("v_base"), nth("v_base", i=V_BASE[name]))
                if name in V_BEFORE:
                    act.wait_ge(sem("av"), nth_all("av", V_BEFORE[name]))
                src = s_bank[turn("v", name, g)[0]][64:128, 0:256].rearrange("p (j s e n) -> p j s e n", j=NJ, e=2, n=DH)
                for e in range(2):
                    dst = v_ext[VALUES[name]][64 * e:64 * e + 64, g * GB + 1:(g + 1) * GB:2, :, e, 0:DH]
                    last = act.activation(dst, src[:, :, :, e, :], ACT.Copy)
                last.then_inc(sem("v_odd"), 1)

            def exps(name, g, i):
                u = T_ORDER.index(("t", name, g, i))
                act.wait_ge(sem("t"), nth("t", name, g, i))
                if name == "l3":
                    n = L3_ORDER.index(("t", name, g, i))
                    if n >= 2:
                        act.wait_ge(sem("square"), nth(*("square",) + L3_ORDER[n - 2][1:]))
                    act.activation(relu[:, n % 2, :], t_bank[u % 2][:, :], ACT.Relu).then_inc(sem("exp"), 1)
                    return
                if u >= P_SLOTS:
                    act.wait_ge(sem("av"), nth(*("av",) + T_ORDER[u - P_SLOTS][1:]))
                else:
                    act.wait_ge(sem("band"), 1)
                    act.wait_ge(sem("ctx_ms"), 1)
                act.activation(probs[:, u % P_SLOTS, :], t_bank[u % 2][:, :], ACT.Exp, scale=SCALE
                               ).then_inc(sem("exp"), 1)

            act.wait_ge(sem("v_loaded"), 16)
            for step, name, g, i in ORDER:
                if step == "k_parts":
                    parts(name, "k", g)
                elif step == "q_parts":
                    parts(name, "q", g)
                elif step == "v_odd":
                    value_half(name, g)
                elif step == "ctx_rep":
                    act.wait_ge(sem("ctx_loaded"), 16)
                    for pi in range(2):
                        for e in range(2):
                            last = act.activation(
                                ctx_rep[:, :, pi, :, e, :],
                                ctxT[:].rearrange("p (b k r) -> p b k r", b=B, r=STRIDE)[:, :, :, 2 * pi + e]
                                .unsqueeze(2).to_broadcast([128, B, 4, K16]), ACT.Copy)
                    last.then_inc(sem("ctx_rep"), 1)
                elif step == "ctx_ms":
                    act.wait_ge(sem("cn_loaded"), 16)
                    for n in range(B // 2):
                        last = act.activation(ctx_sq[:, n * 128:(n + 1) * 128], cn[:, n, :], ACT.Square,
                                              scale=D ** -0.5, accum_out=cms[:, n:n + 1])
                    last.then_inc(sem("ctx_ms"), 1)
                elif step == "ctx_normed":
                    act.wait_ge(sem("ctx_rows"), nth("ctx_rows", g=g))
                    act.activation(ctxT[:, tok(g)], s_bank[turn("ctx_rows", "", g)[0]][:, 0:GT], ACT.Copy
                                   ).then_inc(sem("ctx_normed"), 1)
                elif step == "m_row":
                    act.wait_ge(sem("m"), nth("m", name, g))
                    if name != "sa":
                        act.wait_ge(sem(f"m_stacked{g}"), 16 * ATT.index(name))
                    act.activation(m_row[:, g, :], bank[g][0:32, 0:GT // 2].bitcast(BF), ACT.Copy
                                   ).then_inc(sem("m_row"), 1)
                elif step == "exp":
                    exps(name, g, i)
                elif step == "attT":
                    act.wait_ge(sem("flip"), nth("flip", name, g))
                    act.activation(attT[:, g, :], bank[g][:, 0:GT], ACT.Copy).then_inc(sem("attT"), 1)
                elif step == "var":
                    act.wait_ge(sem("z"), nth("z", name, g))
                    for j in range(NJ):
                        last = act.activation(att[:, g, j, :], bank[g][:, j * 128:(j + 1) * 128], ACT.Square,
                                              scale=D ** -0.5, accum_out=var[:, g, j:j + 1])
                    last.then_inc(sem("var"), 1)
                elif step == "ln":
                    act.wait_ge(sem("flip_x"), nth("flip_x", name, g))
                    if name == "sa":
                        act.wait_ge(sem("k"), nth("k", "ca"))
                    act.activation(X(X_OUT[name])[:, tok(g)], bank[g][:, 0:GT], ACT.Identity,
                                   bias=col(f"{name}_lb"), scale=col(f"{name}_lg")).then_inc(sem("ln"), 1)
                elif step == "gelu":
                    act.wait_ge(sem("h"), nth("h", name, g, i))
                    if name == "f" and i == 0:
                        act.wait_ge(sem("k_low"), nth_all("k_low", "l2"))
                        act.wait_ge(sem("ctx_rows"), nth_all("ctx_rows"))
                        act.wait_ge(sem("kc_rows"), 32)
                        act.wait_ge(sem("k_rows1"), 16)
                    elif i == 0:
                        act.wait_ge(sem("k_low"), nth("k_low", "l3", g))
                    for c in range(2):
                        cc = 2 * i + c
                        last = act.activation(hid[:, cc, tok(g)], bank[g][:, c * GT:(c + 1) * GT], ACT.Gelu,
                                              bias=col(f"{name}_b1_{cc}"), scale=1.0)
                    last.then_inc(sem("gelu"), 1)
                elif step == "x_sq":
                    act.wait_ge(sem("x6"), nth("x6", "g", g))
                    act.activation(k_full[:, g, :], X("x6")[:, tok(g)], ACT.Square, scale=D ** -0.5
                                   ).then_inc(sem("x_sq"), 1)
                elif step == "fin":
                    act.wait_ge(sem("out"), nth("out", "", g))
                    act.activation(fin[:, g, :], bank[g][:, 0:GT], ACT.Copy).then_inc(sem("fin"), 1)

        @block.vector
        def _(dve):
            def weights_kept(i):
                dve.wait_ge(sem("weights"), nth("weights", i=i))
                o = s_bank[turn("weights", "", 0, i)[0]]
                if i < 2:
                    last = dve.tensor_copy(WC[:, 4 * i:4 * i + 4, :].rearrange("p a n -> p (a n)"), o[:, :])
                elif i == 2:
                    last = dve.tensor_copy(WC[:, 8, :], o[:, 0:128])
                elif i == 3:
                    dve.tensor_copy(row_part[:, 0, :], o[:, 0:5]).then_inc(sem("row_part"), 1)
                    dve.wait_ge(sem("row_part"), 1)
                    dve.tensor_tensor(row_rest[:], o[:, 0:5], row_part[:, 0, :], ALU.subtract).then_inc(sem("row_part"), 1)
                    dve.wait_ge(sem("row_part"), 2)
                    dve.tensor_copy(row_part[:, 1, :], row_rest[:]).then_inc(sem("row_part"), 1)
                    dve.wait_ge(sem("row_part"), 3)
                    last = dve.tensor_tensor(row_part[:, 2, :], row_rest[:], row_part[:, 1, :], ALU.subtract)
                else:
                    last = dve.tensor_copy(rows[:], o[0:3, 0:320].bitcast(BF))
                last.then_inc(sem("weights_kept"), 1)

            def value_half(name, g):
                dve.wait_ge(sem("v"), nth("v", name, g))
                dve.wait_ge(sem("v_base"), nth("v_base", i=V_BASE[name]))
                o = s_bank[turn("v", name, g)[0]]
                if name == "ca":
                    vc = v_ext[1][:, g * GB:(g + 1) * GB, :, :, :].rearrange("p b s e n -> p (b s e) n")
                    vc = vc.rearrange("p (c a) n -> p c a n", a=8)
                    dve.tensor_tensor(vc[:, :, :, 0:DH], o[:, :].rearrange("p (c a n) -> p c a n", a=8, n=DH),
                                      e_mask.unsqueeze(1).unsqueeze(3).to_broadcast([128, 2 * GB, 8, DH]), ALU.mult
                                      ).then_inc(sem("v_even"), 1)
                    return
                if name in V_BEFORE:
                    dve.wait_ge(sem("av"), nth_all("av", V_BEFORE[name]))
                src = o[0:64, 0:256].rearrange("p (j s e n) -> p j s e n", j=NJ, e=2, n=DH)
                for e in range(2):
                    dst = v_ext[VALUES[name]][64 * e:64 * e + 64, g * GB:(g + 1) * GB:2, :, e, 0:DH]
                    last = dve.tensor_copy(dst, src[:, :, :, e, :])
                last.then_inc(sem("v_even"), 1)

            def key_mask():
                dve.wait_ge(sem("km_loaded"), 16)
                dve.tensor_scalar(km[:].rearrange("p (k b) -> p b k", b=B),
                                  km_u8[:].rearrange("p (b k) -> p b k", b=B), -1.0, KEY_BIG, ALU.add, ALU.mult
                                  ).then_inc(sem("key_mask"), 1)

            def band_mask():
                dve.wait_ge(sem("idx_loaded"), 16)
                dve.tensor_scalar(dist, idx, cst[0:64, 386:387], None, ALU.subtract).then_inc(sem("distance"), 1)
                dve.wait_ge(sem("distance"), 1)
                dve.tensor_tensor(dist, dist, dist, ALU.mult).then_inc(sem("distance"), 1)
                dve.wait_ge(sem("distance"), 2)
                dve.tensor_scalar(band[:], dist, 1.0, -BIG, ALU.is_gt, ALU.mult).then_inc(sem("band"), 1)

            def maxima(name, g, i):
                dve.wait_ge(sem("s"), nth("s", name, g, i))
                if name == "ca":
                    o, w = m_col[:, g, :, :, :].rearrange("p j s e -> p (j s e)"), K16
                else:
                    o, w = m_col[:, g, i // 2, 4 * (i % 2):4 * (i % 2) + 4, :].rearrange("p s e -> p (s e)"), T
                dve.tensor_reduce(o, s_bank[turn("s", name, g, i)[0]][:, :].rearrange("p (c k) -> p c k", k=w),
                                  AX.X, ALU.max).then_inc(sem("max"), 1)

            def max_parts(name, g):
                dve.wait_ge(sem("max"), max(nth("max", name, g, i) for i in range(S_UNITS[name])))
                src = m_col[:, g, :, :, :].rearrange("p j s e -> p j e s")
                dve.tensor_scalar(m_part[:, g, :, 0, :, :], src, -1.0, None, ALU.mult).then_inc(sem("max_hi"), 1)
                dve.wait_ge(sem("max_hi"), nth("max_parts", name, g))
                dve.tensor_tensor(m_part[:, g, :, 1, :, :], src, m_part[:, g, :, 0, :, :], ALU.add
                                  ).then_inc(sem("max_parts"), 1)

            def divide(name, g):
                src = bank[g][:, 0:NJ * 144].rearrange("p (h n) -> p h n", n=DH + 1)
                rd = rden[:, g, :, :].rearrange("p j h -> p (j h)")
                dve.wait_ge(sem("av"), nth("av", name, g, T_UNITS[name] - 1))
                den = src[:, :, DH]
                if name == "l3":
                    dve.wait_ge(sem("floor"), nth("floor", name, g))
                    dve.tensor_tensor(rden[:, g, :, :], den.rearrange("p (j h) -> p j h", j=NJ),
                                      floor[:, g, :].unsqueeze(2).to_broadcast([128, NJ, H]),
                                      ALU.max).then_inc(sem("den_floored"), 1)
                    dve.wait_ge(sem("den_floored"), nth_of_layer("divide", name, g))
                    den = rd
                dve.reciprocal(rd, den).then_inc(sem("rden"), 1)
                dve.wait_ge(sem("rden"), nth("divide", name, g))
                dve.tensor_tensor(att[:, g, :, :].rearrange("p j (h n) -> p (j h) n", n=DH), src[:, :, 0:DH],
                                  rd.unsqueeze(2).to_broadcast([128, NJ * H, DH]), ALU.mult
                                  ).then_inc(sem("divide"), 1)

            dve.memset(k_stack[0][:, 0:4, :, :].bitcast(F), 0.0).then_inc(sem("k_zero_first"), 1)
            dve.memset(ones_row[:], 1.0)
            dve.memset(ones_col[:], 1.0)
            dve.memset(q_ones[:], 1.0).then_inc(sem("const_ready"), 1)
            for step, name, g, i in ORDER:
                if step == "weights_kept":
                    weights_kept(i)
                elif step == "constants":
                    dve.wait_ge(sem("cst_loaded"), 16)
                    dve.tensor_copy(identb[:], cst[:, 0:128]).then_inc(sem("const_ready"), 1)
                    dve.tensor_copy(two_i[:], cst[0:64, 128:256]).then_inc(sem("const_ready"), 1)
                    dve.tensor_copy(causal[:], cst[0:64, 256:384].rearrange("p (a k) -> p a k", a=2)
                                    ).then_inc(sem("const_ready"), 1)
                    dve.tensor_copy(k_ones, cst[0:4, 384:386].unsqueeze(2).to_broadcast([4, 2, TOK])
                                    ).then_inc(sem("const_ready"), 1)
                elif step == "ca_k_split":
                    dve.memset(ca_k_split[:], 0.0).then_inc(sem("ca_k_zero"), 1)
                    dve.wait_ge(sem("ca_k_zero"), 1)
                    dve.wait_ge(sem("w2_loaded"), 16)
                    for r in range(STRIDE):
                        pi, e = r // 2, r % 2
                        of_e = slice(64 * e, 64 * e + 64)
                        last = dve.tensor_copy(
                            ca_k_split[:, r, of_e].rearrange("p (a c) -> p a c", c=2)[:, :, pi],
                            mat("ca_k")[:, of_e].rearrange("p (a c) -> p a c", c=2)[:, :, pi])
                    last.then_inc(sem("ca_k_split"), 1)
                elif step == "k_rest":
                    dve.wait_ge(sem("k_parts"), nth("k_parts", name, g))
                    part, x = paired(name, "k", 0, g, k_full[:, g, :])
                    dve.tensor_tensor(paired(name, "k", 0, g, k_rest[:, g, :])[1], x, part, ALU.subtract
                                      ).then_inc(sem("k_rest"), 1)
                elif step == "k_mid":
                    dve.wait_ge(sem("k_rest"), nth("k_rest", name, g))
                    dve.tensor_copy(*paired(name, "k", 1, g, k_rest[:, g, :])).then_inc(sem("k_mid"), 1)
                elif step == "k_low":
                    dve.wait_ge(sem("k_mid"), nth("k_mid", name, g))
                    part, x = paired(name, "k", 1, g, k_rest[:, g, :])
                    dve.tensor_tensor(paired(name, "k", 2, g, k_rest[:, g, :])[0], x, part, ALU.subtract
                                      ).then_inc(sem("k_low"), 1)
                elif step == "v_even":
                    value_half(name, g)
                elif step == "key_mask":
                    key_mask()
                elif step == "band":
                    band_mask()
                elif step == "gammas":
                    dve.wait_ge(sem("w3_loaded"), 16)
                    dve.wait_ge(sem("v_loaded"), 16)
                    for n, c in (("l3_q", "l3_gq"), ("l3_k", "l3_gk"), ("l3_v", "l3_gk")):
                        last = dve.tensor_scalar(mat(n), mat(n), col(c), None, ALU.mult)
                    last.then_inc(sem("gammas"), 1)
                elif step == "ctx_scale":
                    dve.wait_ge(sem("ctx_rs"), 1)
                    dve.tensor_tensor(cn, cn, crs[:].unsqueeze(2).to_broadcast([128, B // 2, 128]), ALU.mult
                                      ).then_inc(sem("ctx_scale"), 1)
                elif step == "q_rest":
                    dve.wait_ge(sem("q_parts"), nth("q_parts", name, g))
                    dve.tensor_tensor(q_rest[:, g, :], q_full[:, g, :], q_part[:, 0, g, :], ALU.subtract
                                      ).then_inc(sem("q_rest"), 1)
                elif step == "q_mid":
                    dve.wait_ge(sem("q_rest"), nth("q_rest", name, g))
                    dve.tensor_copy(q_part[:, 1, g, :], q_rest[:, g, :]).then_inc(sem("q_mid"), 1)
                elif step == "q_low":
                    dve.wait_ge(sem("q_mid"), nth("q_mid", name, g))
                    dve.tensor_tensor(q_part[:, 2, g, :], q_rest[:, g, :], q_part[:, 1, g, :], ALU.subtract
                                      ).then_inc(sem("q_low"), 1)
                elif step == "max":
                    maxima(name, g, i)
                elif step == "max_parts":
                    max_parts(name, g)
                elif step == "divide":
                    divide(name, g)
                elif step == "scale":
                    dve.wait_ge(sem("rstd"), nth("rstd", name, g))
                    dve.tensor_tensor(att[:, g, :, :], bank[g][:, 0:GT].rearrange("p (j d) -> p j d", j=NJ),
                                      rstd[:, g, :].unsqueeze(2).to_broadcast([128, NJ, 128]), ALU.mult
                                      ).then_inc(sem("scale"), 1)
                elif step == "x6":
                    dve.wait_ge(sem("y"), nth("y", "g", g))
                    dve.scalar_tensor_tensor(X("x6")[:, tok(g)], bank[g][:, 0:GT], col("g_b2"), X("x5")[:, tok(g)],
                                             ALU.add, ALU.add).then_inc(sem("x6"), 1)
                elif step == "floor":
                    dve.wait_ge(sem("ms"), nth("ms", name, g))
                    dve.tensor_scalar(floor[:, g, :], bank[g][:, 0:NJ], EPS_DEN / SCALE ** 2,
                                      EPS_RMS * EPS_DEN / SCALE ** 2, ALU.mult, ALU.add).then_inc(sem("floor"), 1)
                elif step == "square":
                    u = T_ORDER.index(("t", name, g, i))
                    n = L3_ORDER.index(("t", name, g, i))
                    dve.wait_ge(sem("exp"), nth("exp", name, g, i))
                    dve.wait_ge(sem("av"), nth(*("av",) + T_ORDER[u - P_SLOTS][1:]))
                    dve.tensor_tensor(probs[:, u % P_SLOTS, :], relu[:, n % 2, :], relu[:, n % 2, :], ALU.mult
                                      ).then_inc(sem("square"), 1)

        @block.gpsimd
        def _(pool):
            def v_base(i):
                n = B * SP_
                which = 0 if i == 0 else 1
                pool.wait_ge(sem("cst_loaded"), 16)
                if i == 1:
                    flat = v_ext[1][:, :, :, :, :].rearrange("p b s e n -> p (b s e) n")
                    pool.tensor_copy(flat[:, :, DH].rearrange("p (c a) -> p c a", a=8),
                                     e_mask.unsqueeze(1).to_broadcast([128, 2 * B, 8])).then_inc(sem("v_base"), 1)
                    return
                if i == 2:
                    pool.wait_ge(sem("av"), nth_all("av", "ca"))
                pool.memset(v_ext[which][:], 0.0).then_inc(sem("v_zero"), 1)
                pool.wait_ge(sem("v_zero"), 1 if i == 0 else 2)
                ve = v_ext[which][:, :, :, :, :].rearrange("p b s e n -> p (b s) e n")
                pool.tensor_copy(ve[:, :, :, DH], cst[:, 387:389].unsqueeze(1).to_broadcast([128, n, 2])
                                 ).then_inc(sem("v_base"), 1)

            def k_rows(i):
                pool.wait_ge(sem("const_ready"), 5)
                if i:
                    pool.wait_ge(sem("k_zero"), nth_all("k_zero"))
                else:
                    pool.wait_ge(sem("k_zero_first"), 2)
                    pool.dma_start(q_stack[R_TERMS:R_MASK, :, :, :].rearrange("r g s n -> r (g s) n"),
                                 q_ones[:].unsqueeze(1).to_broadcast([2, G * SP_, GT])
                                 ).then_inc(sem("q_ones_stacked"), 16)
                pool.dma_start(k_stack[i][R_MASK:R_ALL, :, :, :].rearrange("r s e n -> r s (e n)"),
                             k_ones.rearrange("r e n -> r (e n)").unsqueeze(1).to_broadcast([4, SP_, 2 * TOK])
                             ).then_inc(sem(f"k_rows{i}"), 16)

            def kc_rows():
                pool.wait_ge(sem("kc_zero"), nth("kc_zero"))
                pool.wait_ge(sem("const_ready"), 5)
                for e in range(2):
                    pool.dma_start(kc_stack[R_MASK:R_ALL, :, e, :],
                                 k_ones[:, e, 0:B * K16].unsqueeze(1).to_broadcast([4, SP_, B * K16])
                                 ).then_inc(sem("kc_rows"), 16)

            pool.memset(k_stack[0][:, 4:8, :, :].bitcast(F), 0.0).then_inc(sem("k_zero_first"), 1)
            pool.memset(half[:], -0.5).then_inc(sem("half_ready"), 1)
            for step, name, g, i in ORDER:
                if step == "v_base":
                    v_base(i)
                elif step == "k_rows":
                    k_rows(i)
                elif step == "kc_rows":
                    kc_rows()
                elif step == "k_stack" and name in POOL_STACKS:
                    k_stack_term(pool, name, i)
                elif step == "kc_zero":
                    pool.memset(kc_stack[:].bitcast(F), 0.0).then_inc(sem("kc_zero"), 1)
                elif step == "k_zero":
                    if i == 0:
                        pool.wait_ge(sem("v"), nth_all("v", "ca"))
                    pool.memset(k_stack[1][:, 2 * i:2 * i + 2, :, :].bitcast(F), 0.0).then_inc(sem("k_zero"), 1)
                elif step == "ctx_rs":
                    pool.wait_ge(sem("half_ready"), 1)
                    pool.wait_ge(sem("ctx_ms"), 1)
                    pool.tensor_scalar(cmse[:], cms[:], EPS_RMS, None, ALU.add).then_inc(sem("ctx_ms_eps"), 1)
                    pool.wait_ge(sem("ctx_ms_eps"), 1)
                    pool.tensor_tensor(crs[:], cmse[:], half[:], ALU.pow).then_inc(sem("ctx_rs"), 1)
                elif step == "rstd":
                    pool.wait_ge(sem("half_ready"), 1)
                    pool.wait_ge(sem("var"), nth("var", name, g))
                    pool.tensor_scalar(vare[:, g, :], var[:, g, :], EPS, None, ALU.add).then_inc(sem("var_eps"), 1)
                    pool.wait_ge(sem("var_eps"), nth("rstd", name, g))
                    pool.tensor_tensor(rstd[:, g, :], vare[:, g, :], half[:, 0:NJ], ALU.pow
                                       ).then_inc(sem("rstd"), 1)


def constants():
    import numpy as np
    c = np.zeros((128, CST), np.float32)
    c[:, 0:128] = np.eye(128)
    c[0:64, 128:192] = np.eye(64)
    c[0:64, 192:256] = np.eye(64)
    later = np.triu(np.ones((64, 64)), 1) * -BIG
    c[0:64, 256:320] = later
    c[0:64, 320:384] = later.T
    for hl in range(2):
        for e in range(2):
            c[2 * hl + e, 384 + e] = 1 - 2 * hl
    c[:, 386] = np.arange(128)
    c[0:64, 387] = c[64:128, 388] = 1
    for p in range(4):
        for e in range(2):
            c[32 * p + 16 * e:32 * p + 16 * e + 16, CST - 8 + 2 * p + e] = 1
    return c


def kernel(**inp):
    import numpy as np
    import concourse.bacc as bacc
    from concourse.bass_utils import run_bass_kernel_spmd

    def arr(n):
        return np.asarray(inp[n])

    def by_feature(w):
        return w.reshape(w.shape[:-1] + (SP_, 2, DH)).swapaxes(-3, -2).swapaxes(-2, -1).reshape(w.shape)

    L0, L1, L2, L3 = "L0_xattn_", "L1_xattn_", "L2_xattn_", "L3_xattn_"
    sa_w, sa_b = arr(L0 + "sa_in_w"), arr(L0 + "sa_in_b")
    upd, tokw = arr(L1 + "W_upd"), arr(L1 + "W_token")
    f1, f2 = arr(L0 + "ffn_w1").T, arr(L0 + "ffn_w2")
    g1, g2 = arr(L2 + "W1").T, arr(L2 + "W2").T
    m = {
        "ident": np.eye(D, dtype=np.float32),
        "center": np.eye(D, dtype=np.float32) - np.float32(1 / D),
        "sa_q": by_feature(sa_w[0:D].T), "sa_k": by_feature(sa_w[D:2 * D].T), "sa_v": sa_w[2 * D:].T,
        "ca_q": by_feature(arr(L0 + "ca_q_w").T), "ca_k": by_feature(arr(L0 + "ca_k_w").T),
        "ca_v": arr(L0 + "ca_v_w").T,
        "l1_q": by_feature(arr(L1 + "W_state")), "l1_k": by_feature(tokw), "l1_v": tokw,
        "sa_o": arr(L0 + "sa_out_w"), "ca_o": arr(L0 + "ca_o_w"),
        "l1_updT": upd[D:].T, "l1_updsT": upd[:D].T, "l1_outT": arr(L1 + "W_out").T,
        "l2_q": by_feature(arr(L2 + "Wq").T), "l2_k": by_feature(arr(L2 + "Wk").T), "l2_v": arr(L2 + "Wv").T,
        "l3_q": by_feature(arr(L3 + "Wq").T), "l3_k": by_feature(arr(L3 + "Wk").T), "l3_v": arr(L3 + "Wv").T,
        "l3_o": arr(L3 + "Wo").T,
    }
    for c in range(F_CHUNKS):
        s = slice(c * D, (c + 1) * D)
        m[f"f_w1_{c}"], m[f"f_w2_{c}"] = f1[:, s], f2[:, s]
        m[f"g_w1_{c}"], m[f"g_w2_{c}"] = g1[:, s], g2[s, :]
    v = {
        "sa_qb": by_feature(sa_b[0:D]), "sa_kb": by_feature(sa_b[D:2 * D]), "sa_vb": sa_b[2 * D:],
        "ca_qb": by_feature(arr(L0 + "ca_q_b")), "ca_kb": by_feature(arr(L0 + "ca_k_b")),
        "l1_qb": by_feature(arr(L1 + "b_state")), "l1_kb": by_feature(arr(L1 + "b_token")),
        "l2_qb": by_feature(arr(L2 + "bq")), "l2_kb": by_feature(arr(L2 + "bk")),
        "sa_ob": arr(L0 + "sa_out_b"), "ca_vb": arr(L0 + "ca_v_b"), "ca_ob": arr(L0 + "ca_o_b"),
        "f_b2": arr(L0 + "ffn_b2"), "l1_tb": arr(L1 + "b_token"), "l1_ob": arr(L1 + "b_out"),
        "l1_ub": arr(L1 + "b_upd"), "l2_vb": arr(L2 + "bv"), "g_b2": arr(L2 + "b2"),
        "sa_lg": arr(L0 + "ln1_g"), "sa_lb": arr(L0 + "ln1_b"), "ca_lg": arr(L0 + "ln2_g"), "ca_lb": arr(L0 + "ln2_b"),
        "f_lg": arr(L0 + "ln3_g"), "f_lb": arr(L0 + "ln3_b"), "l1_lg": arr(L1 + "ln_gamma"),
        "l1_lb": arr(L1 + "ln_beta"), "l2_lg": arr(L2 + "ln_g"), "l2_lb": arr(L2 + "ln_b"),
        "l3_gq": arr(L3 + "gamma_q"), "l3_gk": arr(L3 + "gamma_kv"),
    }
    for c in range(F_CHUNKS):
        v[f"f_b1_{c}"] = arr(L0 + "ffn_b1")[c * D:(c + 1) * D]
        v[f"g_b1_{c}"] = arr(L2 + "b1")[c * D:(c + 1) * D]
    arrays = {
        "xT": arr("x").reshape(TOK, D).T,
        "ctxT": arr("ctx_1024").reshape(TOK, D).T,
        "ctx": arr("ctx_1024").reshape(TOK, D),
        "idx": arr("itok_BxS_0_255").reshape(1, TOK),
        "key_mask": arr("mask_BxS2_bf1").reshape(1, TOK).view(np.uint8),
        "mats": np.stack([m[n] for n in MATS], axis=1),
        "cols": np.stack([v[n] for n in COLS], axis=1),
        "consts": constants(),
    }
    arrays = {n: np.ascontiguousarray(x) for n, x in arrays.items()}
    nc = bacc.Bacc("TRN2", target_bir_lowering=False, num_devices=1)
    a = {n: nc.dram_tensor(f"in_{n}", x.shape, mybir.dt.from_np(x.dtype), kind="ExternalInput").ap()
         for n, x in arrays.items()}
    out = nc.dram_tensor("out", (TOK, D), mybir.dt.float32, kind="ExternalOutput").ap()
    build(nc, a, out)
    r = run_bass_kernel_spmd(nc, [{f"in_{n}": x for n, x in arrays.items()}], core_ids=[0])
    return r.results[0]["out"].reshape(B, T, D)
```
